# Optimizing a Trainium2 kernel written in Bass

```python
import numpy as np
import jax
import jax.numpy as jnp

def _softmax(x, axis=-1):
    return jax.nn.softmax(x, axis=axis)

def _gelu(x):
    return jax.nn.gelu(x, approximate=True)

def _silu(x):
    return jax.nn.silu(x)

def _sigmoid(x):
    return jax.nn.sigmoid(x)

def _layernorm(x, axis=-1, eps=1e-05):
    m = jnp.mean(x, axis=axis, keepdims=True)
    v = jnp.var(x, axis=axis, keepdims=True)
    return (x - m) / jnp.sqrt(v + eps)

def _scatter_add(tgt, idx, src, axis=0):
    return tgt.at[idx].add(src)

def _segment_sum(src, seg, n):
    return jax.ops.segment_sum(src, seg, n)
kernel_name = 'mk_xattn_ffn_d2_seqx_r8_e43553'

def setup_inputs(seed: int=0):
    np.random.seed(seed)
    _w = jnp.asarray

    def _rec_inputs():
        import jax
        import jax.numpy as jnp
        _rk = jax.random.key(seed)
        x = 7.22e-05 + 1 * jax.random.normal(jax.random.fold_in(_rk, 1), (2, 256, 128), jnp.float32)
        _lenS = 256 - jax.random.randint(jax.random.fold_in(_rk, 7), (2,), 0, max(1, 256 // 4) + 1, jnp.int32)
        _lenS2 = 512 - jax.random.randint(jax.random.fold_in(_rk, 8), (2,), 0, max(1, 512 // 4) + 1, jnp.int32)
        _ctx_1024P = jax.random.normal(jax.random.fold_in(_rk, 11), (2, 16, 128), jnp.float32)
        _ctx_1024c = jax.random.dirichlet(jax.random.fold_in(_rk, 511), 0.3 * jnp.ones((16,), jnp.float32), (2, 512))
        _ctx_1024t = jnp.einsum('bsk,bkd->bsd', _ctx_1024c, _ctx_1024P)
        _ctx_1024t = _ctx_1024t * jax.lax.rsqrt(jnp.mean(jnp.square(_ctx_1024t)) + 1e-12) * 0.953939
        ctx_1024 = 4.13588e-05 + 0.999923 * (_ctx_1024t + 0.3 * jax.random.normal(jax.random.fold_in(_rk, 611), (2, 512, 128), jnp.float32))
        return (x, ctx_1024)
    x, ctx_1024 = _rec_inputs()

    def _L0_xattn_setup():
        import jax, jax.numpy as jnp
        import numpy as np
        D_MODEL = 128
        NUM_HEADS = 16
        D_K = D_MODEL // NUM_HEADS

        def _split_heads(x):
            B, S, _ = x.shape
            return x.reshape(B, S, NUM_HEADS, D_K).transpose(0, 2, 1, 3)
        key = jax.random.key(seed)
        ks = jax.random.split(key, 11)
        B, S = (4, 256)
        scale = 1.0 / np.sqrt(D_MODEL)
        inp = {'query': jax.random.normal(ks[0], (B, S, D_MODEL), jnp.float32), 'key': jax.random.normal(ks[1], (B, S, D_MODEL), jnp.float32), 'value': jax.random.normal(ks[2], (B, S, D_MODEL), jnp.float32), 'Wq': jax.random.normal(ks[3], (D_MODEL, D_MODEL), jnp.float32) * scale, 'bq': jnp.zeros((D_MODEL,), jnp.float32), 'Wk': jax.random.normal(ks[4], (D_MODEL, D_MODEL), jnp.float32) * scale, 'bk': jnp.zeros((D_MODEL,), jnp.float32), 'Wv': jax.random.normal(ks[5], (D_MODEL, D_MODEL), jnp.float32) * scale, 'bv': jnp.zeros((D_MODEL,), jnp.float32), 'Wo': jax.random.normal(ks[6], (D_MODEL, D_MODEL), jnp.float32) * scale, 'bo': jnp.zeros((D_MODEL,), jnp.float32)}
        return inp
    _L0_xattn_all = _L0_xattn_setup()
    _L0_xattn_in = {k: v for k, v in _L0_xattn_all.items() if k in ('Wq', 'bq', 'Wk', 'bk', 'Wv', 'bv', 'Wo', 'bo')}
    del _L0_xattn_all

    def _L0_ffn_setup():
        import jax, jax.numpy as jnp
        import numpy as np
        E, D, F, GATE_DIM = (8, 128, 512, 16)
        B, T = (2, 256)
        key = jax.random.key(seed)
        ks = jax.random.split(key, 7)
        s = 0.02
        return {'hidden_states': jax.random.normal(ks[0], (B, T, D), dtype=jnp.float32), 'w_red': jax.random.normal(ks[1], (D, GATE_DIM), dtype=jnp.float32) * s, 'wg': jax.random.normal(ks[2], (E, GATE_DIM), dtype=jnp.float32), 'w1': jax.random.normal(ks[3], (E, D, F), dtype=jnp.float32) * s, 'b1': jax.random.normal(ks[4], (E, F), dtype=jnp.float32) * s, 'w2': jax.random.normal(ks[5], (E, F, D), dtype=jnp.float32) * s, 'b2': jax.random.normal(ks[6], (E, D), dtype=jnp.float32) * s}
    _L0_ffn_all = _L0_ffn_setup()
    _L0_ffn_in = {k: v for k, v in _L0_ffn_all.items() if k in ('w_red', 'wg', 'w1', 'b1', 'w2', 'b2')}
    del _L0_ffn_all

    def _L1_xattn_setup():
        import jax, jax.numpy as jnp
        import numpy as np
        EMBED_DIM = 128
        Q_HEADS = 16
        KV_HEADS = 8
        HEAD_DIM = EMBED_DIM // Q_HEADS
        KV_EMBED = HEAD_DIM * KV_HEADS
        GROUPS = Q_HEADS // KV_HEADS
        LN_EPS = 1e-05
        RMS_EPS = 1e-06

        def _rms_norm(x):
            return x * jax.lax.rsqrt(jnp.mean(jnp.square(x), axis=-1, keepdims=True) + RMS_EPS)

        def _act_quant(x):
            scale = 127.0 / jnp.maximum(jnp.max(jnp.abs(x), axis=-1, keepdims=True), 1e-05)
            return jnp.clip(jnp.round(x * scale), -128.0, 127.0) / scale

        def _weight_quant(w):
            scale = 1.0 / jnp.maximum(jnp.mean(jnp.abs(w)), 1e-05)
            return jnp.clip(jnp.round(w * scale), -1.0, 1.0) / scale

        def _ste(a, q):
            return a + jax.lax.stop_gradient(q - a)

        def bit_linear(x, w):
            xn = _rms_norm(x)
            xq = _ste(xn, _act_quant(xn))
            wq = _ste(w, _weight_quant(w))
            return jnp.einsum('bni,oi->bno', xq, wq)
        key = jax.random.key(seed)
        ks = jax.random.split(key, 6)
        B, N, S, D = (16, 128, 32, EMBED_DIM)
        s = D ** (-0.5)
        return {'x': jax.random.normal(ks[0], (B, N, D), jnp.float32), 'y': jax.random.normal(ks[1], (B, S, D), jnp.float32), 'wq': jax.random.normal(ks[2], (D, D), jnp.float32) * s, 'wk': jax.random.normal(ks[3], (KV_EMBED, D), jnp.float32) * s, 'wv': jax.random.normal(ks[4], (KV_EMBED, D), jnp.float32) * s, 'wo': jax.random.normal(ks[5], (D, D), jnp.float32) * s, 'ln_gamma': jnp.ones((D,), jnp.float32), 'ln_beta': jnp.zeros((D,), jnp.float32)}
    _L1_xattn_all = _L1_xattn_setup()
    _L1_xattn_in = {k: v for k, v in _L1_xattn_all.items() if k in ('wq', 'wk', 'wv', 'wo', 'ln_gamma', 'ln_beta')}
    del _L1_xattn_all

    def _L1_ffn_setup():
        import jax, jax.numpy as jnp
        import numpy as np
        B, L, D = (2, 256, 128)
        E = 15
        H = D * 1
        K = 3
        T = 1.0
        key = jax.random.key(seed)
        ks = jax.random.split(key, 12)
        s = 0.02
        return {'x': jax.random.normal(ks[0], (B, L, D), dtype=jnp.float32), 'router_W': jax.random.normal(ks[1], (D, E), dtype=jnp.float32) * s, 'router_b': jnp.zeros((E,), dtype=jnp.float32), 'sW1': jax.random.normal(ks[2], (D, H), dtype=jnp.float32) * s, 'sb1': jnp.zeros((H,), dtype=jnp.float32), 'sW2': jax.random.normal(ks[3], (H, D), dtype=jnp.float32) * s, 'sb2': jnp.zeros((D,), dtype=jnp.float32), 'eW1': jax.random.normal(ks[4], (E, D, H), dtype=jnp.float32) * s, 'eb1': jnp.zeros((E, H), dtype=jnp.float32), 'eW2': jax.random.normal(ks[5], (E, H, D), dtype=jnp.float32) * s, 'eb2': jnp.zeros((E, D), dtype=jnp.float32)}
    _L1_ffn_all = _L1_ffn_setup()
    _L1_ffn_in = {k: v for k, v in _L1_ffn_all.items() if k in ('router_W', 'router_b', 'sW1', 'sb1', 'sW2', 'sb2', 'eW1', 'eb1', 'eW2', 'eb2')}
    del _L1_ffn_all
    return {'x': x, 'ctx_1024': ctx_1024, 'L0_xattn_Wq': _L0_xattn_in['Wq'], 'L0_xattn_bq': _L0_xattn_in['bq'], 'L0_xattn_Wk': _L0_xattn_in['Wk'], 'L0_xattn_bk': _L0_xattn_in['bk'], 'L0_xattn_Wv': _L0_xattn_in['Wv'], 'L0_xattn_bv': _L0_xattn_in['bv'], 'L0_xattn_Wo': _L0_xattn_in['Wo'], 'L0_xattn_bo': _L0_xattn_in['bo'], 'L0_ffn_w_red': _L0_ffn_in['w_red'], 'L0_ffn_wg': _L0_ffn_in['wg'], 'L0_ffn_w1': _L0_ffn_in['w1'], 'L0_ffn_b1': _L0_ffn_in['b1'], 'L0_ffn_w2': _L0_ffn_in['w2'], 'L0_ffn_b2': _L0_ffn_in['b2'], 'L1_xattn_wq': _L1_xattn_in['wq'], 'L1_xattn_wk': _L1_xattn_in['wk'], 'L1_xattn_wv': _L1_xattn_in['wv'], 'L1_xattn_wo': _L1_xattn_in['wo'], 'L1_xattn_ln_gamma': _L1_xattn_in['ln_gamma'], 'L1_xattn_ln_beta': _L1_xattn_in['ln_beta'], 'L1_ffn_router_W': _L1_ffn_in['router_W'], 'L1_ffn_router_b': _L1_ffn_in['router_b'], 'L1_ffn_sW1': _L1_ffn_in['sW1'], 'L1_ffn_sb1': _L1_ffn_in['sb1'], 'L1_ffn_sW2': _L1_ffn_in['sW2'], 'L1_ffn_sb2': _L1_ffn_in['sb2'], 'L1_ffn_eW1': _L1_ffn_in['eW1'], 'L1_ffn_eb1': _L1_ffn_in['eb1'], 'L1_ffn_eW2': _L1_ffn_in['eW2'], 'L1_ffn_eb2': _L1_ffn_in['eb2']}

def reference(x, ctx_1024, L0_xattn_Wq, L0_xattn_bq, L0_xattn_Wk, L0_xattn_bk, L0_xattn_Wv, L0_xattn_bv, L0_xattn_Wo, L0_xattn_bo, L0_ffn_w_red, L0_ffn_wg, L0_ffn_w1, L0_ffn_b1, L0_ffn_w2, L0_ffn_b2, L1_xattn_wq, L1_xattn_wk, L1_xattn_wv, L1_xattn_wo, L1_xattn_ln_gamma, L1_xattn_ln_beta, L1_ffn_router_W, L1_ffn_router_b, L1_ffn_sW1, L1_ffn_sb1, L1_ffn_sW2, L1_ffn_sb2, L1_ffn_eW1, L1_ffn_eb1, L1_ffn_eW2, L1_ffn_eb2):
    import jax
    import jax.numpy as jnp

    def _L0_xattn_ref(query, key, value, Wq, bq, Wk, bk, Wv, bv, Wo, bo):
        import jax, jax.numpy as jnp
        import numpy as np
        D_MODEL = 128
        NUM_HEADS = 16
        D_K = D_MODEL // NUM_HEADS

        def _split_heads(x):
            B, S, _ = x.shape
            return x.reshape(B, S, NUM_HEADS, D_K).transpose(0, 2, 1, 3)
        q = _split_heads(query @ Wq.T + bq)
        k = _split_heads(key @ Wk.T + bk)
        v = _split_heads(value @ Wv.T + bv)
        scores = jnp.einsum('bhqd,bhkd->bhqk', q, k) / jnp.sqrt(jnp.float32(D_K))
        attn = jax.nn.softmax(scores, axis=-1)
        out = jnp.einsum('bhqk,bhkd->bhqd', attn, v)
        B, H, Sq, dk = out.shape
        out = out.transpose(0, 2, 1, 3).reshape(B, Sq, D_MODEL)
        return out @ Wo.T + bo

    def _L0_ffn_ref(hidden_states, w_red, wg, w1, b1, w2, b2):
        import jax, jax.numpy as jnp
        import numpy as np
        E, D, F, GATE_DIM = (8, 128, 512, 16)
        B, T = (2, 256)
        b, t, c = hidden_states.shape
        x = hidden_states.reshape(-1, c)
        red = x @ w_red
        wg_n = wg / jnp.maximum(jnp.linalg.norm(wg, axis=1, keepdims=True), 0.0001)
        logits = red @ wg_n.T
        gates = jax.nn.softmax(logits, axis=1)
        idx = jnp.argmax(gates, axis=1)
        scores = jnp.take_along_axis(gates, idx[:, None], axis=1)
        h = jax.nn.gelu(jnp.einsum('td,edf->etf', x, w1) + b1[:, None, :], approximate=False)
        y = jnp.einsum('etf,efd->etd', h, w2) + b2[:, None, :]
        out = jnp.take_along_axis(y, idx[None, :, None], axis=0)[0]
        out = out * scores
        return out.reshape(b, t, c)

    def _L1_xattn_ref(x, y, wq, wk, wv, wo, ln_gamma, ln_beta):
        import jax, jax.numpy as jnp
        import numpy as np
        EMBED_DIM = 128
        Q_HEADS = 16
        KV_HEADS = 8
        HEAD_DIM = EMBED_DIM // Q_HEADS
        KV_EMBED = HEAD_DIM * KV_HEADS
        GROUPS = Q_HEADS // KV_HEADS
        LN_EPS = 1e-05
        RMS_EPS = 1e-06

        def _rms_norm(x):
            return x * jax.lax.rsqrt(jnp.mean(jnp.square(x), axis=-1, keepdims=True) + RMS_EPS)

        def _act_quant(x):
            scale = 127.0 / jnp.maximum(jnp.max(jnp.abs(x), axis=-1, keepdims=True), 1e-05)
            return jnp.clip(jnp.round(x * scale), -128.0, 127.0) / scale

        def _weight_quant(w):
            scale = 1.0 / jnp.maximum(jnp.mean(jnp.abs(w)), 1e-05)
            return jnp.clip(jnp.round(w * scale), -1.0, 1.0) / scale

        def _ste(a, q):
            return a + jax.lax.stop_gradient(q - a)

        def bit_linear(x, w):
            xn = _rms_norm(x)
            xq = _ste(xn, _act_quant(xn))
            wq = _ste(w, _weight_quant(w))
            return jnp.einsum('bni,oi->bno', xq, wq)
        B, N, D = x.shape
        S = y.shape[1]
        q = bit_linear(x, wq).reshape(B, N, Q_HEADS, HEAD_DIM)
        k = bit_linear(y, wk).reshape(B, S, KV_HEADS, HEAD_DIM)
        v = bit_linear(y, wv).reshape(B, S, KV_HEADS, HEAD_DIM)
        q = jnp.transpose(q, (0, 2, 1, 3)) / HEAD_DIM ** 0.5
        q = q.reshape(B, KV_HEADS, GROUPS, N, HEAD_DIM)
        k = jnp.transpose(k, (0, 2, 1, 3))
        v = jnp.transpose(v, (0, 2, 1, 3))
        scores = jnp.einsum('bhgnd,bhsd->bhgns', q, k)
        attn = jax.nn.softmax(scores, axis=-1)
        out = jnp.einsum('bhgns,bhsd->bhgnd', attn, v)
        out = jnp.transpose(out, (0, 3, 1, 2, 4)).reshape(B, N, D)
        mu = jnp.mean(out, axis=-1, keepdims=True)
        var = jnp.mean(jnp.square(out - mu), axis=-1, keepdims=True)
        out = (out - mu) * jax.lax.rsqrt(var + LN_EPS) * ln_gamma + ln_beta
        return bit_linear(out, wo)

    def _L1_ffn_ref(x, router_W, router_b, sW1, sb1, sW2, sb2, eW1, eb1, eW2, eb2):
        import jax, jax.numpy as jnp
        import numpy as np
        B, L, D = (2, 256, 128)
        E = 15
        H = D * 1
        K = 3
        T = 1.0
        b, l, d = x.shape
        n = b * l
        xt = x.reshape(n, d)
        shared = jax.nn.relu(xt @ sW1 + sb1) @ sW2 + sb2
        logits = xt @ router_W + router_b
        probs = jax.nn.softmax(logits / T, axis=-1)
        top_p, top_i = jax.lax.top_k(probs, K)
        cw = jnp.zeros((n, E), dtype=probs.dtype)
        cw = cw.at[jnp.arange(n)[:, None], top_i].set(top_p)
        h = jax.nn.relu(jnp.einsum('nd,edh->neh', xt, eW1) + eb1)
        ye = jnp.einsum('neh,ehd->ned', h, eW2) + eb2
        routed = jnp.einsum('ned,ne->nd', ye, cw)
        return (shared + routed).reshape(b, l, d)
    x = x + _L0_xattn_ref(_layernorm(x, axis=-1), ctx_1024, ctx_1024, L0_xattn_Wq, L0_xattn_bq, L0_xattn_Wk, L0_xattn_bk, L0_xattn_Wv, L0_xattn_bv, L0_xattn_Wo, L0_xattn_bo)
    x = x + _L0_ffn_ref(_layernorm(x, axis=-1), L0_ffn_w_red, L0_ffn_wg, L0_ffn_w1, L0_ffn_b1, L0_ffn_w2, L0_ffn_b2)
    x = x + _L1_xattn_ref(_layernorm(x, axis=-1), ctx_1024, L1_xattn_wq, L1_xattn_wk, L1_xattn_wv, L1_xattn_wo, L1_xattn_ln_gamma, L1_xattn_ln_beta)
    x = x + _L1_ffn_ref(_layernorm(x, axis=-1), L1_ffn_router_W, L1_ffn_router_b, L1_ffn_sW1, L1_ffn_sb1, L1_ffn_sW2, L1_ffn_sb2, L1_ffn_eW1, L1_ffn_eb1, L1_ffn_eW2, L1_ffn_eb2)
    return x

_drawn_inputs = setup_inputs


def setup_inputs(seed=0):
    import zlib

    import numpy as np

    out = dict(_drawn_inputs(seed))
    spreads = {'L0_xattn_bq': (0.0, 0.391),
     'L0_xattn_bk': (0.0, 2.0),
     'L0_xattn_bv': (0.0, 0.1),
     'L0_xattn_bo': (0.0, 0.1),
     'L1_xattn_ln_gamma': (1.0, 0.2),
     'L1_xattn_ln_beta': (0.0, 0.1),
     'L1_ffn_router_b': (0.0, 0.8),
     'L1_ffn_sb1': (0.0, 0.76),
     'L1_ffn_sb2': (0.0, 0.1),
     'L1_ffn_eb1': (0.0, 0.8),
     'L1_ffn_eb2': (0.0, 0.654)}
    factors = {'L0_ffn_w_red': 7.814,
     'L0_ffn_wg': 7.742,
     'L0_ffn_w1': 7.882,
     'L0_ffn_b1': 8.0,
     'L0_ffn_w2': 7.842,
     'L0_ffn_b2': 8.0,
     'L1_ffn_router_W': 4.9,
     'L1_ffn_eW1': 8.0,
     'L1_ffn_eW2': 8.0,
     'L1_ffn_sW1': 5.062}
    for name, (base, spread) in spreads.items():
        noise = np.random.default_rng([zlib.crc32(name.encode()), seed]).standard_normal(out[name].shape)
        drawn = base * np.exp(spread * noise) if base else spread * noise
        out[name] = jnp.asarray(drawn.astype(out[name].dtype))
    for name, factor in factors.items():
        out[name] = (out[name] * factor).astype(out[name].dtype)
    return out
```

```python
from contextlib import ExitStack

import numpy as np

import concourse.bass as bass
from concourse import mybir

F32 = mybir.dt.float32
BF16 = mybir.dt.bfloat16
U32 = mybir.dt.uint32
ALU = mybir.AluOpType
ACT = mybir.ActivationFunctionType
AX = mybir.AxisListType.X

P = 128
D = 128
B = 2
R = 2
NQ = R * P
NK = 512
KT = NK // P
H = 16
DH = D // H
NG = H // 4
E0, F0, GD = 8, 512, 16
FC = F0 // P
E1 = 15
TOP = 3
QSCALE = float(1.0 / np.sqrt(DH))
LN_EPS = 1e-5
MAGIC = 1.5 * 2.0 ** 23
TWO_ONES = float(np.array([0x3F803F80], np.uint32).view(np.float32)[0])
LOWEST = -3.0e38
MARK = 3.0e38

K_PART = (0, 1, 2, 0, 1, 0)
Q_PART = (0, 0, 0, 1, 1, 2)
SHIFT_ROW = 8 * len(K_PART)


def value_head(layer, s):
    a, p = divmod(s, 8)
    return 2 * p + a if layer == 0 else 2 * (p // 2) + a


def key_group(layer, s):
    return s % 8 if layer == 0 else (s % 8) // 2


def build_schedule():
    steps = []

    def attention(layer, first, last, extra):
        g0, g1 = 8 * layer, 8 * layer + 8
        for g in range(first, last):
            for i in range(4):
                if i == 1 and g0 <= g + 1 < g1:
                    steps.append(("max_rows", g + 1))
                if g0 <= g + 2 < g1:
                    steps.append(("scores", g + 2, i))
                if g0 <= g < g1:
                    steps.append(("exp", g, i))
                if g0 <= g - 1 < g1:
                    steps.append(("values", g - 1, i))
                steps.extend(extra.get((g, i), []))

    steps += [("ctx_turn", 0), ("w0_turn",), ("stats", "q0", 0), ("norm", "q0", 0), ("kproj", 0, 0),
              ("turn", "q0", 0), ("qproj", 0, 0), ("ctx_turn", 1)]
    attention(0, -2, 9, {
        (-2, 0): [("bulk",), ("vproj", 0, 0)],
        (-2, 1): [("kproj", 0, 1)],
        (-2, 2): [("stats", "q0", 1)],
        (-2, 3): [("norm", "q0", 1)],
        (-1, 0): [("turn", "q0", 1)],
        (-1, 1): [("qproj", 0, 1)],
        (-1, 2): [("vproj", 0, 1)],
        (-1, 3): [("bias_turn",)],
        (0, 1): [("ctx_measure",)],
        (0, 3): [("ctx_quant",)],
        (1, 1): [("w1_measure",)],
        (1, 3): [("w1_quant",)],
        (2, 1): [("w1_turn",)],
        (2, 2): [("ctxq_turn", 0)],
        (2, 3): [("ctxq_turn", 1)],
        (3, 0): [("kproj", 1, 0)],
        (3, 1): [("vproj", 1, 0)],
        (3, 2): [("kproj", 1, 1)],
        (3, 3): [("vproj", 1, 1)],
        (5, 0): [("out_turn", 0, 0)],
        (5, 1): [("att_turn", 0, 0)],
        (5, 2): [("out_proj", 0, 0), ("stats", "f0", 0)],
        (5, 3): [("norm", "f0", 0)],
        (6, 0): [("turn", "f0", 0)],
        (6, 1): [("red0", 0)],
        (6, 2): [("logits0", 0)],
        (6, 3): [("gate_exp0", 0)],
        (7, 0): [("pick0", 0)],
    })

    def experts0(b, extra):
        for e in range(-1, E0):
            for q in range(2):
                if e + 1 < E0:
                    steps.append(("hidden0", b, e + 1, q))
                if e >= 0:
                    steps.append(("output0", b, e, q))
                steps.extend(extra.get((e, q), []))

    experts0(0, {
        (-1, 1): [("out_turn", 0, 1)],
        (0, 0): [("att_turn", 0, 1)],
        (0, 1): [("out_proj", 0, 1), ("stats", "f0", 1)],
        (1, 0): [("norm", "f0", 1)],
        (1, 1): [("turn", "f0", 1)],
        (2, 0): [("red0", 1)],
        (2, 1): [("logits0", 1)],
        (3, 0): [("pick0", 1)],
    })
    early = {
        (0, 0): [("end0", 0), ("stats", "q1", 0)],
        (0, 1): [("norm", "q1", 0)],
        (1, 0): [("quant", "q1", 0)],
        (1, 1): [("turn", "q1", 0)],
        (2, 0): [("qproj", 1, 0)],
    }
    for n in range(8):
        at = (3 + n // 2, n % 2)
        early.setdefault(at, []).append(("scores", 8 + n // 4, n % 4))
    experts0(1, early)
    steps.append(("gate_exp0", 1))
    steps.append(("max_rows", 8))
    attention(1, 8, 17, {
        (8, 0): [("end0", 1), ("stats", "q1", 1)],
        (8, 1): [("norm", "q1", 1)],
        (8, 2): [("quant", "q1", 1)],
        (8, 3): [("turn", "q1", 1)],
        (9, 0): [("qproj", 1, 1)],
        (13, 0): [("out_turn", 1, 0), ("stats", "o1", 0)],
        (13, 1): [("norm", "o1", 0)],
        (13, 2): [("quant", "o1", 0)],
        (13, 3): [("att_turn", 1, 0)],
        (14, 0): [("out_proj", 1, 0), ("stats", "f1", 0)],
        (14, 1): [("norm", "f1", 0)],
        (14, 2): [("turn", "f1", 0)],
        (14, 3): [("logits1", 0)],
        (15, 1): [("pick1", 0)],
    })

    def experts1(b, extra):
        for e in range(-1, E1 + 1):
            if e + 1 <= E1:
                steps.append(("hidden1", b, e + 1))
            if e >= 0:
                steps.append(("output1", b, e, 0))
                steps.append(("output1", b, e, 1))
            steps.extend(extra.get(e, []))
        steps.append(("store", b))

    experts1(0, {
        0: [("out_turn", 1, 1), ("stats", "o1", 1)],
        1: [("norm", "o1", 1)],
        3: [("quant", "o1", 1)],
        4: [("att_turn", 1, 1)],
        5: [("out_proj", 1, 1), ("stats", "f1", 1)],
        7: [("norm", "f1", 1)],
        8: [("turn", "f1", 1)],
        9: [("logits1", 1)],
        12: [("pick1", 1)],
    })
    experts1(1, {})
    return steps


SCHEDULE = build_schedule()

X_FILLS = {
    "ctx_turn": lambda s: [s[1]], "ctxq_turn": lambda s: [s[1]],
    "w0_turn": lambda s: [1], "kproj": lambda s: [0], "vproj": lambda s: [1], "turn": lambda s: [0],
    "qproj": lambda s: [1], "bias_turn": lambda s: [0], "w1_measure": lambda s: [1],
    "w1_turn": lambda s: [1], "out_turn": lambda s: [0, 1], "att_turn": lambda s: [0],
    "out_proj": lambda s: [1], "red0": lambda s: [0], "logits0": lambda s: [1],
    "pick0": lambda s: [0, 1], "logits1": lambda s: [1], "pick1": lambda s: [0, 1],
}
X_COUNT = {}
_seen = [0, 0]
for _s in SCHEDULE:
    for _x in X_FILLS.get(_s[0], lambda s: [])(_s):
        _seen[_x] += 1
        X_COUNT[_x, _s] = _seen[_x]

ORDER = {}
for _s in SCHEDULE:
    ORDER.setdefault(_s[0], []).append(_s)


def nth(*step):
    return ORDER[step[0]].index(step) + 1


def transformer(nc, x, ctx, Wq, bq, Wk, bk, Wv, bv, Wo, bo, w_red, wg, w1, b1, w2, b2, wq1, wk1, wv1, wo1,
                gamma, beta, rW, rb, sW1, sb1, sW2, sb2, eW1, eb1, eW2, eb2, out):
    with ExitStack() as stack:
        def sb(name, shape, dt=F32):
            return stack.enter_context(nc.sbuf_tensor(name, shape, dt))

        def sem(name):
            return stack.enter_context(nc.semaphore(name))

        stack.enter_context(nc.allow_low_precision(reason="exact splits into bfloat16 parts; the shift of a softmax cancels"))

        ident = sb("ident", [P, P])
        negident = sb("negident", [P, P], BF16)
        ones = sb("ones", [P, P])
        halves = sb("halves", [P, P])
        expo = sb("expo", [P, 8])
        expo_half = sb("expo_half", [P, 8])
        xin = sb("xin", [P, B, R, D])
        xres = sb("xres", [P, B, R, D])
        bo_b = sb("bo_b", [P, D])
        gamma_b = sb("gamma_b", [P, D])
        beta_b = sb("beta_b", [P, D])
        rb_b = sb("rb_b", [P, E1])
        x1 = xres
        x2 = sb("x2", [P, B, R, D])
        x3 = xin
        hn = sb("hn", [P, B, R, D])
        hT = sb("hT", [P, B, NQ])
        att = sb("att", [P, B, R, D])
        attT = sb("attT", [P, B, NQ])
        acc = sb("acc", [P, B, R, D])
        bst = sb("bst", [P, R, 6])
        mv = sb("mv", [P, R, 2])
        vareps = sb("vareps", [P, R])
        rstd = sb("rstd", [P, R])
        sumsq = sb("sumsq", [P, R])
        amax = sb("amax", [P, R])
        ms = sb("ms", [P, R])
        rms = sb("rms", [P, R])
        mxn = sb("mxn", [P, R])
        inv = sb("inv", [P, R])
        qs = sb("qs", [P, R])
        dq = sb("dq", [P, R])
        junk = sb("junk", [P, R, D])
        cx = sb("cx", [P, B * KT, D])
        ctxT = sb("ctxT", [P, B * NK])
        csq = sb("csq", [P, B * KT, D])
        cstat = sb("cstat", [P, 7, B * KT])
        w0n = sb("w0n", [P, 4, D])
        wT = [sb(f"wT{n}", [P, 4, D]) for n in range(2)]
        w1n = sb("w1n", [P, 3, D])
        w1t = w1n
        wsum = sb("wsum", [P, 3])
        walpha = sb("walpha", [P, 3])
        winv = sb("winv", [P, 3])
        bias3 = sb("bias3", [P, 3])
        bqs = sb("bqs", [P, 1])
        kf = sb("kf", [P, NK])
        kr = sb("kr", [P, NK])
        kp = sb("kp", [P, 3, NK], BF16)
        qf = sb("qf", [P, NQ])
        qr = sb("qr", [P, NQ])
        qp = sb("qp", [P, 3, NQ], BF16)
        K = [sb("K0", [P, B, 8, NK], BF16), sb("K1", [P, B, 4, NK], BF16)]
        Q = [sb(f"Q{n}", [P, B, H, NQ], BF16) for n in range(2)]
        V = [sb("V0", [P, B, KT, H, 32]), sb("V1", [P, B, KT, 8, 32])]
        prob = sb("prob", [P, 2, 4, KT, NQ])
        mx = sb("mx", [P, 2, R, 4], BF16)
        nm = sb("nm", [4, 2, NQ], BF16)
        oT = sb("oT", [P, NG, NQ])
        rsum = sb("rsum", [P, R, H])
        hid = prob[:, :, 0, :, :]
        w1s = sb("w1s", [P, E0, F0])
        w2s = sb("w2s", [P, E0, FC, D])
        b1r = sb("b1r", [E0 * FC, P])
        b1T = sb("b1T", [P, E0 * FC])
        b2r = sb("b2r", [E0, D])
        wreds = sb("wreds", [P, GD])
        wgn = sb("wgn", [E0, GD])
        wgsq = sb("wgsq", [E0, GD])
        wgs = sb("wgs", [E0, 3])
        wgT = sb("wgT", [GD, E0])
        redT = sb("redT", [GD, NQ])
        lg0 = sb("lg0", [P, R, E0 + 7])
        rep0 = sb("rep0", [P, R, 8])
        mr0 = sb("mr0", [P, R, E0 + 7])
        top0 = sb("top0", [P, R, 8])
        oh0 = sb("oh0", [P, B, R, E0])
        ntop0 = sb("ntop0", [P, B, R])
        lgk0 = sb("lgk0", [P, B, R, E0])
        ge0 = sb("ge0", [P, B, R, E0])
        gsum0 = sb("gsum0", [P, B, R])
        score0 = sb("score0", [P, B, R])
        ohT = sb("ohT", [E0, NQ])
        place = K[0][:, :, :, :].rearrange("p b g k -> p (b g k)").bitcast(F32)
        e1w, e2w = (place[:, n * (E1 + 1) * D:(n + 1) * (E1 + 1) * D].rearrange("p (e d) -> p e d", d=D) for n in range(2))
        e1r = sb("e1r", [E1 + 1, D])
        e1T = sb("e1T", [P, E1 + 1])
        e2r = sb("e2r", [E1 + 1, D])
        rWs = sb("rWs", [P, E1])
        lg1 = sb("lg1", [P, R, E1 + 5])
        rep1 = sb("rep1", [P, R, 8])
        mr1 = sb("mr1", [P, R, E1 + 5])
        top1 = sb("top1", [P, R, 8])
        sel1 = sb("sel1", [P, R, E1])
        ntop1 = sb("ntop1", [P, R])
        ge1 = sb("ge1", [P, R, E1])
        gsum1 = sb("gsum1", [P, R])
        rsum1 = sb("rsum1", [P, R])
        cw = sb("cw", [P, B, R, E1 + 1])
        cwT = sb("cwT", [E1 + 1, NQ])

        SA = [stack.enter_context(nc.psum_tensor(f"SA{n}", [P, 512], F32)) for n in range(2)]
        SB = [stack.enter_context(nc.psum_tensor(f"SB{n}", [P, 512], F32)) for n in range(2)]
        OB = stack.enter_context(nc.psum_tensor("OB", [P, 512], F32))
        MB = stack.enter_context(nc.psum_tensor("MB", [P, 512], F32))
        X = [stack.enter_context(nc.psum_tensor(f"X{n}", [P, 512], F32)) for n in range(2)]
        YB = [OB, MB]

        in_x, in_ctx, in_w0, in_bias0 = [sem("in_x0"), sem("in_x1")], [sem("in_ctx0"), sem("in_ctx1")], sem("in_w0"), sem("in_bias0")
        in_bo, in_gb, in_w1n = sem("in_bo"), sem("in_gb"), sem("in_w1n")
        in_route, in_f0, in_f1 = sem("in_route"), sem("in_f0"), sem("in_f1")
        s_ident, s_const, s_pfill, s_vfill = sem("s_ident"), sem("s_const"), sem("s_pfill"), sem("s_vfill")
        x_full = [sem("x0_full"), sem("x1_full")]
        x_read = [sem("x0_read"), sem("x1_read")]
        s_sa_full, s_sa_max = sem("s_sa_full"), sem("s_sa_max")
        s_mb_full, s_mb_read, s_shift = sem("s_mb_full"), sem("s_mb_read"), sem("s_shift")
        s_sb_full, s_exp = sem("s_sb_full"), sem("s_exp")
        s_ob_full, s_ob_read = sem("s_ob_full"), sem("s_ob_read")
        s_kp, s_qp = sem("s_kp"), sem("s_qp")
        s_kst = [[sem(f"s_kst{n}{b}") for b in range(B)] for n in range(2)]
        s_qst = [[sem(f"s_qst{n}{b}") for b in range(B)] for n in range(2)]
        s_stats, s_rstd, s_norm, s_sq, s_rms, s_quant = (sem("s_stats"), sem("s_rstd"), sem("s_norm"), sem("s_sq"),
                                                         sem("s_rms"), sem("s_quant"))
        s_xres, s_bqs = sem("s_xres"), sem("s_bqs")
        s_csq, s_cstat, s_cq = sem("s_csq"), sem("s_cstat"), sem("s_cq")
        s_wabs, s_walpha, s_wtern = sem("s_wabs"), sem("s_walpha"), sem("s_wtern")
        s_wgsq, s_wgnorm, s_wgn = sem("s_wgsq"), sem("s_wgnorm"), sem("s_wgn")
        s_pick, s_gate, s_cw = sem("s_pick"), sem("s_gate"), sem("s_cw")
        s_h0_full, s_h0, s_y0_full, s_y0 = sem("s_h0_full"), sem("s_h0"), sem("s_y0_full"), sem("s_y0")
        s_h1_full, s_h1, s_y1_full, s_y1 = sem("s_h1_full"), sem("s_h1"), sem("s_y1_full"), sem("s_y1")
        s_end0 = sem("s_end0")
        s_stored = sem("s_stored")
        s_v, s_p = sem("s_v"), sem("s_p")

        GQ = 8 * 2
        stage_in = {"q0": xin, "f0": x1, "q1": x2, "o1": att, "f1": x3}

        def fill_view(t):
            return t.rearrange("p g k -> p (g k)").bitcast(F32)

        def xread(bank, *step):
            return x_read[bank], X_COUNT[bank, step]

        def split_group(g):
            return g // 8, g % 8 // NG, g % NG

        block = stack.enter_context(nc.Block())

        @block.sync
        def _(sp):
            sp.dma_start(xin[:, 0, :, :], x[0].rearrange("(r p) d -> p r d", p=P)).then_inc(in_x[0], 16)
            for b in range(B):
                sp.dma_start(cx[:, b * KT:(b + 1) * KT, :], ctx[b].rearrange("(k p) d -> p k d", p=P)).then_inc(in_ctx[b], 16)
                if b == 0:
                    sp.dma_start(xin[:, 1, :, :], x[1].rearrange("(r p) d -> p r d", p=P)).then_inc(in_x[1], 16)

            def stack_rows(parts, dst, order, done):
                rows = parts.shape[0] // 2
                for a in range(2):
                    for j, part in enumerate(order):
                        sp.dma_start(dst(a)[64 * a + 8 * j:64 * a + 8 * j + 8], parts[rows * a:rows * a + rows, part, :]).then_inc(done, 16)

            for step in SCHEDULE:
                kind = step[0]
                if kind == "kproj":
                    _, n, b = step
                    sp.wait_ge(s_kp, nth(*step))
                    if (n, b) == (0, 0):
                        sp.wait_ge(s_const, 1)
                    else:
                        sp.wait_ge(s_pfill, 3 if n == 0 else 6)
                    stack_rows(kp[0:P // (n + 1)], lambda a: K[n][:, b, :, :], K_PART, s_kst[n][b])
                elif kind == "qproj":
                    _, n, b = step
                    sp.wait_ge(s_qp, nth(*step))
                    sp.wait_ge(s_pfill, (1, 4)[b] if n == 0 else 7)
                    stack_rows(qp[:, :, :], lambda a: Q[n][:, b, 8 * a:8 * a + 8, :], Q_PART, s_qst[n][b])
                elif kind == "max_rows":
                    n, b, g = split_group(step[1])
                    row = 64 * (g // 2) + SHIFT_ROW
                    sp.wait_ge(s_mb_read, step[1] + 1)
                    sp.wait_ge(s_sa_full, 8 * (step[1] + 1))
                    sp.dma_start(Q[n][row:row + 1, b, 4 * g:4 * g + 4, :], nm[:, step[1] % 2, :]).then_inc(s_shift, 16)
                elif step == ("hidden0", 0, 0, 0):
                    sp.wait_ge(s_sb_full, 8 * 8)
                    sp.dma_start(e1w[:, 0:E1, :], eW1.rearrange("e d h -> d e h")).then_inc(in_f1, 16)
                    sp.dma_start(e1w[:, E1, :], sW1).then_inc(in_f1, 16)
                    sp.dma_start(e2w[:, 0:E1, :], eW2.rearrange("e h d -> h e d")).then_inc(in_f1, 16)
                    sp.dma_start(e2w[:, E1, :], sW2).then_inc(in_f1, 16)
                elif kind == "store":
                    b = step[1]
                    sp.wait_ge(s_y1, (b + 1) * (E1 + 1) * R)
                    sp.dma_start(out[b].rearrange("(r p) d -> p r d", p=P), acc[:, b, :, :]).then_inc(s_stored, 16)
            sp.wait_ge(s_stored, 16 * B)

        @block.gpsimd
        def _(pool):
            count = [0]

            def then(ins):
                count[0] += 1
                ins.then_inc(s_p, 1)
                pool.wait_ge(s_p, count[0])

            then(pool.memset(ident[:, :], 0.0))
            pool.affine_select(out=ident[:, :], in_=ident[:, :], compare_op=ALU.not_equal, fill=1.0, base=0,
                               pattern=[[-1, P]], channel_multiplier=1).then_inc(s_ident, 1)
            pool.memset(expo[:, :], -0.5).then_inc(s_vfill, 1)
            pool.memset(expo_half[:, :], 0.5).then_inc(s_vfill, 1)
            pool.wait_ge(s_vfill, 2)
            pool.dma_start(bias3[:, 0:1], bq.rearrange("(p a d) -> a d p", p=8, a=2), allow_slow_non_contiguous=True).then_inc(in_bias0, 16)
            pool.dma_start(bias3[:, 1:2], bk.rearrange("(p a d) -> a d p", p=8, a=2), allow_slow_non_contiguous=True).then_inc(in_bias0, 16)
            pool.dma_start(bias3[:, 2:3], bv.rearrange("(p o) -> p o", o=1)).then_inc(in_bias0, 16)
            pool.memset(fill_view(Q[0][:, 0]), 0.0).then_inc(s_pfill, 1)
            pool.dma_start(bo_b[:, :], bo.rearrange("(o d) -> o d", o=1).broadcast_to([P, D])).then_inc(in_bo, 16)
            pool.memset(V[0][:, 0].rearrange("p k h c -> p (k h c)"), 1.0).then_inc(s_pfill, 1)
            pool.memset(fill_view(K[0][:, 1]), TWO_ONES).then_inc(s_pfill, 1)
            pool.memset(fill_view(Q[0][:, 1]), 0.0).then_inc(s_pfill, 1)
            pool.memset(V[0][:, 1].rearrange("p k h c -> p (k h c)"), 1.0).then_inc(s_pfill, 1)

            for step in SCHEDULE:
                kind = step[0]
                if kind == "stats":
                    _, stage, b = step
                    pool.wait_ge(s_stats, nth(*step))
                    then(pool.tensor_scalar(vareps[:, :], mv[:, :, 1], 1.0, LN_EPS, ALU.mult, ALU.add))
                    pool.tensor_tensor(rstd[:, :], vareps[:, :], expo[:, 0:R], ALU.pow).then_inc(s_rstd, 1)
                elif kind == "norm" and step[1] in ("q1", "o1"):
                    pool.wait_ge(s_sq, NORMQ.index(step) + 1)
                    then(pool.tensor_scalar(ms[:, :], sumsq[:, :], 1.0 / D, 1e-6, ALU.mult, ALU.add))
                    pool.tensor_tensor(rms[:, :], ms[:, :], expo[:, 0:R], ALU.pow).then_inc(s_rms, 1)
                elif kind == "bulk":
                    pool.memset(K[1][:, :, :, :].rearrange("p b g k -> p (b g k)").bitcast(F32), TWO_ONES).then_inc(s_pfill, 1)
                    pool.memset(Q[1][:, :, :, :].rearrange("p b g k -> p (b g k)").bitcast(F32), 0.0).then_inc(s_pfill, 1)
                    pool.memset(V[1][:, :, :, :, :].rearrange("p b k h c -> p (b k h c)"), 1.0).then_inc(s_pfill, 1)
                    pool.wait_ge(in_x[0], 16)
                    pool.wait_ge(in_x[1], 16)
                    pool.wait_ge(in_bo, 16)
                    for b in range(B):
                        for r in range(R):
                            last = pool.tensor_tensor(xres[:, b, r, :], xin[:, b, r, :], bo_b[:, :], ALU.add)
                    last.then_inc(s_xres, 1)
                elif kind == "ctx_measure":
                    pool.wait_ge(in_ctx[0], 16)
                    pool.wait_ge(in_ctx[1], 16)
                    pool.tensor_tensor(csq[:, :, :], cx[:, :, :], cx[:, :, :], ALU.mult).then_inc(s_csq, 1)
                    pool.wait_ge(s_csq, 2)
                    then(pool.tensor_scalar(cstat[:, 2, :], cstat[:, 0, :], 1.0 / D, 1e-6, ALU.mult, ALU.add))
                    pool.tensor_tensor(cstat[:, 3, :], cstat[:, 2, :], expo[:, :], ALU.pow).then_inc(s_cstat, 1)
                elif kind == "ctx_quant":
                    pool.wait_ge(s_cstat, 2)
                    for k in range(B * KT):
                        last = pool.tensor_scalar(csq[:, k, :], cx[:, k, :], cstat[:, 5, k:k + 1], MAGIC, ALU.mult, ALU.add)
                    then(last)
                    for k in range(B * KT):
                        last = pool.tensor_scalar(csq[:, k, :], csq[:, k, :], -MAGIC, cstat[:, 6, k:k + 1], ALU.add, ALU.mult)
                    last.then_inc(s_cq, 1)
                elif kind == "w1_quant":
                    pool.wait_ge(s_walpha, 1)
                    for n in range(3):
                        last = pool.tensor_scalar(w1t[:, n, :], w1n[:, n, :], winv[:, n:n + 1], MAGIC, ALU.mult, ALU.add)
                    then(last)
                    then(pool.tensor_scalar(w1t[:, :, :], w1t[:, :, :], -MAGIC, 1.0, ALU.add, ALU.mult))
                    then(pool.tensor_scalar(w1t[:, :, :], w1t[:, :, :], 1.0, -1.0, ALU.min, ALU.max))
                    for n in range(3):
                        last = pool.tensor_scalar(w1t[:, n, :], w1t[:, n, :], walpha[:, n:n + 1], 1.0, ALU.mult, ALU.mult)
                    last.then_inc(s_wtern, 1)
                elif kind == "bias_turn":
                    pool.wait_ge(s_wgsq, 1)
                    pool.tensor_tensor(wgs[:, 1:2], wgs[:, 0:1], expo_half[0:E0, 0:1], ALU.pow).then_inc(s_wgnorm, 1)

        @block.scalar
        def _(act):
            for n, w in enumerate((Wk, Wq, Wv, Wo)):
                act.dma_start(w0n[:, n, :], w).then_inc(in_w0, 16)

            for step in SCHEDULE:
                kind = step[0]
                if kind == "ctx_turn":
                    c = step[1]
                    act.wait_ge(x_full[c], X_COUNT[c, step])
                    act.activation(ctxT[:, c * NK:(c + 1) * NK], X[c][:, :], ACT.Copy).then_inc(x_read[c], 1)
                elif kind == "ctxq_turn":
                    c = step[1]
                    act.wait_ge(x_full[c], X_COUNT[c, step])
                    act.wait_ge(*xread(1, "vproj", 0, 1))
                    act.wait_ge(*xread(0, "kproj", 0, 1))
                    act.activation(ctxT[:, c * NK:(c + 1) * NK], X[c][:, :], ACT.Copy).then_inc(x_read[c], 1)
                elif kind == "bulk":
                    act.dma_start(w1n[:, 0, :], wq1).then_inc(in_w1n, 16)
                    act.dma_start(w1n[0:64, 1, :], wk1).then_inc(in_w1n, 16)
                    act.dma_start(w1n[64:128, 1, :], wv1).then_inc(in_w1n, 16)
                    act.dma_start(w1n[:, 2, :], wo1).then_inc(in_w1n, 16)
                    act.dma_start(b1r[:, :], b1.rearrange("e (c f) -> (e c) f", c=FC)).then_inc(in_route, 16)
                    act.dma_start(b2r[:, :], b2).then_inc(in_route, 16)
                    act.dma_start(wgn[:, :], wg).then_inc(in_route, 16)
                    act.dma_start(wreds[:, :], w_red).then_inc(in_route, 16)
                    act.dma_start(e1r[0:E1, :], eb1).then_inc(in_route, 16)
                    act.dma_start(e1r[E1:E1 + 1, :], sb1.rearrange("(o d) -> o d", o=1)).then_inc(in_route, 16)
                    act.dma_start(e2r[0:E1, :], eb2).then_inc(in_route, 16)
                    act.dma_start(e2r[E1:E1 + 1, :], sb2.rearrange("(o d) -> o d", o=1)).then_inc(in_route, 16)
                    act.dma_start(rWs[:, :], rW).then_inc(in_route, 16)
                elif kind == "bias_turn":
                    act.dma_start(gamma_b[:, :], gamma.rearrange("(o d) -> o d", o=1).broadcast_to([P, D])).then_inc(in_gb, 16)
                    act.dma_start(beta_b[:, :], beta.rearrange("(o d) -> o d", o=1).broadcast_to([P, D])).then_inc(in_gb, 16)
                    act.dma_start(rb_b[:, :], rb.rearrange("(o d) -> o d", o=1).broadcast_to([P, E1])).then_inc(in_gb, 16)
                    for h in range(2):
                        e = slice(h * E0 // 2, (h + 1) * E0 // 2)
                        act.dma_start(w1s[:, e, :], w1[e].rearrange("e d f -> d e f")).then_inc(in_f0, 16)
                        act.dma_start(w2s[:, e, :, :].rearrange("p e c d -> p (e c) d"),
                                      w2[e].rearrange("e (c f) d -> f (e c) d", c=FC)).then_inc(in_f0, 16)
                elif kind == "kproj":
                    _, n, b = step
                    act.wait_ge(x_full[0], X_COUNT[0, step])
                    if n == 0 and b == 0:
                        act.wait_ge(in_bias0, 48)
                    if nth(*step) > 1:
                        act.wait_ge(s_kp, nth(*step) - 1)
                    rows = P // (n + 1)
                    if n == 0:
                        act.activation(kf[:, :], X[0][:, :], ACT.Identity, bias=bias3[:, 1:2]).then_inc(x_read[0], 1)
                    else:
                        act.activation(kf[0:rows, :], X[0][0:rows, :], ACT.Copy).then_inc(x_read[0], 1)
                elif kind == "qproj":
                    _, n, b = step
                    act.wait_ge(x_full[1], X_COUNT[1, step])
                    if nth(*step) > 1:
                        act.wait_ge(s_qp, nth(*step) - 1)
                    if n == 0:
                        act.wait_ge(s_bqs, 1)
                        act.activation(qf[:, :], X[1][:, 0:NQ], ACT.Identity, bias=bqs[:, :], scale=QSCALE).then_inc(x_read[1], 1)
                    else:
                        act.activation(qf[:, :], X[1][:, 0:NQ], ACT.Copy, scale=QSCALE).then_inc(x_read[1], 1)
                elif kind == "vproj":
                    _, n, b = step
                    heads = H // (n + 1)
                    act.wait_ge(x_full[1], X_COUNT[1, step])
                    act.wait_ge(s_pfill, (2, 5)[b] if n == 0 else 8)
                    act.activation(V[n][:, b].rearrange("p k h c -> p (k h) c")[:, :, 0:DH],
                                   X[1][:, 0:KT * heads * DH].rearrange("p (n c) -> p n c", c=DH),
                                   ACT.Copy).then_inc(x_read[1], 1)
                elif kind == "max_rows":
                    g = step[1]
                    act.wait_ge(s_mb_full, g + 1)
                    if g >= 2:
                        act.wait_ge(s_shift, 16 * (g - 1))
                    act.activation(nm[:, g % 2, :], MB[0:4, 0:NQ], ACT.Copy).then_inc(s_mb_read, 1)
                elif kind == "exp":
                    _, g, i = step
                    if i == 0 and g >= 2:
                        act.wait_ge(s_ob_full, g - 1)
                    if i == 0 and g in (8, 9):
                        act.wait_ge(s_y0_full, B * E0 * R)
                    for u in range(2):
                        n = 8 * g + 2 * i + u
                        act.wait_ge(s_sb_full, n + 1)
                        act.activation(prob[:, g % 2, i, 2 * u:2 * u + 2, :].rearrange("p k q -> p (k q)"), SB[u][:, :],
                                       ACT.Exp).then_inc(s_exp, 1)
                elif kind == "values" and step[2] == KT - 1:
                    g = step[1]
                    act.wait_ge(s_ob_full, g + 1)
                    if g % NG == 0 and g:
                        n, b, _ = split_group(g - 1)
                        act.wait_ge(x_full[1], X_COUNT[1, ("out_turn", n, b)])
                    act.activation(oT[:, g % NG, :], OB[:, 0:NQ], ACT.Copy).then_inc(s_ob_read, 1)
                elif kind == "gate_exp0":
                    b = step[1]
                    act.wait_ge(s_gate, LOGITS0[b])
                    for r in range(R):
                        act.activation(ge0[:, b, r, :], lgk0[:, b, r, :], ACT.Exp, bias=ntop0[:, b, r:r + 1],
                                       accum_out=gsum0[:, b, r:r + 1]).then_inc(s_pick, 1)
                elif kind == "logits1":
                    b = step[1]
                    act.wait_ge(s_gate, LOGITS1[b])
                    for r in range(R):
                        act.activation(ge1[:, r, :], lg1[:, r, 0:E1], ACT.Exp, bias=ntop1[:, r:r + 1],
                                       accum_out=gsum1[:, r:r + 1]).then_inc(s_pick, 1)
                elif kind == "hidden0":
                    _, b, e, q = step
                    if b == 0 and e < 2 and q == 0:
                        act.wait_ge(s_ob_full, 8)
                    if (b, e, q) == (0, 0, 0):
                        act.wait_ge(*xread(0, "bias_turn"))
                    n = b * E0 + e
                    if n >= 2:
                        act.wait_ge(s_y0_full, R * (n - 1))
                    act.wait_ge(s_h0_full, 2 * n + q + 1)
                    for c in range(2 * q, 2 * q + 2):
                        last = act.activation(hid[:, n % 2, c, :], SB[q][:, (c % 2) * NQ:(c % 2 + 1) * NQ], ACT.Gelu,
                                              bias=b1T[:, e * FC + c:e * FC + c + 1])
                    last.then_inc(s_h0, 1)
                elif kind == "hidden1":
                    _, b, e = step
                    n = b * (E1 + 1) + e
                    if n < 2:
                        act.wait_ge(s_ob_full, GQ)
                    else:
                        act.wait_ge(s_y1_full, R * (n - 1))
                    act.wait_ge(s_h1_full, n + 1)
                    act.activation(hid[:, n % 2, 0, :], SB[n % 2][:, 0:NQ], ACT.Relu, bias=e1T[:, e:e + 1]).then_inc(s_h1, 1)

        @block.vector
        def _(dve):
            count = [0]

            def then(ins):
                count[0] += 1
                ins.then_inc(s_v, 1)
                dve.wait_ge(s_v, count[0])

            def split(full, rest, parts, done):
                then(dve.tensor_copy(parts[:, 0, :], full))
                then(dve.tensor_tensor(rest, full, parts[:, 0, :], ALU.subtract))
                then(dve.tensor_copy(parts[:, 1, :], rest))
                dve.tensor_tensor(parts[:, 2, :], rest, parts[:, 1, :], ALU.subtract).then_inc(done, 1)

            dve.memset(fill_view(K[0][:, 0]), TWO_ONES).then_inc(s_const, 1)
            dve.memset(ones[:, :], 1.0).then_inc(s_const, 1)
            then(dve.memset(halves[:, :], 0.0))
            for a in range(2):
                last = dve.memset(halves[64 * a:64 * a + 64, 64 * a:64 * a + 64], 1.0)
            last.then_inc(s_const, 1)
            dve.wait_ge(s_ident, 1)
            dve.tensor_scalar(negident[:, :], ident[:, :], -1.0, None, ALU.mult).then_inc(s_ident, 1)
            for t in (lg0, lg1, rep0, rep1):
                last = dve.memset(t[:, :, :], LOWEST)
            last.then_inc(s_const, 1)
            dve.memset(cw[:, :, :, E1:E1 + 1], 1.0).then_inc(s_const, 1)

            for step in SCHEDULE:
                kind = step[0]
                if kind == "w0_turn":
                    dve.wait_ge(x_full[1], X_COUNT[1, step])
                    for n in range(2):
                        dve.tensor_copy(wT[0][:, n, :].rearrange("i (a d p) -> i a d p", a=2, d=8),
                                        X[1][:, n * D:(n + 1) * D].rearrange("i (p a d) -> i a d p", p=8, a=2))
                    dve.tensor_copy(wT[0][:, 2:4, :].rearrange("i n o -> i (n o)"), X[1][:, 2 * D:4 * D]).then_inc(x_read[1], 1)
                    dve.wait_ge(in_bias0, 48)
                    dve.tensor_scalar(bqs[:, :], bias3[:, 0:1], QSCALE, None, ALU.mult).then_inc(s_bqs, 1)
                elif kind == "stats":
                    _, stage, b = step
                    src = stage_in[stage]
                    if stage == "q0":
                        dve.wait_ge(in_x[b], 16)
                    elif stage == "q1":
                        dve.wait_ge(s_end0, b + 1)
                    elif stage == "o1":
                        dve.wait_ge(*xread(1, "out_turn", 1, b))
                    else:
                        dve.wait_ge(*xread(1, "out_proj", int(stage == "f1"), b))
                    for r in range(R):
                        last = dve.bn_stats(bst[:, r, :], src[:, b, r, :])
                    then(last)
                    for r in range(R):
                        last = dve.bn_aggr(mv[:, r, :], bst[:, r, :])
                    last.then_inc(s_stats, 1)
                elif kind == "norm":
                    _, stage, b = step
                    src = stage_in[stage]
                    dve.wait_ge(s_rstd, nth("stats", stage, b))
                    for r in range(R):
                        last = dve.tensor_scalar(hn[:, b, r, :], src[:, b, r, :], mv[:, r, 0:1], rstd[:, r:r + 1],
                                                 ALU.subtract, ALU.mult)
                    if stage in ("q0", "f0", "f1"):
                        last.then_inc(s_norm, 1)
                        continue
                    then(last)
                    if stage == "o1":
                        dve.wait_ge(in_gb, 48)
                        for r in range(R):
                            last = dve.tensor_tensor(hn[:, b, r, :], hn[:, b, r, :], gamma_b[:, :], ALU.mult)
                        then(last)
                        for r in range(R):
                            last = dve.tensor_tensor(hn[:, b, r, :], hn[:, b, r, :], beta_b[:, :], ALU.add)
                        then(last)
                    for r in range(R):
                        last = dve.tensor_tensor_reduce(junk[:, r, :], hn[:, b, r, :], hn[:, b, r, :], 1.0, 0.0, ALU.mult,
                                                        ALU.add, sumsq[:, r:r + 1])
                    last.then_inc(s_sq, 1)
                    then(dve.tensor_reduce(amax[:, :], hn[:, b, :, :], AX, ALU.max, apply_absolute_value=True))
                elif kind == "quant":
                    _, stage, b = step
                    dve.wait_ge(s_rms, nth(*step))
                    then(dve.tensor_tensor(mxn[:, :], amax[:, :], rms[:, :], ALU.mult))
                    then(dve.tensor_scalar(mxn[:, :], mxn[:, :], 1e-5, None, ALU.max))
                    then(dve.reciprocal(inv[:, :], mxn[:, :]))
                    dve.tensor_scalar(dq[:, :], mxn[:, :], 1.0 / 127.0, None, ALU.mult)
                    then(dve.scalar_tensor_tensor(qs[:, :], inv[:, :], 127.0, rms[:, :], ALU.mult, ALU.mult))
                    for r in range(R):
                        last = dve.tensor_scalar(hn[:, b, r, :], hn[:, b, r, :], qs[:, r:r + 1], MAGIC, ALU.mult, ALU.add)
                    then(last)
                    for r in range(R):
                        last = dve.tensor_scalar(hn[:, b, r, :], hn[:, b, r, :], -MAGIC, dq[:, r:r + 1], ALU.add, ALU.mult)
                    last.then_inc(s_quant, 1)
                elif kind == "turn":
                    _, stage, b = step
                    dve.wait_ge(x_full[0], X_COUNT[0, step])
                    dve.tensor_copy(hT[:, b, :], X[0][:, 0:NQ]).then_inc(x_read[0], 1)
                elif kind == "kproj":
                    _, n, b = step
                    rows = P // (n + 1)
                    dve.wait_ge(*xread(0, *step))
                    if nth(*step) > 1:
                        pn, pb = ((0, 0), (0, 1), (1, 0))[nth(*step) - 2]
                        dve.wait_ge(s_kst[pn][pb], 16 * 12)
                    split(kf[0:rows, :], kr[0:rows, :], kp[0:rows, :, :], s_kp)
                elif kind == "qproj":
                    _, n, b = step
                    dve.wait_ge(*xread(1, *step))
                    if nth(*step) > 1:
                        pn, pb = ((0, 0), (0, 1), (1, 0))[nth(*step) - 2]
                        dve.wait_ge(s_qst[pn][pb], 16 * 12)
                    split(qf[:, :], qr[:, :], qp[:, :, :], s_qp)
                elif kind == "scores":
                    _, g, i = step
                    for r in range(R):
                        n = 8 * g + 2 * i + r
                        if i == 0 and g >= 2:
                            dve.wait_ge(s_mb_full, g - 1)
                        dve.wait_ge(s_sa_full, n + 1)
                        dve.tensor_reduce(mx[:, g % 2, r, i:i + 1], SA[r][:, :], AX, ALU.max).then_inc(s_sa_max, 1)
                elif kind == "bias_turn":
                    dve.wait_ge(x_full[0], X_COUNT[0, step])
                    dve.tensor_copy(b1T[:, :], X[0][:, 0:E0 * FC])
                    dve.tensor_copy(e1T[:, :], X[0][:, 64:64 + E1 + 1]).then_inc(x_read[0], 1)
                    dve.wait_ge(in_route, 16 * 9)
                    dve.tensor_tensor_reduce(wgsq[:, :], wgn[:, :], wgn[:, :], 1.0, 0.0, ALU.mult, ALU.add,
                                             wgs[:, 0:1]).then_inc(s_wgsq, 1)
                elif kind == "ctx_measure":
                    dve.wait_ge(s_csq, 1)
                    dve.tensor_reduce(cstat[:, 0, :], csq[:, :, :], AX, ALU.add)
                    dve.tensor_reduce(cstat[:, 1, :], cx[:, :, :], AX, ALU.max, apply_absolute_value=True).then_inc(s_csq, 1)
                elif kind == "ctx_quant":
                    dve.wait_ge(s_csq, 2)
                    dve.wait_ge(s_cstat, 1)
                    then(dve.tensor_tensor(cstat[:, 4, :], cstat[:, 1, :], cstat[:, 3, :], ALU.mult))
                    then(dve.tensor_scalar(cstat[:, 4, :], cstat[:, 4, :], 1e-5, None, ALU.max))
                    then(dve.reciprocal(cstat[:, 5, :], cstat[:, 4, :]))
                    then(dve.scalar_tensor_tensor(cstat[:, 5, :], cstat[:, 5, :], 127.0, cstat[:, 3, :], ALU.mult, ALU.mult))
                    dve.tensor_scalar(cstat[:, 6, :], cstat[:, 4, :], 1.0 / 127.0, None, ALU.mult).then_inc(s_cstat, 1)
                    dve.wait_ge(s_wgnorm, 1)
                    then(dve.tensor_scalar(wgs[:, 1:2], wgs[:, 1:2], 1e-4, None, ALU.max))
                    then(dve.reciprocal(wgs[:, 2:3], wgs[:, 1:2]))
                    dve.tensor_scalar(wgn[:, :], wgn[:, :], wgs[:, 2:3], None, ALU.mult).then_inc(s_wgn, 1)
                elif kind == "w1_measure":
                    dve.wait_ge(in_w1n, 64)
                    dve.tensor_reduce(wsum[:, :], w1n[:, :, :], AX, ALU.add, apply_absolute_value=True).then_inc(s_wabs, 1)
                    dve.wait_ge(x_full[1], X_COUNT[1, step])
                    for n, size in enumerate((D * D, D * D // 2, D * D)):
                        last = dve.tensor_scalar(walpha[:, n:n + 1], X[1][:, n:n + 1], 1.0 / size, 1e-5, ALU.mult, ALU.max)
                    last.then_inc(x_read[1], 1)
                    dve.wait_ge(*xread(1, *step))
                    dve.reciprocal(winv[:, :], walpha[:, :]).then_inc(s_walpha, 1)
                elif kind == "w1_turn":
                    dve.wait_ge(x_full[1], X_COUNT[1, step])
                    dve.tensor_copy(wT[1][:, 0, 0:64].rearrange("i (a d r) -> i a d r", a=2, d=8),
                                    X[1][:, D:D + 64].rearrange("i (r a d) -> i a d r", r=4, a=2))
                    dve.tensor_copy(wT[1][:, 2, 0:64], X[1][:, D + 64:2 * D])
                    for a in range(2):
                        dve.tensor_copy(wT[1][:, 1, 64 * a:64 * a + 64].rearrange("i (d r g) -> i d r g", d=8, r=4),
                                        X[1][:, 0:D].rearrange("i (r a g d) -> i a d r g", r=4, a=2, g=2)[:, a])
                    dve.tensor_copy(wT[1][:, 3, :], X[1][:, 2 * D:3 * D])
                    dve.tensor_copy(wgT[:, :], X[1][0:GD, 3 * D:3 * D + E0]).then_inc(x_read[1], 1)
                elif kind == "out_turn":
                    _, n, b = step
                    for r in range(R):
                        dve.wait_ge(x_full[r], X_COUNT[r, step])
                        slots = X[r][:, :].rearrange("q (s c) -> q s c", c=32)
                        then(dve.reciprocal(rsum[:, r, :], slots[:, :, DH]))
                        for a in range(2):
                            src = slots[:, 8 * a:8 * a + 8, 0:DH]
                            w = rsum[:, r, 8 * a:8 * a + 8].unsqueeze(2).broadcast_to([P, 8, DH])
                            if n == 0:
                                dst = att[:, b, r, :].rearrange("q (p a d) -> q a p d", p=8, a=2)[:, a]
                            else:
                                src = src.rearrange("q (r g) d -> q r g d", g=2)
                                w = w.rearrange("q (r g) d -> q r g d", g=2)
                                dst = att[:, b, r, :].rearrange("q (r a g d) -> q a r g d", r=4, a=2, g=2)[:, a]
                            last = dve.tensor_tensor(dst, src, w, ALU.mult)
                        if r == 0:
                            last.then_inc(x_read[0], 1)
                        else:
                            last.then_inc(x_read[1], 1)
                elif kind == "att_turn":
                    _, n, b = step
                    dve.wait_ge(x_full[0], X_COUNT[0, step])
                    if n == 0:
                        dve.tensor_scalar(attT[:, b, :], X[0][:, 0:NQ], bias3[:, 2:3], None, ALU.add).then_inc(x_read[0], 1)
                    else:
                        dve.tensor_copy(attT[:, b, :], X[0][:, 0:NQ]).then_inc(x_read[0], 1)
                elif kind == "out_proj":
                    _, n, b = step
                    dve.wait_ge(x_full[1], X_COUNT[1, step])
                    if n == 0:
                        dve.wait_ge(s_xres, 1)
                    dst, res = ((x1, xres), (x3, x2))[n]
                    dve.tensor_tensor(dst[:, b].rearrange("p r d -> p (r d)"), X[1][:, 0:NQ],
                                      res[:, b].rearrange("p r d -> p (r d)"), ALU.add).then_inc(x_read[1], 1)
                elif kind == "red0":
                    b = step[1]
                    dve.wait_ge(x_full[0], X_COUNT[0, step])
                    dve.tensor_copy(redT[:, :], X[0][0:GD, 0:NQ]).then_inc(x_read[0], 1)
                elif kind == "logits0":
                    b = step[1]
                    dve.wait_ge(s_const, 5)
                    dve.wait_ge(x_full[1], X_COUNT[1, step])
                    logits = X[1][:, 0:R * E0].rearrange("p (r e) -> p r e", r=R)
                    dve.tensor_copy(lgk0[:, b, :, :], logits)
                    dve.tensor_copy(lg0[:, :, 0:E0], logits).then_inc(x_read[1], 1)
                    dve.wait_ge(*xread(1, *step))
                    for r in range(R):
                        last = dve.max(top0[:, r, :], lg0[:, r, :])
                    then(last)
                    dve.tensor_scalar(ntop0[:, b, :], top0[:, :, 0], -1.0, None, ALU.mult).then_inc(s_gate, 1)
                    then(dve.tensor_copy(rep0[:, :, 0:1], top0[:, :, 0:1]))
                    for r in range(R):
                        last = dve.match_replace(mr0[:, r, :], rep0[:, r, :], lg0[:, r, :], MARK)
                    then(last)
                    dve.tensor_tensor(oh0[:, b, :, :], mr0[:, :, 0:E0], lg0[:, :, 0:E0], ALU.not_equal).then_inc(s_cw, 1)
                elif kind == "pick0":
                    b = step[1]
                    dve.wait_ge(x_full[0], X_COUNT[0, step])
                    dve.tensor_copy(ohT[:, :], X[0][0:E0, 0:NQ]).then_inc(x_read[0], 1)
                    dve.wait_ge(x_full[1], X_COUNT[1, step])
                    dve.tensor_copy(acc[:, b].rearrange("p r d -> p (r d)"), X[1][:, 0:NQ]).then_inc(x_read[1], 1)
                elif kind == "output0":
                    _, b, e, r = step
                    n = R * (b * E0 + e) + r
                    dve.wait_ge(s_y0_full, n + 1)
                    if e == 0:
                        dve.wait_ge(*xread(1, "pick0", b))
                    else:
                        dve.wait_ge(s_y0, n - 1)
                    dve.scalar_tensor_tensor(acc[:, b, r, :], YB[r][:, 0:D], oh0[:, b, r, e:e + 1], acc[:, b, r, :],
                                             ALU.mult, ALU.add).then_inc(s_y0, 1)
                elif kind == "end0":
                    b = step[1]
                    dve.wait_ge(s_pick, GATE_EXP0[b] + R)
                    dve.wait_ge(s_y0, (b + 1) * E0 * R)
                    then(dve.reciprocal(score0[:, b, :], gsum0[:, b, :]))
                    for r in range(R):
                        last = dve.scalar_tensor_tensor(x2[:, b, r, :], acc[:, b, r, :], score0[:, b, r:r + 1],
                                                        x1[:, b, r, :], ALU.mult, ALU.add)
                    last.then_inc(s_end0, 1)
                elif kind == "logits1":
                    b = step[1]
                    dve.wait_ge(x_full[1], X_COUNT[1, step])
                    dve.tensor_tensor(lg1[:, :, 0:E1], X[1][:, 0:R * E1].rearrange("p (r e) -> p r e", r=R),
                                      rb_b[:, :].unsqueeze(1).broadcast_to([P, R, E1]), ALU.add).then_inc(x_read[1], 1)
                    dve.wait_ge(*xread(1, *step))
                    for r in range(R):
                        last = dve.max(top1[:, r, :], lg1[:, r, :])
                    then(last)
                    dve.tensor_scalar(ntop1[:, :], top1[:, :, 0], -1.0, None, ALU.mult).then_inc(s_gate, 1)
                    then(dve.tensor_copy(rep1[:, :, 0:TOP], top1[:, :, 0:TOP]))
                    for r in range(R):
                        last = dve.match_replace(mr1[:, r, :], rep1[:, r, :], lg1[:, r, :], MARK)
                    then(last)
                    then(dve.tensor_tensor(sel1[:, :, :], mr1[:, :, 0:E1], lg1[:, :, 0:E1], ALU.not_equal))
                elif kind == "pick1":
                    b = step[1]
                    dve.wait_ge(s_pick, EXP1[b])
                    then(dve.reciprocal(rsum1[:, :], gsum1[:, :]))
                    for r in range(R):
                        last = dve.scalar_tensor_tensor(cw[:, b, r, 0:E1], ge1[:, r, :], rsum1[:, r:r + 1], sel1[:, r, :],
                                                        ALU.mult, ALU.mult)
                    last.then_inc(s_cw, 1)
                    dve.wait_ge(x_full[0], X_COUNT[0, step])
                    dve.tensor_copy(cwT[:, :], X[0][0:E1 + 1, 0:NQ]).then_inc(x_read[0], 1)
                    dve.wait_ge(x_full[1], X_COUNT[1, step])
                    dve.tensor_tensor(acc[:, b].rearrange("p r d -> p (r d)"), X[1][:, 0:NQ],
                                      x3[:, b].rearrange("p r d -> p (r d)"), ALU.add).then_inc(x_read[1], 1)
                elif kind == "output1":
                    _, b, e, r = step
                    n = R * (b * (E1 + 1) + e) + r
                    dve.wait_ge(s_y1_full, n + 1)
                    if e == 0:
                        dve.wait_ge(*xread(1, "pick1", b))
                    else:
                        dve.wait_ge(s_y1, n - 1)
                    dve.scalar_tensor_tensor(acc[:, b, r, :], YB[r][:, 0:D], cw[:, b, r, e:e + 1], acc[:, b, r, :],
                                             ALU.mult, ALU.add).then_inc(s_y1, 1)

        @block.tensor
        def _(pe):
            pe.wait_ge(s_ident, 2)
            pe.wait_ge(s_const, 3)

            def fill(bank, step):
                n = X_COUNT[bank, step]
                if n > 1:
                    pe.wait_ge(x_read[bank], n - 1)

            for step in SCHEDULE:
                kind = step[0]
                if kind == "ctx_turn" or kind == "ctxq_turn":
                    c = step[1]
                    src = cx if kind == "ctx_turn" else csq
                    fill(c, step)
                    if kind == "ctx_turn":
                        pe.wait_ge(in_ctx[c], 16)
                    else:
                        pe.wait_ge(s_cq, 1)
                    for k in range(KT):
                        last = pe.transpose(X[c][:, k * P:(k + 1) * P], src[:, c * KT + k, :], ident[:, :])
                    last.then_inc(x_full[c], 1)
                elif kind == "w0_turn":
                    fill(1, step)
                    pe.wait_ge(in_w0, 64)
                    for n in range(4):
                        last = pe.transpose(X[1][:, n * D:(n + 1) * D], w0n[:, n, :], ident[:, :])
                    last.then_inc(x_full[1], 1)
                elif kind == "w1_measure":
                    fill(1, step)
                    pe.wait_ge(s_wabs, 1)
                    for n in range(3):
                        last = pe.matmul(X[1][:, n:n + 1], (halves if n == 1 else ones)[:, :], wsum[:, n:n + 1],
                                         start=True, stop=True)
                    last.then_inc(x_full[1], 1)
                elif kind == "w1_turn":
                    fill(1, step)
                    pe.wait_ge(s_wtern, 1)
                    for n in range(3):
                        pe.transpose(X[1][:, n * D:(n + 1) * D], w1t[:, n, :], ident[:, :])
                    pe.wait_ge(s_wgn, 1)
                    pe.transpose(X[1][0:GD, 3 * D:3 * D + E0], wgn[:, :], ident[0:E0, 0:E0]).then_inc(x_full[1], 1)
                elif kind == "bias_turn":
                    fill(0, step)
                    pe.wait_ge(in_route, 16 * 9)
                    pe.transpose(X[0][:, 0:E0 * FC], b1r[:, :], ident[0:E0 * FC, 0:E0 * FC])
                    pe.transpose(X[0][:, 64:64 + E1 + 1], e1r[:, :], ident[0:E1 + 1, 0:E1 + 1]).then_inc(x_full[0], 1)
                elif kind == "turn":
                    _, stage, b = step
                    fill(0, step)
                    if stage in ("q0", "f0", "f1"):
                        pe.wait_ge(s_norm, NORM.index(("norm", stage, b)) + 1)
                    else:
                        pe.wait_ge(s_quant, nth("quant", stage, b))
                    for r in range(R):
                        last = pe.transpose(X[0][:, r * P:(r + 1) * P], hn[:, b, r, :], ident[:, :])
                    last.then_inc(x_full[0], 1)
                elif kind == "kproj":
                    _, n, b = step
                    fill(0, step)
                    pe.wait_ge(*xread(1, ("w0_turn", "w1_turn")[n]))
                    pe.wait_ge(*xread(b, ("ctx_turn", "ctxq_turn")[n], b))
                    rows = P // (n + 1)
                    pe.matmul(X[0][0:rows, :], wT[n][:, 0, 0:rows], ctxT[:, b * NK:(b + 1) * NK],
                              start=True, stop=True).then_inc(x_full[0], 1)
                elif kind == "vproj":
                    _, n, b = step
                    fill(1, step)
                    pe.wait_ge(*xread(b, ("ctx_turn", "ctxq_turn")[n], b))
                    w = D // (n + 1)
                    for k in range(KT):
                        last = pe.matmul(X[1][:, k * w:(k + 1) * w], ctxT[:, b * NK + k * P:b * NK + (k + 1) * P],
                                         wT[n][:, 2, 0:w], start=True, stop=True)
                    last.then_inc(x_full[1], 1)
                elif kind == "qproj":
                    _, n, b = step
                    fill(1, step)
                    pe.wait_ge(*xread(0, "turn", ("q0", "q1")[n], b))
                    pe.matmul(X[1][:, 0:NQ], wT[n][:, 1, :], hT[:, b, :], start=True, stop=True).then_inc(x_full[1], 1)
                elif kind == "scores":
                    _, gg, i = step
                    n, b, g = split_group(gg)
                    if i == 0 and g == 0:
                        pe.wait_ge(s_kst[n][b], 16 * 12)
                        pe.wait_ge(s_qst[n][b], 16 * 12)
                    s = 4 * g + i
                    for r in range(R):
                        u = 8 * gg + 2 * i + r
                        if u >= 2:
                            pe.wait_ge(s_sa_max, u - 1)
                        pe.matmul(SA[r][:, :], Q[n][:, b, s, r * P:(r + 1) * P], K[n][:, b, key_group(n, s), :],
                                  start=True, stop=True).then_inc(s_sa_full, 1)
                elif kind == "max_rows":
                    g = step[1]
                    pe.wait_ge(s_sa_max, 8 * (g + 1))
                    if g:
                        pe.wait_ge(s_mb_read, g)
                    if g == 8:
                        pe.wait_ge(s_y0, B * E0 * R)
                    for r in range(R):
                        last = pe.matmul(MB[0:4, r * P:(r + 1) * P], mx[:, g % 2, r, :], negident[:, :], start=True, stop=True)
                    last.then_inc(s_mb_full, 1)
                elif kind == "exp":
                    _, gg, i = step
                    n, b, g = split_group(gg)
                    s = 4 * g + i
                    if i == 0:
                        pe.wait_ge(s_shift, 16 * (gg + 1))
                    if gg == 8 and i == 0:
                        pe.wait_ge(s_h0, 2 * B * E0)
                    for u in range(2):
                        m = 8 * gg + 2 * i + u
                        if m >= 2:
                            pe.wait_ge(s_exp, m - 1)
                        for k in range(2):
                            kt = 2 * u + k
                            last = pe.matmul(SB[u][:, k * NQ:(k + 1) * NQ],
                                             K[n][:, b, key_group(n, s), kt * P:(kt + 1) * P], Q[n][:, b, s, :],
                                             start=True, stop=True)
                        last.then_inc(s_sb_full, 1)
                elif kind == "values":
                    _, gg, kt = step
                    n, b, g = split_group(gg)
                    if kt == 0:
                        pe.wait_ge(s_exp, 8 * (gg + 1))
                        pe.wait_ge(*xread(1, "vproj", n, b))
                        if gg:
                            pe.wait_ge(s_ob_read, gg)
                        if gg == 8:
                            pe.wait_ge(s_y0, B * E0 * R)
                    for j in range(4):
                        last = pe.matmul(OB[32 * j:32 * j + 32, 0:NQ], V[n][:, b, kt, value_head(n, 4 * g + j), :],
                                         prob[:, gg % 2, j, kt, :], start=(kt == 0), stop=(kt == KT - 1))
                    if kt == KT - 1:
                        last.then_inc(s_ob_full, 1)
                elif kind == "out_turn":
                    _, n, b = step
                    pe.wait_ge(s_ob_read, 8 * n + NG * (b + 1))
                    for r in range(R):
                        fill(r, step)
                        for g in range(NG):
                            last = pe.transpose(X[r][:, g * P:(g + 1) * P], oT[:, g, r * P:(r + 1) * P], ident[:, :])
                        last.then_inc(x_full[r], 1)
                elif kind == "att_turn":
                    _, n, b = step
                    fill(0, step)
                    if n == 0:
                        pe.wait_ge(*xread(1, "out_turn", n, b))
                    else:
                        pe.wait_ge(s_quant, nth("quant", "o1", b))
                    for r in range(R):
                        last = pe.transpose(X[0][:, r * P:(r + 1) * P], (att, hn)[n][:, b, r, :], ident[:, :])
                    last.then_inc(x_full[0], 1)
                elif kind == "out_proj":
                    _, n, b = step
                    fill(1, step)
                    pe.wait_ge(*xread(0, "att_turn", n, b))
                    for r in range(R):
                        last = pe.matmul(X[1][:, r * D:(r + 1) * D], attT[:, b, r * P:(r + 1) * P], wT[n][:, 3, :],
                                         start=True, stop=True)
                    last.then_inc(x_full[1], 1)
                elif kind == "red0":
                    b = step[1]
                    fill(0, step)
                    pe.wait_ge(*xread(0, "turn", "f0", b))
                    pe.matmul(X[0][0:GD, 0:NQ], wreds[:, :], hT[:, b, :], start=True, stop=True).then_inc(x_full[0], 1)
                elif kind == "logits0":
                    b = step[1]
                    fill(1, step)
                    pe.wait_ge(*xread(0, "red0", b))
                    for r in range(R):
                        last = pe.matmul(X[1][:, r * E0:(r + 1) * E0], redT[:, r * P:(r + 1) * P], wgT[:, :], start=True, stop=True)
                    last.then_inc(x_full[1], 1)
                elif kind == "pick0":
                    b = step[1]
                    fill(0, step)
                    pe.wait_ge(s_cw, CW_AT["logits0", b])
                    for r in range(R):
                        last = pe.transpose(X[0][0:E0, r * P:(r + 1) * P], oh0[:, b, r, :], ident[:, :])
                    last.then_inc(x_full[0], 1)
                    fill(1, step)
                    pe.wait_ge(*xread(0, *step))
                    for r in range(R):
                        last = pe.matmul(X[1][:, r * D:(r + 1) * D], ohT[:, r * P:(r + 1) * P], b2r[:, :], start=True, stop=True)
                    last.then_inc(x_full[1], 1)
                elif kind == "hidden0":
                    _, b, e, q = step
                    n = b * E0 + e
                    if n == 0 and q == 0:
                        pe.wait_ge(s_exp, 64)
                        pe.wait_ge(in_f0, 64)
                    if n >= 1:
                        pe.wait_ge(s_h0, 2 * n + q - 1)
                    for c in range(2 * q, 2 * q + 2):
                        last = pe.matmul(SB[q][:, (c % 2) * NQ:(c % 2 + 1) * NQ], w1s[:, e, c * P:(c + 1) * P], hT[:, b, :],
                                         start=True, stop=True)
                    last.then_inc(s_h0_full, 1)
                elif kind == "output0":
                    _, b, e, r = step
                    n = b * E0 + e
                    pe.wait_ge(s_h0, 2 * n + 2)
                    if n == 0 and r == 0:
                        pe.wait_ge(s_ob_read, 8)
                        pe.wait_ge(s_mb_read, 8)
                    if n >= 1:
                        pe.wait_ge(s_y0, R * n + r - 1)
                    for c in range(FC):
                        last = pe.matmul(YB[r][:, 0:D], hid[:, n % 2, c, r * P:(r + 1) * P], w2s[:, e, c, :],
                                         start=(c == 0), stop=(c == FC - 1))
                    last.then_inc(s_y0_full, 1)
                elif kind == "logits1":
                    b = step[1]
                    fill(1, step)
                    pe.wait_ge(*xread(0, "turn", "f1", b))
                    for r in range(R):
                        last = pe.matmul(X[1][:, r * E1:(r + 1) * E1], hT[:, b, r * P:(r + 1) * P], rWs[:, :], start=True, stop=True)
                    last.then_inc(x_full[1], 1)
                elif kind == "pick1":
                    b = step[1]
                    fill(0, step)
                    pe.wait_ge(s_cw, CW_AT["pick1", b])
                    for r in range(R):
                        last = pe.transpose(X[0][0:E1 + 1, r * P:(r + 1) * P], cw[:, b, r, :], ident[:, :])
                    last.then_inc(x_full[0], 1)
                    fill(1, step)
                    pe.wait_ge(*xread(0, *step))
                    for r in range(R):
                        last = pe.matmul(X[1][:, r * D:(r + 1) * D], cwT[:, r * P:(r + 1) * P], e2r[:, :], start=True, stop=True)
                    last.then_inc(x_full[1], 1)
                elif kind == "hidden1":
                    _, b, e = step
                    n = b * (E1 + 1) + e
                    if n == 0:
                        pe.wait_ge(s_exp, 128)
                        pe.wait_ge(in_f1, 64)
                    if n >= 2:
                        pe.wait_ge(s_h1, n - 1)
                    pe.matmul(SB[n % 2][:, 0:NQ], e1w[:, e, :], hT[:, b, :], start=True, stop=True).then_inc(s_h1_full, 1)
                elif kind == "output1":
                    _, b, e, r = step
                    n = b * (E1 + 1) + e
                    pe.wait_ge(s_h1, n + 1)
                    if n == 0 and r == 0:
                        pe.wait_ge(s_ob_read, GQ)
                        pe.wait_ge(s_mb_read, GQ)
                    if n >= 1:
                        pe.wait_ge(s_y1, R * n + r - 1)
                    pe.matmul(YB[r][:, 0:D], hid[:, n % 2, 0, r * P:(r + 1) * P], e2w[:, e, :],
                              start=True, stop=True).then_inc(s_y1_full, 1)


def _counts():
    gate, pick, cws = 0, 0, 0
    logits0, logits1, gexp0, exp1, cw_at = {}, {}, {}, {}, {}
    norm, normq = [], []
    for s in SCHEDULE:
        if s[0] == "norm":
            (norm if s[1] in ("q0", "f0", "f1") else normq).append(s)
        if s[0] in ("logits0", "logits1"):
            gate += 1
            (logits0 if s[0] == "logits0" else logits1)[s[1]] = gate
        if s[0] == "gate_exp0":
            gexp0[s[1]] = pick
            pick += R
        if s[0] == "logits1":
            pick += R
            exp1[s[1]] = pick
        if s[0] in ("logits0", "pick1"):
            cws += 1
            cw_at[s[0], s[1]] = cws
    return logits0, logits1, gexp0, exp1, cw_at, norm, normq


LOGITS0, LOGITS1, GATE_EXP0, EXP1, CW_AT, NORM, NORMQ = _counts()


_INS = ["x", "ctx_1024", "L0_xattn_Wq", "L0_xattn_bq", "L0_xattn_Wk", "L0_xattn_bk", "L0_xattn_Wv", "L0_xattn_bv",
        "L0_xattn_Wo", "L0_xattn_bo", "L0_ffn_w_red", "L0_ffn_wg", "L0_ffn_w1", "L0_ffn_b1", "L0_ffn_w2", "L0_ffn_b2",
        "L1_xattn_wq", "L1_xattn_wk", "L1_xattn_wv", "L1_xattn_wo", "L1_xattn_ln_gamma", "L1_xattn_ln_beta",
        "L1_ffn_router_W", "L1_ffn_router_b", "L1_ffn_sW1", "L1_ffn_sb1", "L1_ffn_sW2", "L1_ffn_sb2",
        "L1_ffn_eW1", "L1_ffn_eb1", "L1_ffn_eW2", "L1_ffn_eb2"]


def kernel(**inputs):
    import concourse.bacc as _bacc
    from concourse.bass_utils import run_bass_kernel_spmd as _run

    nc = _bacc.Bacc("TRN2", target_bir_lowering=False, num_devices=1)
    arrays, args = {}, []
    for name in _INS:
        a = np.ascontiguousarray(inputs[name])
        arrays[f"in_{name}_dram"] = a
        args.append(nc.dram_tensor(f"in_{name}_dram", a.shape, mybir.dt.from_np(a.dtype), kind="ExternalInput").ap())
    args.append(nc.dram_tensor("out_0_dram", (B, NQ, D), F32, kind="ExternalOutput").ap())
    transformer(nc, *args)
    r = _run(nc, [arrays], core_ids=[0])
    return r.results[0]["out_0_dram"]
```

```python
from contextlib import ExitStack

import numpy as np

import concourse.bass as bass
from concourse import mybir

F32 = mybir.dt.float32
BF16 = mybir.dt.bfloat16
U32 = mybir.dt.uint32
ALU = mybir.AluOpType
ACT = mybir.ActivationFunctionType
AX = mybir.AxisListType.X

P = 128
D = 128
B = 2
R = 2
NQ = R * P
NK = 512
KT = NK // P
H = 16
DH = D // H
NG = H // 4
E0, F0, GD = 8, 512, 16
FC = F0 // P
E1 = 15
TOP = 3
QSCALE = float(1.0 / np.sqrt(DH))
LN_EPS = 1e-5
MAGIC = 1.5 * 2.0 ** 23
TWO_ONES = float(np.array([0x3F803F80], np.uint32).view(np.float32)[0])
LOWEST = -3.0e38
MARK = 3.0e38

K_PART = (0, 1, 2, 0, 1, 0)
Q_PART = (0, 0, 0, 1, 1, 2)
K_RUNS = ((0, 3, 0, True), (3, 2, 0, True), (5, 1, 0, True))
Q_RUNS = ((0, 3, 0, False), (3, 2, 1, False), (5, 1, 2, False))
SHIFT_ROW = 8 * len(K_PART)


def value_head(layer, s):
    a, p = divmod(s, 8)
    return 2 * p + a if layer == 0 else 2 * (p // 2) + a


def key_group(layer, s):
    return s % 8 if layer == 0 else (s % 8) // 2


PROLOGUE = [("ctx_turn", 0), ("stats", "q0", 0), ("norm", "q0", 0), ("w0_turn",), ("kwrite", 0, 0),
    ("turn", "q0", 0), ("kproj", 0, 0), ("qproj", 0, 0), ("stats", "q0", 1), ("kstack", 0, 0), ("ctx_turn", 1),
    ("qstack", 0, 0), ("norm", "q0", 1), ("bulk",), ("turn", "q0", 1), ("vproj", 0, 0), ("load_small",),
    ("kproj", 0, 1), ("kwrite", 0, 1), ("load_w1",), ("qproj", 0, 1), ("qstack", 0, 1), ("kstack", 0, 1)]
BETWEEN = [("end0", 1), ("max_rows", 8), ("stats", "q1", 1), ("scores", 9, 2), ("norm", "q1", 1), ("scores", 9, 3),
    ("quant", "q1", 1)]
IN_ATTENTION0 = {
    (-2, 0): [("vproj", 0, 1)],
    (0, 1): [("ctx_measure",), ("load_expert", 0)],
    (0, 3): [("ctx_quant",), ("bias_turn",)],
    (1, 1): [("w1_measure",), ("load_expert", 1)],
    (2, 0): [("wg_norm",), ("w1_quant",)],
    (2, 1): [("w1_turn",)],
    (2, 2): [("ctxq_turn", 1), ("ctxq_turn", 0), ("load_expert", 2)],
    (3, 1): [("load_expert", 3), ("kproj", 1, 0), ("vproj", 1, 1)],
    (3, 2): [("vproj", 1, 0)],
    (4, 1): [("kwrite", 1, 0), ("kstack", 1, 0)],
    (4, 3): [("kproj", 1, 1), ("load_expert", 4)],
    (5, 0): [("out_turn", 0, 0), ("load_expert", 5)],
    (5, 1): [("att_turn", 0, 0)],
    (5, 2): [("out_proj", 0, 0), ("stats", "f0", 0)],
    (5, 3): [("load_expert", 6), ("norm", "f0", 0), ("kwrite", 1, 1)],
    (6, 0): [("turn", "f0", 0)],
    (6, 1): [("red0", 0), ("load_expert", 7)],
    (6, 2): [("logits0", 0), ("kstack", 1, 1)],
    (7, 0): [("gate_exp0", 0)],
    (7, 1): [("pick0", 0)],
}
IN_EXPERTS00 = {
    (-1, 1): [("out_turn", 0, 1)],
    (0, 1): [("att_turn", 0, 1)],
    (1, 0): [("out_proj", 0, 1), ("stats", "f0", 1)],
    (1, 1): [("norm", "f0", 1)],
    (3, 0): [("turn", "f0", 1)],
    (3, 1): [("red0", 1)],
    (4, 0): [("logits0", 1)],
    (5, 0): [("pick0", 1)],
}
IN_EXPERTS01 = {
    (-1, 1): [("end0", 0), ("stats", "q1", 0)],
    (0, 1): [("norm", "q1", 0)],
    (1, 0): [("quant", "q1", 0)],
    (2, 0): [("turn", "q1", 0)],
    (2, 1): [("qproj", 1, 0), ("qstack", 1, 0)],
    (4, 0): [("gate_exp0", 1)],
    (4, 1): [("scores", 8, 0)],
    (5, 0): [("scores", 8, 1)],
    (5, 1): [("scores", 8, 2)],
    (6, 0): [("scores", 8, 3)],
    (6, 1): [("scores", 9, 0)],
    (7, 0): [("scores", 9, 1)],
}
IN_ATTENTION1 = {
    (8, 0): [("turn", "q1", 1)],
    (8, 2): [("qproj", 1, 1)],
    (9, 0): [("qstack", 1, 1)],
    (13, 0): [("out_turn", 1, 0), ("stats", "o1", 0)],
    (13, 1): [("norm", "o1", 0)],
    (13, 2): [("quant", "o1", 0)],
    (13, 3): [("att_turn", 1, 0)],
    (14, 0): [("out_proj", 1, 0)],
    (14, 2): [("stats", "f1", 0)],
    (15, 0): [("norm", "f1", 0), ("turn", "f1", 0)],
    (15, 1): [("logits1", 0)],
    (15, 3): [("pick1", 0)],
}
IN_EXPERTS10 = {
    -2: [("out_turn", 1, 1)],
    -1: [("stats", "o1", 1)],
    0: [("norm", "o1", 1)],
    2: [("quant", "o1", 1)],
    5: [("att_turn", 1, 1)],
    7: [("out_proj", 1, 1), ("stats", "f1", 1)],
    9: [("norm", "f1", 1)],
    11: [("turn", "f1", 1)],
    12: [("logits1", 1)],
    14: [("pick1", 1)],
}


def build_schedule():
    steps = []

    def attention(layer, first, last, extra):
        g0, g1 = 8 * layer, 8 * layer + 8
        for g in range(first, last):
            for i in range(4):
                if i == 1 and g0 <= g + 1 < g1:
                    steps.append(("max_rows", g + 1))
                if g0 <= g + 2 < g1:
                    steps.append(("scores", g + 2, i))
                if g0 <= g < g1:
                    steps.append(("exp", g, i))
                if g0 <= g - 1 < g1:
                    steps.append(("values", g - 1, i))
                steps.extend(extra.get((g, i), []))

    def experts0(b, extra):
        for e in range(-1, E0):
            for q in range(2):
                if e + 1 < E0:
                    steps.append(("hidden0", b, e + 1, q))
                if e >= 0:
                    steps.append(("output0", b, e, q))
                steps.extend(extra.get((e, q), []))

    def experts1(b, extra):
        for e in range(-2, E1 + 1):
            if e + 2 <= E1:
                steps.append(("hidden1", b, e + 2))
            if e >= 0:
                steps.append(("output1", b, e, 0))
                steps.append(("output1", b, e, 1))
            steps.extend(extra.get(e, []))
        steps.append(("store", b))

    steps.extend(PROLOGUE)
    attention(0, -2, 9, IN_ATTENTION0)
    experts0(0, IN_EXPERTS00)
    experts0(1, IN_EXPERTS01)
    steps.extend(BETWEEN)
    attention(1, 8, 17, IN_ATTENTION1)
    experts1(0, IN_EXPERTS10)
    experts1(1, {})
    return steps


SCHEDULE = build_schedule()

X_FILLS = {
    "ctx_turn": lambda s: [s[1]], "ctxq_turn": lambda s: [s[1]],
    "w0_turn": lambda s: [1], "kproj": lambda s: [0], "vproj": lambda s: [1], "turn": lambda s: [0],
    "qproj": lambda s: [1], "bias_turn": lambda s: [0], "w1_measure": lambda s: [1],
    "w1_turn": lambda s: [1], "out_turn": lambda s: [0, 1], "att_turn": lambda s: [0],
    "out_proj": lambda s: [1], "red0": lambda s: [0], "logits0": lambda s: [1],
    "pick0": lambda s: [0, 1], "logits1": lambda s: [1], "pick1": lambda s: [0, 1],
}
X_COUNT = {}
_seen = [0, 0]
for _s in SCHEDULE:
    for _x in X_FILLS.get(_s[0], lambda s: [])(_s):
        _seen[_x] += 1
        X_COUNT[_x, _s] = _seen[_x]

ORDER = {}
for _s in SCHEDULE:
    ORDER.setdefault(_s[0], []).append(_s)


def nth(*step):
    return ORDER[step[0]].index(step) + 1


def transformer(nc, x, ctx, Wq, bq, Wk, bk, Wv, bv, Wo, bo, w_red, wg, w1, b1, w2, b2, wq1, wk1, wv1, wo1,
                gamma, beta, rW, rb, sW1, sb1, sW2, sb2, eW1, eb1, eW2, eb2, out):
    with ExitStack() as stack:
        def sb(name, shape, dt=F32):
            return stack.enter_context(nc.sbuf_tensor(name, shape, dt))

        def sem(name):
            return stack.enter_context(nc.semaphore(name))

        stack.enter_context(nc.allow_low_precision(reason="exact splits into bfloat16 parts; the shift of a softmax cancels"))

        ident = sb("ident", [P, P])
        negident = sb("negident", [P, P], BF16)
        ones = sb("ones", [P, P])
        halves = sb("halves", [P, P])
        expo = sb("expo", [P, 8])
        expo_half = sb("expo_half", [P, 8])
        xin = sb("xin", [P, B, R, D])
        xres = sb("xres", [P, B, R, D])
        bo_b = sb("bo_b", [P, D])
        gamma_b = sb("gamma_b", [P, D])
        beta_b = sb("beta_b", [P, D])
        rb_b = sb("rb_b", [P, E1])
        x1 = xres
        x2 = sb("x2", [P, B, R, D])
        x3 = xin
        hn = sb("hn", [P, B, R, D])
        hT = sb("hT", [P, B, NQ])
        att = sb("att", [P, B, R, D])
        attT = sb("attT", [P, B, NQ])
        acc = sb("acc", [P, B, R, D])
        bst = sb("bst", [P, R, 6])
        mv = sb("mv", [P, R, 2])
        vareps = sb("vareps", [P, R])
        rstd = sb("rstd", [P, R])
        sumsq = sb("sumsq", [P, R])
        amax = sb("amax", [P, R])
        ms = sb("ms", [P, R])
        rms = sb("rms", [P, R])
        mxn = sb("mxn", [P, R])
        inv = sb("inv", [P, R])
        qs = sb("qs", [P, R])
        dq = sb("dq", [P, R])
        junk = sb("junk", [P, R, D])
        cx = sb("cx", [P, B * KT, D])
        ctxT = sb("ctxT", [P, B * NK])
        csq = sb("csq", [P, B * KT, D])
        cstat = sb("cstat", [P, 7, B * KT])
        w0n = sb("w0n", [P, 4, D])
        wT = [sb(f"wT{n}", [P, 4, D]) for n in range(2)]
        w1n = sb("w1n", [P, 3, D])
        w1t = w1n
        wsum = sb("wsum", [P, 3])
        walpha = sb("walpha", [P, 3])
        winv = sb("winv", [P, 3])
        bias3 = sb("bias3", [P, 3])
        bqs = sb("bqs", [P, 1])
        kf = sb("kf", [P, NK])
        kr = sb("kr", [P, NK])
        kp = sb("kp", [P, 3, NK], BF16)
        qf = sb("qf", [P, NQ])
        qr = sb("qr", [P, NQ])
        qp = sb("qp", [P, 3, NQ], BF16)
        K = [sb("K0", [P, B, 8, NK], BF16), sb("K1", [P, B, 4, NK], BF16)]
        Q = [sb(f"Q{n}", [P, B, H, NQ], BF16) for n in range(2)]
        V = [sb("V0", [P, B, KT, H, 32]), sb("V1", [P, B, KT, 8, 32])]
        prob = sb("prob", [P, 2, 4, KT, NQ])
        mx = sb("mx", [P, 2, R, 4], BF16)
        nm = sb("nm", [4, 2, NQ], BF16)
        oT = sb("oT", [P, NG, NQ])
        rsum = sb("rsum", [P, R, H])
        hid = prob[:, :, 0, :, :]
        hid1 = prob[:, 0, 0, :, :]
        w1s = sb("w1s", [P, E0, F0])
        w2s = sb("w2s", [P, E0, FC, D])
        b1r = sb("b1r", [E0 * FC, P])
        b1T = sb("b1T", [P, E0 * FC])
        b2r = sb("b2r", [E0, D])
        wreds = sb("wreds", [P, GD])
        wgn = sb("wgn", [E0, GD])
        wgsq = sb("wgsq", [E0, GD])
        wgs = sb("wgs", [E0, 3])
        wgT = sb("wgT", [GD, E0])
        redT = sb("redT", [GD, NQ])
        lg0 = sb("lg0", [P, R, E0 + 7])
        rep0 = sb("rep0", [P, R, 8])
        mr0 = sb("mr0", [P, R, E0 + 7])
        top0 = sb("top0", [P, R, 8])
        oh0 = sb("oh0", [P, B, R, E0])
        ntop0 = sb("ntop0", [P, B, R])
        lgk0 = sb("lgk0", [P, B, R, E0])
        ge0 = sb("ge0", [P, B, R, E0])
        gsum0 = sb("gsum0", [P, B, R])
        score0 = sb("score0", [P, B, R])
        ohT = sb("ohT", [E0, NQ])
        place = K[0][:, :, :, :].rearrange("p b g k -> p (b g k)").bitcast(F32)
        e1w, e2w = (place[:, n * (E1 + 1) * D:(n + 1) * (E1 + 1) * D].rearrange("p (e d) -> p e d", d=D) for n in range(2))
        e1r = sb("e1r", [E1 + 1, D])
        e1T = sb("e1T", [P, E1 + 1])
        e2r = sb("e2r", [E1 + 1, D])
        rWs = sb("rWs", [P, E1])
        lg1 = sb("lg1", [P, R, E1 + 5])
        rep1 = sb("rep1", [P, R, 8])
        mr1 = sb("mr1", [P, R, E1 + 5])
        top1 = sb("top1", [P, R, 8])
        sel1 = sb("sel1", [P, R, E1])
        ntop1 = sb("ntop1", [P, R])
        ge1 = sb("ge1", [P, R, E1])
        gsum1 = sb("gsum1", [P, R])
        rsum1 = sb("rsum1", [P, R])
        cw = sb("cw", [P, B, R, E1 + 1])
        cwT = sb("cwT", [E1 + 1, NQ])

        k_dram = [[nc.dram_tensor(f"k_dram{n}{b}", [6, 2, 64 // (n + 1), NK], BF16, kind="Internal").ap() for b in range(B)]
                  for n in range(2)]
        q_dram = [[nc.dram_tensor(f"q_dram{n}{b}", [6, 2, 64, NQ], BF16, kind="Internal").ap() for b in range(B)]
                  for n in range(2)]

        SA = [stack.enter_context(nc.psum_tensor(f"SA{n}", [P, 512], F32)) for n in range(2)]
        SB = [stack.enter_context(nc.psum_tensor(f"SB{n}", [P, 512], F32)) for n in range(2)]
        OB = stack.enter_context(nc.psum_tensor("OB", [P, 512], F32))
        MB = stack.enter_context(nc.psum_tensor("MB", [P, 512], F32))
        X = [stack.enter_context(nc.psum_tensor(f"X{n}", [P, 512], F32)) for n in range(2)]
        YB = [OB, MB]
        Y1 = [OB, MB, SA[0], SA[1]]

        in_x, in_ctx, in_w0, in_bias0 = [sem("in_x0"), sem("in_x1")], [sem("in_ctx0"), sem("in_ctx1")], sem("in_w0"), sem("in_bias0")
        in_bo, in_gb, in_w1n = sem("in_bo"), sem("in_gb"), sem("in_w1n")
        in_route, in_f0, in_f1 = sem("in_route"), sem("in_f0"), sem("in_f1")
        s_ident, s_const, s_pfill, s_vfill = sem("s_ident"), sem("s_const"), sem("s_pfill"), sem("s_vfill")
        x_full = [sem("x0_full"), sem("x1_full")]
        x_read = [sem("x0_read"), sem("x1_read")]
        s_sa_full, s_sa_max = sem("s_sa_full"), sem("s_sa_max")
        s_mb_full, s_mb_read, s_shift = sem("s_mb_full"), sem("s_mb_read"), sem("s_shift")
        s_sb_full, s_exp = sem("s_sb_full"), sem("s_exp")
        s_ob_full, s_ob_read = sem("s_ob_full"), sem("s_ob_read")
        s_kp, s_qp = sem("s_kp"), sem("s_qp")
        s_kwr = [[sem(f"s_kwr{n}{b}") for b in range(B)] for n in range(2)]
        s_qwr = [[sem(f"s_qwr{n}{b}") for b in range(B)] for n in range(2)]
        s_kst = [[sem(f"s_kst{n}{b}") for b in range(B)] for n in range(2)]
        s_qst = [[sem(f"s_qst{n}{b}") for b in range(B)] for n in range(2)]
        s_stats, s_rstd, s_norm, s_sq, s_rms, s_quant = (sem("s_stats"), sem("s_rstd"), sem("s_norm"), sem("s_sq"),
                                                         sem("s_rms"), sem("s_quant"))
        s_xres, s_bqs = sem("s_xres"), sem("s_bqs")
        s_csq, s_cstat, s_cq = sem("s_csq"), sem("s_cstat"), sem("s_cq")
        s_wabs, s_walpha, s_wtern = sem("s_wabs"), sem("s_walpha"), sem("s_wtern")
        s_wgsq, s_wgnorm, s_wgn = sem("s_wgsq"), sem("s_wgnorm"), sem("s_wgn")
        s_pick, s_gate, s_cw = sem("s_pick"), sem("s_gate"), sem("s_cw")
        s_h0_full, s_h0, s_y0_full, s_y0 = sem("s_h0_full"), sem("s_h0"), sem("s_y0_full"), sem("s_y0")
        s_h1_full, s_h1, s_y1_full, s_y1 = sem("s_h1_full"), sem("s_h1"), sem("s_y1_full"), sem("s_y1")
        s_end0 = sem("s_end0")
        s_stored = sem("s_stored")
        s_v, s_p = sem("s_v"), sem("s_p")

        GQ = 8 * 2
        stage_in = {"q0": xin, "f0": x1, "q1": x2, "o1": att, "f1": x3}

        def fill_view(t):
            return t.rearrange("p g k -> p (g k)").bitcast(F32)

        def xread(bank, *step):
            return x_read[bank], X_COUNT[bank, step]

        def split_group(g):
            return g // 8, g % 8 // NG, g % NG

        def split(engine, then, full, rest, parts, done):
            then(engine.tensor_copy(parts[:, 0, :], full))
            then(engine.tensor_tensor(rest, full, parts[:, 0, :], ALU.subtract))
            then(engine.tensor_copy(parts[:, 1, :], rest))
            engine.tensor_tensor(parts[:, 2, :], rest, parts[:, 1, :], ALU.subtract).then_inc(done, 1)

        block = stack.enter_context(nc.Block())

        @block.sync
        def _(sp):
            sp.dma_start(xin[:, 0, :, :], x[0].rearrange("(r p) d -> p r d", p=P)).then_inc(in_x[0], 16)
            for b in range(B):
                sp.dma_start(cx[:, b * KT:(b + 1) * KT, :], ctx[b].rearrange("(k p) d -> p k d", p=P)).then_inc(in_ctx[b], 16)
                if b == 0:
                    sp.dma_start(xin[:, 1, :, :], x[1].rearrange("(r p) d -> p r d", p=P)).then_inc(in_x[1], 16)

            def write_blocks(parts, runs, dram, written):
                rows, _, cols = parts.shape
                for j, m, part, rising in runs:
                    src = parts[:, part:part + m, :] if rising else parts[:, part:part + 1, :].broadcast_to([rows, m, cols])
                    sp.dma_start(dram[j:j + m].rearrange("m a r c -> (a r) m c"), src).then_inc(written, 16)

            def read_stack(dst, dram, done):
                for a in range(2):
                    sp.dma_start(dst(a)[64 * a:64 * a + SHIFT_ROW].rearrange("r s c -> r (s c)"),
                                 dram[:, a].rearrange("j (d s) c -> j d (s c)", d=DH)).then_inc(done, 16)

            for step in SCHEDULE:
                kind = step[0]
                if kind == "kwrite":
                    _, n, b = step
                    sp.wait_ge(s_kp, nth("kproj", n, b))
                    write_blocks(kp[0:P // (n + 1), :, :], K_RUNS, k_dram[n][b], s_kwr[n][b])
                elif kind == "qproj":
                    _, n, b = step
                    sp.wait_ge(s_qp, nth(*step))
                    write_blocks(qp[:, :, :], Q_RUNS, q_dram[n][b], s_qwr[n][b])
                elif kind == "kstack":
                    _, n, b = step
                    sp.wait_ge(s_kwr[n][b], 16 * len(K_RUNS))
                    if (n, b) == (0, 0):
                        sp.wait_ge(s_const, 1)
                    else:
                        sp.wait_ge(s_pfill, 2 if n == 0 else 5)
                    read_stack(lambda a: K[n][:, b, :, :], k_dram[n][b], s_kst[n][b])
                elif kind == "qstack":
                    _, n, b = step
                    sp.wait_ge(s_qwr[n][b], 16 * len(Q_RUNS))
                    if (n, b) == (0, 0):
                        sp.wait_ge(s_const, 4)
                    else:
                        sp.wait_ge(s_pfill, 3 if n == 0 else 6)
                    read_stack(lambda a: Q[n][:, b, 8 * a:8 * a + 8, :], q_dram[n][b], s_qst[n][b])
                elif kind == "load_w1":
                    sp.dma_start(w1n[:, 0, :], wq1).then_inc(in_w1n, 16)
                    sp.dma_start(w1n[0:64, 1, :], wk1).then_inc(in_w1n, 16)
                    sp.dma_start(w1n[64:128, 1, :], wv1).then_inc(in_w1n, 16)
                    sp.dma_start(w1n[:, 2, :], wo1).then_inc(in_w1n, 16)
                elif kind == "load_small":
                    sp.dma_start(b1r[:, :], b1.rearrange("e (c f) -> (e c) f", c=FC)).then_inc(in_route, 16)
                    sp.dma_start(b2r[:, :], b2).then_inc(in_route, 16)
                    sp.dma_start(wgn[:, :], wg).then_inc(in_route, 16)
                    sp.dma_start(wreds[:, :], w_red).then_inc(in_route, 16)
                    sp.dma_start(e1r[0:E1, :], eb1).then_inc(in_route, 16)
                    sp.dma_start(e1r[E1:E1 + 1, :], sb1.rearrange("(o d) -> o d", o=1)).then_inc(in_route, 16)
                    sp.dma_start(e2r[0:E1, :], eb2).then_inc(in_route, 16)
                    sp.dma_start(e2r[E1:E1 + 1, :], sb2.rearrange("(o d) -> o d", o=1)).then_inc(in_route, 16)
                    sp.dma_start(rWs[:, :], rW).then_inc(in_route, 16)
                    sp.dma_start(gamma_b[:, :], gamma.rearrange("(o d) -> o d", o=1).broadcast_to([P, D])).then_inc(in_gb, 16)
                    sp.dma_start(beta_b[:, :], beta.rearrange("(o d) -> o d", o=1).broadcast_to([P, D])).then_inc(in_gb, 16)
                    sp.dma_start(rb_b[:, :], rb.rearrange("(o d) -> o d", o=1).broadcast_to([P, E1])).then_inc(in_gb, 16)
                elif kind == "load_expert":
                    e = step[1]
                    sp.dma_start(w1s[:, e, :], w1[e]).then_inc(in_f0, 16)
                    sp.dma_start(w2s[:, e, :, :], w2[e].rearrange("(c f) d -> f c d", c=FC)).then_inc(in_f0, 16)
                elif kind == "max_rows":
                    n, b, g = split_group(step[1])
                    row = 64 * (g // 2) + SHIFT_ROW
                    sp.wait_ge(s_mb_read, step[1] + 1)
                    sp.wait_ge(s_sa_full, 8 * (step[1] + 1))
                    sp.dma_start(Q[n][row:row + 1, b, 4 * g:4 * g + 4, :], nm[:, step[1] % 2, :]).then_inc(s_shift, 16)
                elif step == ("hidden0", 0, 0, 0):
                    sp.wait_ge(s_sb_full, 8 * 8)
                    sp.dma_start(e1w[:, 0:E1, :], eW1.rearrange("e d h -> d e h")).then_inc(in_f1, 16)
                    sp.dma_start(e1w[:, E1, :], sW1).then_inc(in_f1, 16)
                    sp.dma_start(e2w[:, 0:E1, :], eW2.rearrange("e h d -> h e d")).then_inc(in_f1, 16)
                    sp.dma_start(e2w[:, E1, :], sW2).then_inc(in_f1, 16)
                elif kind == "store":
                    b = step[1]
                    sp.wait_ge(s_y1, (b + 1) * (E1 + 1) * R)
                    sp.dma_start(out[b].rearrange("(r p) d -> p r d", p=P), acc[:, b, :, :]).then_inc(s_stored, 16)
            sp.wait_ge(s_stored, 16 * B)

        @block.gpsimd
        def _(pool):
            count = [0]

            def then(ins):
                count[0] += 1
                ins.then_inc(s_p, 1)
                pool.wait_ge(s_p, count[0])

            then(pool.memset(ident[:, :], 0.0))
            pool.affine_select(out=ident[:, :], in_=ident[:, :], compare_op=ALU.not_equal, fill=1.0, base=0,
                               pattern=[[-1, P]], channel_multiplier=1).then_inc(s_ident, 1)
            pool.memset(expo[:, :], -0.5).then_inc(s_vfill, 1)
            pool.memset(expo_half[:, :], 0.5).then_inc(s_vfill, 1)
            pool.wait_ge(s_vfill, 2)
            pool.dma_start(bias3[:, 0:1], bq.rearrange("(p a d) -> a d p", p=8, a=2), allow_slow_non_contiguous=True).then_inc(in_bias0, 16)
            pool.dma_start(bias3[:, 1:2], bk.rearrange("(p a d) -> a d p", p=8, a=2), allow_slow_non_contiguous=True).then_inc(in_bias0, 16)
            pool.dma_start(bias3[:, 2:3], bv.rearrange("(p o) -> p o", o=1)).then_inc(in_bias0, 16)
            pool.dma_start(bo_b[:, :], bo.rearrange("(o d) -> o d", o=1).broadcast_to([P, D])).then_inc(in_bo, 16)

            for step in SCHEDULE:
                kind = step[0]
                if kind == "stats":
                    _, stage, b = step
                    pool.wait_ge(s_stats, nth(*step))
                    then(pool.tensor_scalar(vareps[:, :], mv[:, :, 1], 1.0, LN_EPS, ALU.mult, ALU.add))
                    pool.tensor_tensor(rstd[:, :], vareps[:, :], expo[:, 0:R], ALU.pow).then_inc(s_rstd, 1)
                elif kind == "norm" and step[1] in ("q1", "o1"):
                    pool.wait_ge(s_sq, NORMQ.index(step) + 1)
                    then(pool.tensor_scalar(ms[:, :], sumsq[:, :], 1.0 / D, 1e-6, ALU.mult, ALU.add))
                    pool.tensor_tensor(rms[:, :], ms[:, :], expo[:, 0:R], ALU.pow).then_inc(s_rms, 1)
                elif kind == "kproj" and step == ("kproj", 0, 0):
                    pool.memset(V[0][:, 0].rearrange("p k h c -> p (k h c)"), 1.0).then_inc(s_pfill, 1)
                    pool.memset(fill_view(K[0][:, 1]), TWO_ONES).then_inc(s_pfill, 1)
                    pool.memset(fill_view(Q[0][:, 1]), 0.0).then_inc(s_pfill, 1)
                    pool.memset(V[0][:, 1].rearrange("p k h c -> p (k h c)"), 1.0).then_inc(s_pfill, 1)
                elif kind == "bulk":
                    pool.memset(K[1][:, :, :, :].rearrange("p b g k -> p (b g k)").bitcast(F32), TWO_ONES).then_inc(s_pfill, 1)
                    pool.memset(Q[1][:, :, :, :].rearrange("p b g k -> p (b g k)").bitcast(F32), 0.0).then_inc(s_pfill, 1)
                    pool.memset(V[1][:, :, :, :, :].rearrange("p b k h c -> p (b k h c)"), 1.0).then_inc(s_pfill, 1)
                    pool.wait_ge(in_x[0], 16)
                    pool.wait_ge(in_x[1], 16)
                    pool.wait_ge(in_bo, 16)
                    for b in range(B):
                        for r in range(R):
                            last = pool.tensor_tensor(xres[:, b, r, :], xin[:, b, r, :], bo_b[:, :], ALU.add)
                    last.then_inc(s_xres, 1)
                elif kind == "kproj" and step[1] == 1:
                    _, n, b = step
                    rows = P // (n + 1)
                    pool.wait_ge(*xread(0, *step))
                    if nth(*step) > 1:
                        pn, pb = ((0, 0), (0, 1), (1, 0))[nth(*step) - 2]
                        pool.wait_ge(s_kwr[pn][pb], 48)
                    split(pool, then, kf[0:rows, :], kr[0:rows, :], kp[0:rows, :, :], s_kp)
                elif kind == "ctx_measure":
                    pool.wait_ge(in_ctx[0], 16)
                    pool.wait_ge(in_ctx[1], 16)
                    pool.tensor_tensor(csq[:, :, :], cx[:, :, :], cx[:, :, :], ALU.mult).then_inc(s_csq, 1)
                    pool.wait_ge(s_csq, 2)
                    then(pool.tensor_scalar(cstat[:, 2, :], cstat[:, 0, :], 1.0 / D, 1e-6, ALU.mult, ALU.add))
                    pool.tensor_tensor(cstat[:, 3, :], cstat[:, 2, :], expo[:, :], ALU.pow).then_inc(s_cstat, 1)
                elif kind == "ctx_quant":
                    pool.wait_ge(s_cstat, 2)
                    for k in range(B * KT):
                        last = pool.tensor_scalar(csq[:, k, :], cx[:, k, :], cstat[:, 5, k:k + 1], MAGIC, ALU.mult, ALU.add)
                    then(last)
                    for k in range(B * KT):
                        last = pool.tensor_scalar(csq[:, k, :], csq[:, k, :], -MAGIC, cstat[:, 6, k:k + 1], ALU.add, ALU.mult)
                    last.then_inc(s_cq, 1)
                elif kind == "w1_quant":
                    pool.wait_ge(s_walpha, 1)
                    for n in range(3):
                        last = pool.tensor_scalar(w1t[:, n, :], w1n[:, n, :], winv[:, n:n + 1], MAGIC, ALU.mult, ALU.add)
                    then(last)
                    then(pool.tensor_scalar(w1t[:, :, :], w1t[:, :, :], -MAGIC, 1.0, ALU.add, ALU.mult))
                    then(pool.tensor_scalar(w1t[:, :, :], w1t[:, :, :], 1.0, -1.0, ALU.min, ALU.max))
                    for n in range(3):
                        last = pool.tensor_scalar(w1t[:, n, :], w1t[:, n, :], walpha[:, n:n + 1], 1.0, ALU.mult, ALU.mult)
                    last.then_inc(s_wtern, 1)
                elif kind == "wg_norm":
                    pool.wait_ge(s_wgsq, 1)
                    pool.tensor_tensor(wgs[:, 1:2], wgs[:, 0:1], expo_half[0:E0, 0:1], ALU.pow).then_inc(s_wgnorm, 1)

        @block.scalar
        def _(act):
            for n, w in enumerate((Wk, Wq, Wv, Wo)):
                act.dma_start(w0n[:, n, :], w).then_inc(in_w0, 16)

            for step in SCHEDULE:
                kind = step[0]
                if kind == "ctx_turn":
                    c = step[1]
                    act.wait_ge(x_full[c], X_COUNT[c, step])
                    act.activation(ctxT[:, c * NK:(c + 1) * NK], X[c][:, :], ACT.Copy).then_inc(x_read[c], 1)
                elif kind == "ctxq_turn":
                    c = step[1]
                    act.wait_ge(x_full[c], X_COUNT[c, step])
                    act.wait_ge(*xread(1, "vproj", 0, 1))
                    act.wait_ge(*xread(0, "kproj", 0, 1))
                    act.activation(ctxT[:, c * NK:(c + 1) * NK], X[c][:, :], ACT.Copy).then_inc(x_read[c], 1)
                elif kind == "kproj":
                    _, n, b = step
                    act.wait_ge(x_full[0], X_COUNT[0, step])
                    if n == 0 and b == 0:
                        act.wait_ge(in_bias0, 48)
                    if nth(*step) > 1:
                        act.wait_ge(s_kp, nth(*step) - 1)
                    rows = P // (n + 1)
                    if n == 0:
                        act.activation(kf[:, :], X[0][:, :], ACT.Identity, bias=bias3[:, 1:2]).then_inc(x_read[0], 1)
                    else:
                        act.activation(kf[0:rows, :], X[0][0:rows, :], ACT.Copy).then_inc(x_read[0], 1)
                elif kind == "qproj":
                    _, n, b = step
                    act.wait_ge(x_full[1], X_COUNT[1, step])
                    if nth(*step) > 1:
                        act.wait_ge(s_qp, nth(*step) - 1)
                    if n == 0:
                        act.wait_ge(s_bqs, 1)
                        act.activation(qf[:, :], X[1][:, 0:NQ], ACT.Identity, bias=bqs[:, :], scale=QSCALE).then_inc(x_read[1], 1)
                    else:
                        act.activation(qf[:, :], X[1][:, 0:NQ], ACT.Copy, scale=QSCALE).then_inc(x_read[1], 1)
                elif kind == "vproj":
                    _, n, b = step
                    heads = H // (n + 1)
                    act.wait_ge(x_full[1], X_COUNT[1, step])
                    act.wait_ge(s_pfill, (1, 4)[b] if n == 0 else 7)
                    act.activation(V[n][:, b].rearrange("p k h c -> p (k h) c")[:, :, 0:DH],
                                   X[1][:, 0:KT * heads * DH].rearrange("p (n c) -> p n c", c=DH),
                                   ACT.Copy).then_inc(x_read[1], 1)
                elif kind == "max_rows":
                    g = step[1]
                    act.wait_ge(s_mb_full, g + 1)
                    if g >= 2:
                        act.wait_ge(s_shift, 16 * (g - 1))
                    act.activation(nm[:, g % 2, :], MB[0:4, 0:NQ], ACT.Copy).then_inc(s_mb_read, 1)
                elif kind == "exp":
                    _, g, i = step
                    if i == 0 and g >= 2:
                        act.wait_ge(s_ob_full, g - 1)
                    if i == 0 and g in (8, 9):
                        act.wait_ge(s_y0_full, B * E0 * R)
                    for u in range(2):
                        n = 8 * g + 2 * i + u
                        act.wait_ge(s_sb_full, n + 1)
                        act.activation(prob[:, g % 2, i, 2 * u:2 * u + 2, :].rearrange("p k q -> p (k q)"), SB[u][:, :],
                                       ACT.Exp).then_inc(s_exp, 1)
                elif kind == "values" and step[2] == KT - 1:
                    g = step[1]
                    act.wait_ge(s_ob_full, g + 1)
                    if g % NG == 0 and g:
                        n, b, _ = split_group(g - 1)
                        act.wait_ge(x_full[1], X_COUNT[1, ("out_turn", n, b)])
                    act.activation(oT[:, g % NG, :], OB[:, 0:NQ], ACT.Copy).then_inc(s_ob_read, 1)
                elif kind == "norm" and step[1] in ("q1", "o1"):
                    b = step[2]
                    act.wait_ge(s_norm, nth(*step))
                    for r in range(R):
                        last = act.activation(junk[:, r, :], hn[:, b, r, :], ACT.Square, accum_out=sumsq[:, r:r + 1])
                    last.then_inc(s_sq, 1)
                elif kind == "gate_exp0":
                    b = step[1]
                    act.wait_ge(s_gate, LOGITS0[b])
                    for r in range(R):
                        act.activation(ge0[:, b, r, :], lgk0[:, b, r, :], ACT.Exp, bias=ntop0[:, b, r:r + 1],
                                       accum_out=gsum0[:, b, r:r + 1]).then_inc(s_pick, 1)
                elif kind == "logits1":
                    b = step[1]
                    act.wait_ge(s_gate, LOGITS1[b])
                    for r in range(R):
                        act.activation(ge1[:, r, :], lg1[:, r, 0:E1], ACT.Exp, bias=ntop1[:, r:r + 1],
                                       accum_out=gsum1[:, r:r + 1]).then_inc(s_pick, 1)
                elif kind == "hidden0":
                    _, b, e, q = step
                    if b == 0 and e < 2 and q == 0:
                        act.wait_ge(s_ob_full, 8)
                    if (b, e, q) == (0, 0, 0):
                        act.wait_ge(*xread(0, "bias_turn"))
                    n = b * E0 + e
                    if n >= 2:
                        act.wait_ge(s_y0_full, R * (n - 1))
                    act.wait_ge(s_h0_full, 2 * n + q + 1)
                    for c in range(2 * q, 2 * q + 2):
                        last = act.activation(hid[:, n % 2, c, :], SB[q][:, (c % 2) * NQ:(c % 2 + 1) * NQ], ACT.Gelu,
                                              bias=b1T[:, e * FC + c:e * FC + c + 1])
                    last.then_inc(s_h0, 1)
                elif kind == "hidden1":
                    _, b, e = step
                    n = b * (E1 + 1) + e
                    if n == 0:
                        act.wait_ge(s_ob_full, GQ)
                    if n >= 4:
                        act.wait_ge(s_y1_full, R * (n - 3))
                    act.wait_ge(s_h1_full, n + 1)
                    act.activation(hid1[:, n % 4, :], SB[n % 2][:, 0:NQ], ACT.Relu, bias=e1T[:, e:e + 1]).then_inc(s_h1, 1)

        @block.vector
        def _(dve):
            count = [0]

            def then(ins):
                count[0] += 1
                ins.then_inc(s_v, 1)
                dve.wait_ge(s_v, count[0])

            dve.memset(fill_view(K[0][:, 0]), TWO_ONES).then_inc(s_const, 1)
            dve.memset(ones[:, :], 1.0).then_inc(s_const, 1)
            then(dve.memset(halves[:, :], 0.0))
            for a in range(2):
                last = dve.memset(halves[64 * a:64 * a + 64, 64 * a:64 * a + 64], 1.0)
            last.then_inc(s_const, 1)
            dve.memset(fill_view(Q[0][:, 0]), 0.0).then_inc(s_const, 1)
            dve.wait_ge(s_ident, 1)
            dve.tensor_scalar(negident[:, :], ident[:, :], -1.0, None, ALU.mult).then_inc(s_ident, 1)
            for t in (lg0, lg1, rep0, rep1):
                last = dve.memset(t[:, :, :], LOWEST)
            last.then_inc(s_const, 1)
            dve.memset(cw[:, :, :, E1:E1 + 1], 1.0).then_inc(s_const, 1)

            for step in SCHEDULE:
                kind = step[0]
                if kind == "w0_turn":
                    dve.wait_ge(x_full[1], X_COUNT[1, step])
                    for n in range(2):
                        dve.tensor_copy(wT[0][:, n, :].rearrange("i (a d p) -> i a d p", a=2, d=8),
                                        X[1][:, n * D:(n + 1) * D].rearrange("i (p a d) -> i a d p", p=8, a=2))
                    dve.tensor_copy(wT[0][:, 2:4, :].rearrange("i n o -> i (n o)"), X[1][:, 2 * D:4 * D]).then_inc(x_read[1], 1)
                    dve.wait_ge(in_bias0, 48)
                    dve.tensor_scalar(bqs[:, :], bias3[:, 0:1], QSCALE, None, ALU.mult).then_inc(s_bqs, 1)
                elif kind == "stats":
                    _, stage, b = step
                    src = stage_in[stage]
                    if stage == "q0":
                        dve.wait_ge(in_x[b], 16)
                    elif stage == "q1":
                        dve.wait_ge(s_end0, b + 1)
                    elif stage == "o1":
                        dve.wait_ge(*xread(1, "out_turn", 1, b))
                    else:
                        dve.wait_ge(*xread(1, "out_proj", int(stage == "f1"), b))
                    for r in range(R):
                        last = dve.bn_stats(bst[:, r, :], src[:, b, r, :])
                    then(last)
                    for r in range(R):
                        last = dve.bn_aggr(mv[:, r, :], bst[:, r, :])
                    last.then_inc(s_stats, 1)
                elif kind == "norm":
                    _, stage, b = step
                    src = stage_in[stage]
                    if stage == "o1":
                        dve.wait_ge(in_gb, 48)
                        dve.wait_ge(s_stats, nth("stats", stage, b))
                        for r in range(R):
                            last = dve.tensor_scalar(hn[:, b, r, :], src[:, b, r, :], mv[:, r, 0:1], None, ALU.subtract)
                        then(last)
                    dve.wait_ge(s_rstd, nth("stats", stage, b))
                    if stage == "o1":
                        for r in range(R):
                            last = dve.scalar_tensor_tensor(hn[:, b, r, :], hn[:, b, r, :], rstd[:, r:r + 1], gamma_b[:, :],
                                                            ALU.mult, ALU.mult)
                        then(last)
                    for r in range(R):
                        if stage == "o1":
                            last = dve.tensor_tensor(hn[:, b, r, :], hn[:, b, r, :], beta_b[:, :], ALU.add)
                        else:
                            last = dve.tensor_scalar(hn[:, b, r, :], src[:, b, r, :], mv[:, r, 0:1], rstd[:, r:r + 1],
                                                     ALU.subtract, ALU.mult)
                    last.then_inc(s_norm, 1)
                    if stage in ("q0", "f0", "f1"):
                        continue
                    dve.wait_ge(s_norm, nth(*step))
                    then(dve.tensor_reduce(amax[:, :], hn[:, b, :, :], AX, ALU.max, apply_absolute_value=True))
                elif kind == "quant":
                    _, stage, b = step
                    dve.wait_ge(s_rms, nth(*step))
                    then(dve.tensor_tensor(mxn[:, :], amax[:, :], rms[:, :], ALU.mult))
                    then(dve.tensor_scalar(mxn[:, :], mxn[:, :], 1e-5, None, ALU.max))
                    then(dve.reciprocal(inv[:, :], mxn[:, :]))
                    dve.tensor_scalar(dq[:, :], mxn[:, :], 1.0 / 127.0, None, ALU.mult)
                    then(dve.scalar_tensor_tensor(qs[:, :], inv[:, :], 127.0, rms[:, :], ALU.mult, ALU.mult))
                    for r in range(R):
                        last = dve.tensor_scalar(hn[:, b, r, :], hn[:, b, r, :], qs[:, r:r + 1], MAGIC, ALU.mult, ALU.add)
                    then(last)
                    for r in range(R):
                        last = dve.tensor_scalar(hn[:, b, r, :], hn[:, b, r, :], -MAGIC, dq[:, r:r + 1], ALU.add, ALU.mult)
                    last.then_inc(s_quant, 1)
                elif kind == "turn":
                    _, stage, b = step
                    dve.wait_ge(x_full[0], X_COUNT[0, step])
                    dve.tensor_copy(hT[:, b, :], X[0][:, 0:NQ]).then_inc(x_read[0], 1)
                elif kind == "kproj" and step[1] == 0:
                    _, n, b = step
                    rows = P // (n + 1)
                    dve.wait_ge(*xread(0, *step))
                    if nth(*step) > 1:
                        pn, pb = ((0, 0), (0, 1), (1, 0))[nth(*step) - 2]
                        dve.wait_ge(s_kwr[pn][pb], 48)
                    split(dve, then, kf[0:rows, :], kr[0:rows, :], kp[0:rows, :, :], s_kp)
                elif kind == "qproj":
                    _, n, b = step
                    dve.wait_ge(*xread(1, *step))
                    if nth(*step) > 1:
                        pn, pb = ((0, 0), (0, 1), (1, 0))[nth(*step) - 2]
                        dve.wait_ge(s_qwr[pn][pb], 48)
                    split(dve, then, qf[:, :], qr[:, :], qp[:, :, :], s_qp)
                elif kind == "scores":
                    _, g, i = step
                    for r in range(R):
                        n = 8 * g + 2 * i + r
                        if i == 0 and g >= 2:
                            dve.wait_ge(s_mb_full, g - 1)
                        dve.wait_ge(s_sa_full, n + 1)
                        dve.tensor_reduce(mx[:, g % 2, r, i:i + 1], SA[r][:, :], AX, ALU.max).then_inc(s_sa_max, 1)
                elif kind == "bias_turn":
                    dve.wait_ge(x_full[0], X_COUNT[0, step])
                    dve.tensor_copy(b1T[:, :], X[0][:, 0:E0 * FC])
                    dve.tensor_copy(e1T[:, :], X[0][:, 64:64 + E1 + 1]).then_inc(x_read[0], 1)
                    dve.wait_ge(in_route, 16 * 9)
                    dve.tensor_tensor_reduce(wgsq[:, :], wgn[:, :], wgn[:, :], 1.0, 0.0, ALU.mult, ALU.add,
                                             wgs[:, 0:1]).then_inc(s_wgsq, 1)
                elif kind == "ctx_measure":
                    dve.wait_ge(s_csq, 1)
                    dve.tensor_reduce(cstat[:, 0, :], csq[:, :, :], AX, ALU.add)
                    dve.tensor_reduce(cstat[:, 1, :], cx[:, :, :], AX, ALU.max, apply_absolute_value=True).then_inc(s_csq, 1)
                elif kind == "ctx_quant":
                    dve.wait_ge(s_csq, 2)
                    dve.wait_ge(s_cstat, 1)
                    then(dve.tensor_tensor(cstat[:, 4, :], cstat[:, 1, :], cstat[:, 3, :], ALU.mult))
                    then(dve.tensor_scalar(cstat[:, 4, :], cstat[:, 4, :], 1e-5, None, ALU.max))
                    then(dve.reciprocal(cstat[:, 5, :], cstat[:, 4, :]))
                    then(dve.scalar_tensor_tensor(cstat[:, 5, :], cstat[:, 5, :], 127.0, cstat[:, 3, :], ALU.mult, ALU.mult))
                    dve.tensor_scalar(cstat[:, 6, :], cstat[:, 4, :], 1.0 / 127.0, None, ALU.mult).then_inc(s_cstat, 1)
                elif kind == "wg_norm":
                    dve.wait_ge(s_wgnorm, 1)
                    then(dve.tensor_scalar(wgs[:, 1:2], wgs[:, 1:2], 1e-4, None, ALU.max))
                    then(dve.reciprocal(wgs[:, 2:3], wgs[:, 1:2]))
                    dve.tensor_scalar(wgn[:, :], wgn[:, :], wgs[:, 2:3], None, ALU.mult).then_inc(s_wgn, 1)
                elif kind == "w1_measure":
                    dve.wait_ge(in_w1n, 64)
                    dve.tensor_reduce(wsum[:, :], w1n[:, :, :], AX, ALU.add, apply_absolute_value=True).then_inc(s_wabs, 1)
                    dve.wait_ge(x_full[1], X_COUNT[1, step])
                    for n, size in enumerate((D * D, D * D // 2, D * D)):
                        last = dve.tensor_scalar(walpha[:, n:n + 1], X[1][:, n:n + 1], 1.0 / size, 1e-5, ALU.mult, ALU.max)
                    last.then_inc(x_read[1], 1)
                    dve.wait_ge(*xread(1, *step))
                    dve.reciprocal(winv[:, :], walpha[:, :]).then_inc(s_walpha, 1)
                elif kind == "w1_turn":
                    dve.wait_ge(x_full[1], X_COUNT[1, step])
                    dve.tensor_copy(wT[1][:, 0, 0:64].rearrange("i (a d r) -> i a d r", a=2, d=8),
                                    X[1][:, D:D + 64].rearrange("i (r a d) -> i a d r", r=4, a=2))
                    dve.tensor_copy(wT[1][:, 2, 0:64], X[1][:, D + 64:2 * D])
                    for a in range(2):
                        dve.tensor_copy(wT[1][:, 1, 64 * a:64 * a + 64].rearrange("i (d r g) -> i d r g", d=8, r=4),
                                        X[1][:, 0:D].rearrange("i (r a g d) -> i a d r g", r=4, a=2, g=2)[:, a])
                    dve.tensor_copy(wT[1][:, 3, :], X[1][:, 2 * D:3 * D])
                    dve.tensor_copy(wgT[:, :], X[1][0:GD, 3 * D:3 * D + E0]).then_inc(x_read[1], 1)
                elif kind == "out_turn":
                    _, n, b = step
                    for r in range(R):
                        dve.wait_ge(x_full[r], X_COUNT[r, step])
                        slots = X[r][:, :].rearrange("q (s c) -> q s c", c=32)
                        then(dve.reciprocal(rsum[:, r, :], slots[:, :, DH]))
                        for a in range(2):
                            src = slots[:, 8 * a:8 * a + 8, 0:DH]
                            w = rsum[:, r, 8 * a:8 * a + 8].unsqueeze(2).broadcast_to([P, 8, DH])
                            if n == 0:
                                dst = att[:, b, r, :].rearrange("q (p a d) -> q a p d", p=8, a=2)[:, a]
                            else:
                                src = src.rearrange("q (r g) d -> q r g d", g=2)
                                w = w.rearrange("q (r g) d -> q r g d", g=2)
                                dst = att[:, b, r, :].rearrange("q (r a g d) -> q a r g d", r=4, a=2, g=2)[:, a]
                            last = dve.tensor_tensor(dst, src, w, ALU.mult)
                        if r == 0:
                            last.then_inc(x_read[0], 1)
                        else:
                            last.then_inc(x_read[1], 1)
                elif kind == "att_turn":
                    _, n, b = step
                    dve.wait_ge(x_full[0], X_COUNT[0, step])
                    if n == 0:
                        dve.tensor_scalar(attT[:, b, :], X[0][:, 0:NQ], bias3[:, 2:3], None, ALU.add).then_inc(x_read[0], 1)
                    else:
                        dve.tensor_copy(attT[:, b, :], X[0][:, 0:NQ]).then_inc(x_read[0], 1)
                elif kind == "out_proj":
                    _, n, b = step
                    dve.wait_ge(x_full[1], X_COUNT[1, step])
                    if n == 0:
                        dve.wait_ge(s_xres, 1)
                    dst, res = ((x1, xres), (x3, x2))[n]
                    dve.tensor_tensor(dst[:, b].rearrange("p r d -> p (r d)"), X[1][:, 0:NQ],
                                      res[:, b].rearrange("p r d -> p (r d)"), ALU.add).then_inc(x_read[1], 1)
                elif kind == "red0":
                    b = step[1]
                    dve.wait_ge(x_full[0], X_COUNT[0, step])
                    dve.tensor_copy(redT[:, :], X[0][0:GD, 0:NQ]).then_inc(x_read[0], 1)
                elif kind == "logits0":
                    b = step[1]
                    dve.wait_ge(s_const, 6)
                    dve.wait_ge(x_full[1], X_COUNT[1, step])
                    logits = X[1][:, 0:R * E0].rearrange("p (r e) -> p r e", r=R)
                    dve.tensor_copy(lgk0[:, b, :, :], logits)
                    dve.tensor_copy(lg0[:, :, 0:E0], logits).then_inc(x_read[1], 1)
                    dve.wait_ge(*xread(1, *step))
                    for r in range(R):
                        last = dve.max(top0[:, r, :], lg0[:, r, :])
                    then(last)
                    dve.tensor_scalar(ntop0[:, b, :], top0[:, :, 0], -1.0, None, ALU.mult).then_inc(s_gate, 1)
                    then(dve.tensor_copy(rep0[:, :, 0:1], top0[:, :, 0:1]))
                    for r in range(R):
                        last = dve.match_replace(mr0[:, r, :], rep0[:, r, :], lg0[:, r, :], MARK)
                    then(last)
                    dve.tensor_tensor(oh0[:, b, :, :], mr0[:, :, 0:E0], lg0[:, :, 0:E0], ALU.not_equal).then_inc(s_cw, 1)
                elif kind == "pick0":
                    b = step[1]
                    dve.wait_ge(x_full[0], X_COUNT[0, step])
                    dve.tensor_copy(ohT[:, :], X[0][0:E0, 0:NQ]).then_inc(x_read[0], 1)
                    dve.wait_ge(x_full[1], X_COUNT[1, step])
                    dve.tensor_copy(acc[:, b].rearrange("p r d -> p (r d)"), X[1][:, 0:NQ]).then_inc(x_read[1], 1)
                elif kind == "output0":
                    _, b, e, r = step
                    n = R * (b * E0 + e) + r
                    dve.wait_ge(s_y0_full, n + 1)
                    if e == 0:
                        dve.wait_ge(*xread(1, "pick0", b))
                    else:
                        dve.wait_ge(s_y0, n - 1)
                    dve.scalar_tensor_tensor(acc[:, b, r, :], YB[r][:, 0:D], oh0[:, b, r, e:e + 1], acc[:, b, r, :],
                                             ALU.mult, ALU.add).then_inc(s_y0, 1)
                elif kind == "end0":
                    b = step[1]
                    dve.wait_ge(s_pick, GATE_EXP0[b] + R)
                    dve.wait_ge(s_y0, (b + 1) * E0 * R)
                    then(dve.reciprocal(score0[:, b, :], gsum0[:, b, :]))
                    for r in range(R):
                        last = dve.scalar_tensor_tensor(x2[:, b, r, :], acc[:, b, r, :], score0[:, b, r:r + 1],
                                                        x1[:, b, r, :], ALU.mult, ALU.add)
                    last.then_inc(s_end0, 1)
                elif kind == "logits1":
                    b = step[1]
                    dve.wait_ge(x_full[1], X_COUNT[1, step])
                    dve.tensor_tensor(lg1[:, :, 0:E1], X[1][:, 0:R * E1].rearrange("p (r e) -> p r e", r=R),
                                      rb_b[:, :].unsqueeze(1).broadcast_to([P, R, E1]), ALU.add).then_inc(x_read[1], 1)
                    dve.wait_ge(*xread(1, *step))
                    for r in range(R):
                        last = dve.max(top1[:, r, :], lg1[:, r, :])
                    then(last)
                    dve.tensor_scalar(ntop1[:, :], top1[:, :, 0], -1.0, None, ALU.mult).then_inc(s_gate, 1)
                    then(dve.tensor_copy(rep1[:, :, 0:TOP], top1[:, :, 0:TOP]))
                    for r in range(R):
                        last = dve.match_replace(mr1[:, r, :], rep1[:, r, :], lg1[:, r, :], MARK)
                    then(last)
                    then(dve.tensor_tensor(sel1[:, :, :], mr1[:, :, 0:E1], lg1[:, :, 0:E1], ALU.not_equal))
                elif kind == "pick1":
                    b = step[1]
                    dve.wait_ge(s_pick, EXP1[b])
                    then(dve.reciprocal(rsum1[:, :], gsum1[:, :]))
                    for r in range(R):
                        last = dve.scalar_tensor_tensor(cw[:, b, r, 0:E1], ge1[:, r, :], rsum1[:, r:r + 1], sel1[:, r, :],
                                                        ALU.mult, ALU.mult)
                    last.then_inc(s_cw, 1)
                    dve.wait_ge(x_full[0], X_COUNT[0, step])
                    dve.tensor_copy(cwT[:, :], X[0][0:E1 + 1, 0:NQ]).then_inc(x_read[0], 1)
                    dve.wait_ge(x_full[1], X_COUNT[1, step])
                    dve.tensor_tensor(acc[:, b].rearrange("p r d -> p (r d)"), X[1][:, 0:NQ],
                                      x3[:, b].rearrange("p r d -> p (r d)"), ALU.add).then_inc(x_read[1], 1)
                elif kind == "output1":
                    _, b, e, r = step
                    n = R * (b * (E1 + 1) + e) + r
                    dve.wait_ge(s_y1_full, n - r + R)
                    if e == 0:
                        dve.wait_ge(*xread(1, "pick1", b))
                    else:
                        dve.wait_ge(s_y1, n - 1)
                    dve.scalar_tensor_tensor(acc[:, b, r, :], Y1[n // R % 4][:, r * D:(r + 1) * D], cw[:, b, r, e:e + 1], acc[:, b, r, :],
                                             ALU.mult, ALU.add).then_inc(s_y1, 1)

        @block.tensor
        def _(pe):
            pe.wait_ge(s_ident, 2)
            pe.wait_ge(s_const, 3)

            def fill(bank, step):
                n = X_COUNT[bank, step]
                if n > 1:
                    pe.wait_ge(x_read[bank], n - 1)

            for step in SCHEDULE:
                kind = step[0]
                if kind == "ctx_turn" or kind == "ctxq_turn":
                    c = step[1]
                    src = cx if kind == "ctx_turn" else csq
                    fill(c, step)
                    if kind == "ctx_turn":
                        pe.wait_ge(in_ctx[c], 16)
                    else:
                        pe.wait_ge(s_cq, 1)
                    for k in range(KT):
                        last = pe.transpose(X[c][:, k * P:(k + 1) * P], src[:, c * KT + k, :], ident[:, :])
                    last.then_inc(x_full[c], 1)
                elif kind == "w0_turn":
                    fill(1, step)
                    pe.wait_ge(in_w0, 64)
                    for n in range(4):
                        last = pe.transpose(X[1][:, n * D:(n + 1) * D], w0n[:, n, :], ident[:, :])
                    last.then_inc(x_full[1], 1)
                elif kind == "w1_measure":
                    fill(1, step)
                    pe.wait_ge(s_wabs, 1)
                    for n in range(3):
                        last = pe.matmul(X[1][:, n:n + 1], (halves if n == 1 else ones)[:, :], wsum[:, n:n + 1],
                                         start=True, stop=True)
                    last.then_inc(x_full[1], 1)
                elif kind == "w1_turn":
                    fill(1, step)
                    pe.wait_ge(s_wtern, 1)
                    for n in range(3):
                        pe.transpose(X[1][:, n * D:(n + 1) * D], w1t[:, n, :], ident[:, :])
                    pe.wait_ge(s_wgn, 1)
                    pe.transpose(X[1][0:GD, 3 * D:3 * D + E0], wgn[:, :], ident[0:E0, 0:E0]).then_inc(x_full[1], 1)
                elif kind == "bias_turn":
                    fill(0, step)
                    pe.wait_ge(in_route, 16 * 9)
                    pe.transpose(X[0][:, 0:E0 * FC], b1r[:, :], ident[0:E0 * FC, 0:E0 * FC])
                    pe.transpose(X[0][:, 64:64 + E1 + 1], e1r[:, :], ident[0:E1 + 1, 0:E1 + 1]).then_inc(x_full[0], 1)
                elif kind == "turn":
                    _, stage, b = step
                    fill(0, step)
                    if stage in ("q0", "f0", "f1"):
                        pe.wait_ge(s_norm, nth("norm", stage, b))
                    else:
                        pe.wait_ge(s_quant, nth("quant", stage, b))
                    for r in range(R):
                        last = pe.transpose(X[0][:, r * P:(r + 1) * P], hn[:, b, r, :], ident[:, :])
                    last.then_inc(x_full[0], 1)
                elif kind == "kproj":
                    _, n, b = step
                    fill(0, step)
                    pe.wait_ge(*xread(1, ("w0_turn", "w1_turn")[n]))
                    pe.wait_ge(*xread(b, ("ctx_turn", "ctxq_turn")[n], b))
                    rows = P // (n + 1)
                    pe.matmul(X[0][0:rows, :], wT[n][:, 0, 0:rows], ctxT[:, b * NK:(b + 1) * NK],
                              start=True, stop=True).then_inc(x_full[0], 1)
                elif kind == "vproj":
                    _, n, b = step
                    fill(1, step)
                    pe.wait_ge(*xread(b, ("ctx_turn", "ctxq_turn")[n], b))
                    w = D // (n + 1)
                    for k in range(KT):
                        last = pe.matmul(X[1][:, k * w:(k + 1) * w], ctxT[:, b * NK + k * P:b * NK + (k + 1) * P],
                                         wT[n][:, 2, 0:w], start=True, stop=True)
                    last.then_inc(x_full[1], 1)
                elif kind == "qproj":
                    _, n, b = step
                    fill(1, step)
                    pe.wait_ge(*xread(0, "turn", ("q0", "q1")[n], b))
                    pe.matmul(X[1][:, 0:NQ], wT[n][:, 1, :], hT[:, b, :], start=True, stop=True).then_inc(x_full[1], 1)
                elif kind == "scores":
                    _, gg, i = step
                    n, b, g = split_group(gg)
                    if i == 0 and g == 0:
                        pe.wait_ge(s_kst[n][b], 16 * 2)
                        pe.wait_ge(s_qst[n][b], 16 * 2)
                    s = 4 * g + i
                    for r in range(R):
                        u = 8 * gg + 2 * i + r
                        if u >= 2:
                            pe.wait_ge(s_sa_max, u - 1)
                        pe.matmul(SA[r][:, :], Q[n][:, b, s, r * P:(r + 1) * P], K[n][:, b, key_group(n, s), :],
                                  start=True, stop=True).then_inc(s_sa_full, 1)
                elif kind == "max_rows":
                    g = step[1]
                    pe.wait_ge(s_sa_max, 8 * (g + 1))
                    if g:
                        pe.wait_ge(s_mb_read, g)
                    if g == 8:
                        pe.wait_ge(s_y0, B * E0 * R)
                    for r in range(R):
                        last = pe.matmul(MB[0:4, r * P:(r + 1) * P], mx[:, g % 2, r, :], negident[:, :], start=True, stop=True)
                    last.then_inc(s_mb_full, 1)
                elif kind == "exp":
                    _, gg, i = step
                    n, b, g = split_group(gg)
                    s = 4 * g + i
                    if i == 0:
                        pe.wait_ge(s_shift, 16 * (gg + 1))
                    if gg == 8 and i == 0:
                        pe.wait_ge(s_h0, 2 * B * E0)
                    for u in range(2):
                        m = 8 * gg + 2 * i + u
                        if m >= 2:
                            pe.wait_ge(s_exp, m - 1)
                        for k in range(2):
                            kt = 2 * u + k
                            last = pe.matmul(SB[u][:, k * NQ:(k + 1) * NQ],
                                             K[n][:, b, key_group(n, s), kt * P:(kt + 1) * P], Q[n][:, b, s, :],
                                             start=True, stop=True)
                        last.then_inc(s_sb_full, 1)
                elif kind == "values":
                    _, gg, kt = step
                    n, b, g = split_group(gg)
                    if kt == 0:
                        pe.wait_ge(s_exp, 8 * (gg + 1))
                        pe.wait_ge(*xread(1, "vproj", n, b))
                        if gg:
                            pe.wait_ge(s_ob_read, gg)
                        if gg == 8:
                            pe.wait_ge(s_y0, B * E0 * R)
                    for j in range(4):
                        last = pe.matmul(OB[32 * j:32 * j + 32, 0:NQ], V[n][:, b, kt, value_head(n, 4 * g + j), :],
                                         prob[:, gg % 2, j, kt, :], start=(kt == 0), stop=(kt == KT - 1))
                    if kt == KT - 1:
                        last.then_inc(s_ob_full, 1)
                elif kind == "out_turn":
                    _, n, b = step
                    pe.wait_ge(s_ob_read, 8 * n + NG * (b + 1))
                    for r in range(R):
                        fill(r, step)
                        for g in range(NG):
                            last = pe.transpose(X[r][:, g * P:(g + 1) * P], oT[:, g, r * P:(r + 1) * P], ident[:, :])
                        last.then_inc(x_full[r], 1)
                elif kind == "att_turn":
                    _, n, b = step
                    fill(0, step)
                    if n == 0:
                        pe.wait_ge(*xread(1, "out_turn", n, b))
                    else:
                        pe.wait_ge(s_quant, nth("quant", "o1", b))
                    for r in range(R):
                        last = pe.transpose(X[0][:, r * P:(r + 1) * P], (att, hn)[n][:, b, r, :], ident[:, :])
                    last.then_inc(x_full[0], 1)
                elif kind == "out_proj":
                    _, n, b = step
                    fill(1, step)
                    pe.wait_ge(*xread(0, "att_turn", n, b))
                    for r in range(R):
                        last = pe.matmul(X[1][:, r * D:(r + 1) * D], attT[:, b, r * P:(r + 1) * P], wT[n][:, 3, :],
                                         start=True, stop=True)
                    last.then_inc(x_full[1], 1)
                elif kind == "red0":
                    b = step[1]
                    fill(0, step)
                    pe.wait_ge(*xread(0, "turn", "f0", b))
                    pe.matmul(X[0][0:GD, 0:NQ], wreds[:, :], hT[:, b, :], start=True, stop=True).then_inc(x_full[0], 1)
                elif kind == "logits0":
                    b = step[1]
                    fill(1, step)
                    pe.wait_ge(*xread(0, "red0", b))
                    for r in range(R):
                        last = pe.matmul(X[1][:, r * E0:(r + 1) * E0], redT[:, r * P:(r + 1) * P], wgT[:, :], start=True, stop=True)
                    last.then_inc(x_full[1], 1)
                elif kind == "pick0":
                    b = step[1]
                    fill(0, step)
                    pe.wait_ge(s_cw, CW_AT["logits0", b])
                    for r in range(R):
                        last = pe.transpose(X[0][0:E0, r * P:(r + 1) * P], oh0[:, b, r, :], ident[:, :])
                    last.then_inc(x_full[0], 1)
                    fill(1, step)
                    pe.wait_ge(*xread(0, *step))
                    for r in range(R):
                        last = pe.matmul(X[1][:, r * D:(r + 1) * D], ohT[:, r * P:(r + 1) * P], b2r[:, :], start=True, stop=True)
                    last.then_inc(x_full[1], 1)
                elif kind == "hidden0":
                    _, b, e, q = step
                    n = b * E0 + e
                    if n == 0 and q == 0:
                        pe.wait_ge(s_exp, 64)
                        pe.wait_ge(in_f0, 16 * 2 * E0)
                    if n >= 1:
                        pe.wait_ge(s_h0, 2 * n + q - 1)
                    for c in range(2 * q, 2 * q + 2):
                        last = pe.matmul(SB[q][:, (c % 2) * NQ:(c % 2 + 1) * NQ], w1s[:, e, c * P:(c + 1) * P], hT[:, b, :],
                                         start=True, stop=True)
                    last.then_inc(s_h0_full, 1)
                elif kind == "output0":
                    _, b, e, r = step
                    n = b * E0 + e
                    pe.wait_ge(s_h0, 2 * n + 2)
                    if n == 0 and r == 0:
                        pe.wait_ge(s_ob_read, 8)
                        pe.wait_ge(s_mb_read, 8)
                    if n >= 1:
                        pe.wait_ge(s_y0, R * n + r - 1)
                    for c in range(FC):
                        last = pe.matmul(YB[r][:, 0:D], hid[:, n % 2, c, r * P:(r + 1) * P], w2s[:, e, c, :],
                                         start=(c == 0), stop=(c == FC - 1))
                    last.then_inc(s_y0_full, 1)
                elif kind == "logits1":
                    b = step[1]
                    fill(1, step)
                    pe.wait_ge(*xread(0, "turn", "f1", b))
                    for r in range(R):
                        last = pe.matmul(X[1][:, r * E1:(r + 1) * E1], hT[:, b, r * P:(r + 1) * P], rWs[:, :], start=True, stop=True)
                    last.then_inc(x_full[1], 1)
                elif kind == "pick1":
                    b = step[1]
                    fill(0, step)
                    pe.wait_ge(s_cw, CW_AT["pick1", b])
                    for r in range(R):
                        last = pe.transpose(X[0][0:E1 + 1, r * P:(r + 1) * P], cw[:, b, r, :], ident[:, :])
                    last.then_inc(x_full[0], 1)
                    fill(1, step)
                    pe.wait_ge(*xread(0, *step))
                    for r in range(R):
                        last = pe.matmul(X[1][:, r * D:(r + 1) * D], cwT[:, r * P:(r + 1) * P], e2r[:, :], start=True, stop=True)
                    last.then_inc(x_full[1], 1)
                elif kind == "hidden1":
                    _, b, e = step
                    n = b * (E1 + 1) + e
                    if n == 0:
                        pe.wait_ge(s_exp, 128)
                        pe.wait_ge(in_f1, 64)
                    if n >= 2:
                        pe.wait_ge(s_h1, n - 1)
                    pe.matmul(SB[n % 2][:, 0:NQ], e1w[:, e, :], hT[:, b, :], start=True, stop=True).then_inc(s_h1_full, 1)
                elif kind == "output1":
                    _, b, e, r = step
                    n = b * (E1 + 1) + e
                    pe.wait_ge(s_h1, n + 1)
                    if n == 0 and r == 0:
                        pe.wait_ge(s_ob_read, GQ)
                        pe.wait_ge(s_mb_read, GQ)
                    if n == 2 and r == 0:
                        pe.wait_ge(s_sa_max, 8 * GQ)
                    if n >= 4 and r == 0:
                        pe.wait_ge(s_y1, R * (n - 3))
                    pe.matmul(Y1[n % 4][:, r * D:(r + 1) * D], hid1[:, n % 4, r * P:(r + 1) * P], e2w[:, e, :],
                              start=True, stop=True).then_inc(s_y1_full, 1)


def _counts():
    gate, pick, cws = 0, 0, 0
    logits0, logits1, gexp0, exp1, cw_at = {}, {}, {}, {}, {}
    normq = []
    for s in SCHEDULE:
        if s[0] == "norm":
            if s[1] in ("q1", "o1"):
                normq.append(s)
        if s[0] in ("logits0", "logits1"):
            gate += 1
            (logits0 if s[0] == "logits0" else logits1)[s[1]] = gate
        if s[0] == "gate_exp0":
            gexp0[s[1]] = pick
            pick += R
        if s[0] == "logits1":
            pick += R
            exp1[s[1]] = pick
        if s[0] in ("logits0", "pick1"):
            cws += 1
            cw_at[s[0], s[1]] = cws
    return logits0, logits1, gexp0, exp1, cw_at, normq


LOGITS0, LOGITS1, GATE_EXP0, EXP1, CW_AT, NORMQ = _counts()


_INS = ["x", "ctx_1024", "L0_xattn_Wq", "L0_xattn_bq", "L0_xattn_Wk", "L0_xattn_bk", "L0_xattn_Wv", "L0_xattn_bv",
        "L0_xattn_Wo", "L0_xattn_bo", "L0_ffn_w_red", "L0_ffn_wg", "L0_ffn_w1", "L0_ffn_b1", "L0_ffn_w2", "L0_ffn_b2",
        "L1_xattn_wq", "L1_xattn_wk", "L1_xattn_wv", "L1_xattn_wo", "L1_xattn_ln_gamma", "L1_xattn_ln_beta",
        "L1_ffn_router_W", "L1_ffn_router_b", "L1_ffn_sW1", "L1_ffn_sb1", "L1_ffn_sW2", "L1_ffn_sb2",
        "L1_ffn_eW1", "L1_ffn_eb1", "L1_ffn_eW2", "L1_ffn_eb2"]


def kernel(**inputs):
    import concourse.bacc as _bacc
    from concourse.bass_utils import run_bass_kernel_spmd as _run

    nc = _bacc.Bacc("TRN2", target_bir_lowering=False, num_devices=1)
    arrays, args = {}, []
    for name in _INS:
        a = np.ascontiguousarray(inputs[name])
        arrays[f"in_{name}_dram"] = a
        args.append(nc.dram_tensor(f"in_{name}_dram", a.shape, mybir.dt.from_np(a.dtype), kind="ExternalInput").ap())
    args.append(nc.dram_tensor("out_0_dram", (B, NQ, D), F32, kind="ExternalOutput").ap())
    transformer(nc, *args)
    r = _run(nc, [arrays], core_ids=[0])
    return r.results[0]["out_0_dram"]
```

```python
from contextlib import ExitStack

import numpy as np

import concourse.bass as bass
from concourse import mybir

F32 = mybir.dt.float32
BF16 = mybir.dt.bfloat16
U32 = mybir.dt.uint32
ALU = mybir.AluOpType
ACT = mybir.ActivationFunctionType
AX = mybir.AxisListType.X

P = 128
D = 128
B = 2
R = 2
NQ = R * P
NK = 512
KT = NK // P
H = 16
DH = D // H
NG = H // 4
E0, F0, GD = 8, 512, 16
FC = F0 // P
E1 = 15
TOP = 3
QSCALE = float(1.0 / np.sqrt(DH))
LN_EPS = 1e-5
MAGIC = 1.5 * 2.0 ** 23
TWO_ONES = float(np.array([0x3F803F80], np.uint32).view(np.float32)[0])
LOWEST = -3.0e38
MARK = 3.0e38

K_PART = (0, 1, 2, 0, 1, 0)
Q_PART = (0, 0, 0, 1, 1, 2)
K_RUNS = ((0, 3, 0, True), (3, 2, 0, True), (5, 1, 0, True))
Q_RUNS = ((0, 3, 0, False), (3, 2, 1, False), (5, 1, 2, False))
SHIFT_ROW = 8 * len(K_PART)
K_PARTS = ((2, 1), (1, 1))


def value_head(layer, s):
    a, p = divmod(s, 8)
    return 2 * p + a if layer == 0 else 2 * (p // 2) + a


def key_group(layer, s):
    return s % 8 if layer == 0 else (s % 8) // 2


PROLOGUE = [("kwrite", 0, 0), ("stats", "q0", 0), ("norm", "q0", 0), ("ctx_turn", 0), ("w0_turn", 0),
    ("turn", "q0", 0), ("fills",), ("stats", "q0", 1), ("kproj", 0, 0), ("constants",), ("ctx_turn", 1),
    ("norm", "q0", 1), ("qproj", 0, 0), ("kstack", 0, 0), ("w0_turn", 1), ("kproj", 0, 1), ("kwrite", 0, 1),
    ("ctx_measure",), ("turn", "q0", 1), ("bulk",), ("vproj", 0, 0), ("qstack", 0, 0), ("vproj", 0, 1)]
BETWEEN = [("gate_exp0", 1), ("end0", 1), ("scores", 9, 1), ("max_rows", 8), ("stats", "q1", 1), ("scores", 9, 2)]
ON_SCALAR = [("att_turn", 0, 0), ("att_turn", 1, 0), ("bias0", 0), ("bias0", 1), ("bias1", 0), ("bias1", 1),
    ("red0", 1), ("turn", "f0", 0), ("turn", "f0", 1), ("turn", "f1", 1), ("turn", "q0", 0), ("turn", "q0", 1),
    ("turn", "q1", 0)]
ON_GPSIMD = [("kproj", 1, 0), ("kproj", 1, 1), ("qproj", 0, 0), ("qproj", 1, 0)]
IN_ATTENTION0 = {
    (-2, 0): [("qproj", 0, 1), ("qstack", 0, 1), ("ctx_quant",), ("load_expert", 0)],
    (-2, 2): [("load_w1", 0)],
    (-1, 2): [("kstack", 0, 1)],
    (-1, 3): [("load_small", 0)],
    (0, 0): [("load_w1", 1)],
    (0, 1): [("load_small", 2)],
    (1, 0): [("load_small", 1), ("w1_measure",)],
    (1, 2): [("bias_turn",)],
    (2, 1): [("load_expert", 2), ("ctxq_turn", 0), ("w1_quant",), ("wg_norm",)],
    (2, 2): [("w1_turn",)],
    (2, 3): [("kproj", 1, 0), ("load_expert", 1)],
    (3, 0): [("ctxq_turn", 1)],
    (3, 3): [("vproj", 1, 1), ("load_expert", 3)],
    (4, 0): [("vproj", 1, 0), ("load_expert", 5), ("kwrite", 1, 0)],
    (4, 3): [("kproj", 1, 1), ("load_small", 3)],
    (5, 2): [("load_expert", 6), ("out_turn", 0, 0)],
    (5, 3): [("kstack", 1, 0), ("att_turn", 0, 0), ("kwrite", 1, 1)],
    (6, 0): [("out_proj", 0, 0), ("stats", "f0", 0), ("load_expert", 4)],
    (6, 1): [("load_expert", 7)],
    (6, 3): [("turn", "f0", 0), ("norm", "f0", 0)],
    (7, 0): [("red0", 0)],
    (7, 3): [("gate_exp0", 0), ("logits0", 0)],
}
IN_EXPERTS00 = {
    (-1, 0): [("out_turn", 0, 1)],
    (-1, 1): [("att_turn", 0, 1)],
    (0, 0): [("out_proj", 0, 1), ("stats", "f0", 1), ("norm", "f0", 1)],
    (0, 1): [("bias0", 0)],
    (1, 0): [("turn", "f0", 1)],
    (2, 0): [("red0", 1)],
}
IN_EXPERTS01 = {
    (-1, 0): [("end0", 0), ("stats", "q1", 0)],
    (-1, 1): [("kstack", 1, 1), ("norm", "q1", 0), ("logits0", 1)],
    (0, 0): [("quant", "q1", 0)],
    (1, 0): [("bias0", 1), ("turn", "q1", 0)],
    (1, 1): [("qproj", 1, 0)],
    (4, 1): [("scores", 8, 0)],
    (5, 0): [("scores", 8, 1)],
    (5, 1): [("scores", 8, 2), ("qstack", 1, 0)],
    (6, 0): [("scores", 8, 3)],
    (6, 1): [("scores", 9, 0)],
}
IN_ATTENTION1 = {
    (8, 0): [("norm", "q1", 1)],
    (8, 2): [("quant", "q1", 1)],
    (8, 3): [("turn", "q1", 1)],
    (9, 0): [("qproj", 1, 1)],
    (9, 2): [("qstack", 1, 1)],
    (13, 0): [("out_turn", 1, 0)],
    (13, 1): [("stats", "o1", 0)],
    (13, 2): [("norm", "o1", 0)],
    (14, 0): [("quant", "o1", 0)],
    (14, 2): [("att_turn", 1, 0)],
    (14, 3): [("out_proj", 1, 0)],
    (15, 0): [("stats", "f1", 0)],
    (15, 2): [("norm", "f1", 0), ("turn", "f1", 0)],
    (15, 3): [("logits1", 0)],
    (16, 2): [("pick1", 0)],
}
IN_EXPERTS10 = {
    -1: [("out_turn", 1, 1), ("stats", "o1", 1)],
    0: [("bias1", 0), ("norm", "o1", 1)],
    1: [("quant", "o1", 1)],
    5: [("att_turn", 1, 1)],
    8: [("out_proj", 1, 1), ("stats", "f1", 1)],
    9: [("norm", "f1", 1)],
    12: [("turn", "f1", 1)],
}
IN_EXPERTS11 = {
    -1: [("logits1", 1), ("pick1", 1)],
    5: [("bias1", 1)],
}


LEAD = 7


def build_schedule():
    steps = []

    def attention(layer, first, last, extra):
        g0, g1 = 8 * layer, 8 * layer + 8
        for g in range(first, last):
            for i in range(4):
                if i == 1 and g0 <= g + 1 < g1:
                    steps.append(("max_rows", g + 1))
                ahead = 4 * g + i + LEAD
                if 4 * g0 <= ahead < 4 * g1:
                    steps.append(("scores", ahead // 4, ahead % 4))
                if g0 <= g < g1:
                    steps.append(("exp", g, i))
                if g0 <= g - 1 < g1:
                    steps.append(("values", g - 1, i))
                steps.extend(extra.get((g, i), []))

    def experts0(b, extra):
        for e in range(-1, E0):
            for q in range(2):
                if e + 1 < E0:
                    steps.append(("hidden0", b, e + 1, q))
                if e >= 0:
                    steps.append(("output0", b, e, q))
                steps.extend(extra.get((e, q), []))

    def experts1(b, extra):
        for e in range(-2, E1 + 1):
            if e + 2 <= E1:
                steps.append(("hidden1", b, e + 2))
            if e >= 0:
                steps.append(("output1", b, e, 0))
                steps.append(("output1", b, e, 1))
            steps.extend(extra.get(e, []))
        steps.append(("store", b))

    steps.extend(PROLOGUE)
    attention(0, -2, 9, IN_ATTENTION0)
    experts0(0, IN_EXPERTS00)
    experts0(1, IN_EXPERTS01)
    steps.extend(BETWEEN)
    attention(1, 8, 17, IN_ATTENTION1)
    experts1(0, IN_EXPERTS10)
    experts1(1, IN_EXPERTS11)
    return steps


SCHEDULE = build_schedule()

X_FILLS = {
    "ctx_turn": lambda s: [s[1]], "ctxq_turn": lambda s: [s[1]],
    "w0_turn": lambda s: [1], "kproj": lambda s: [0], "vproj": lambda s: [1], "turn": lambda s: [0],
    "qproj": lambda s: [1], "bias_turn": lambda s: [0], "w1_measure": lambda s: [1],
    "w1_turn": lambda s: [1], "out_turn": lambda s: [0, 1], "att_turn": lambda s: [0],
    "out_proj": lambda s: [1], "red0": lambda s: [0], "logits0": lambda s: [1],
    "max_rows": lambda s: [0], "bias0": lambda s: [0, 1], "logits1": lambda s: [1], "bias1": lambda s: [0, 1],
}
X_COUNT = {}
_seen = [0, 0]
for _s in SCHEDULE:
    for _x in X_FILLS.get(_s[0], lambda s: [])(_s):
        _seen[_x] += 1
        X_COUNT[_x, _s] = _seen[_x]

_last_output = SCHEDULE.index(("output0", B - 1, E0 - 1, 1))
LENT_UNTIL = 64 + 2 * sum(s[0] == "scores" and s[1] >= 8 for s in SCHEDULE[:_last_output])
SCORE_BANK, SCORE_BEFORE, _turn = [], [], {0: -1, 1: -1, 2: -1}
for _u in range(128):
    _banks = [0, 1] if 64 <= _u < LENT_UNTIL else [2, 0, 1] if _u == LENT_UNTIL else [0, 1, 2]
    _bank = _banks[0] if _u == LENT_UNTIL else min(_banks, key=_turn.get)
    SCORE_BANK.append(_bank)
    SCORE_BEFORE.append(_turn[_bank])
    _turn[_bank] = _u

OUTPUTS_BEFORE = {("bias%d" % n, b): sum(s[0] == "output%d" % n for s in SCHEDULE[:SCHEDULE.index(("bias%d" % n, b))])
                  for n in range(2) for b in range(B)}

ORDER = {}
for _s in SCHEDULE:
    ORDER.setdefault(_s[0], []).append(_s)


def nth(*step):
    return ORDER[step[0]].index(step) + 1


def transformer(nc, x, ctx, Wq, bq, Wk, bk, Wv, bv, Wo, bo, w_red, wg, w1, b1, w2, b2, wq1, wk1, wv1, wo1,
                gamma, beta, rW, rb, sW1, sb1, sW2, sb2, eW1, eb1, eW2, eb2, out):
    with ExitStack() as stack:
        def sb(name, shape, dt=F32):
            return stack.enter_context(nc.sbuf_tensor(name, shape, dt))

        def sem(name):
            return stack.enter_context(nc.semaphore(name))

        stack.enter_context(nc.allow_low_precision(reason="exact splits into bfloat16 parts; the shift of a softmax cancels"))

        ident = sb("ident", [P, P])
        negident = sb("negident", [P, P], BF16)
        ones = sb("ones", [P, P])
        halves = sb("halves", [P, P])
        expo = sb("expo", [P, 8])
        expo_half = sb("expo_half", [P, 8])
        xin = sb("xin", [P, B, R, D])
        xres = sb("xres", [P, B, R, D])
        bo_b = sb("bo_b", [P, D])
        gamma_b = sb("gamma_b", [P, D])
        beta_b = sb("beta_b", [P, D])
        rb_b = sb("rb_b", [P, E1])
        x1 = xres
        x2 = sb("x2", [P, B, R, D])
        x3 = xin
        hn = sb("hn", [P, B, R, D])
        hT = sb("hT", [P, B, NQ])
        att = sb("att", [P, B, R, D])
        attT = sb("attT", [P, B, NQ])
        acc = sb("acc", [P, B, R, D])
        bst = sb("bst", [P, R, 6])
        mv = sb("mv", [P, R, 2])
        vareps = sb("vareps", [P, R])
        rstd = sb("rstd", [P, R])
        sumsq = sb("sumsq", [P, R])
        amax = sb("amax", [P, R])
        ms = sb("ms", [P, R])
        rms = sb("rms", [P, R])
        mxn = sb("mxn", [P, R])
        inv = sb("inv", [P, R])
        qs = sb("qs", [P, R])
        dq = sb("dq", [P, R])
        junk = sb("junk", [P, R, D])
        cx = sb("cx", [P, B * KT, D])
        ctxT = sb("ctxT", [P, B * NK])
        csq = sb("csq", [P, B * KT, D])
        cstat = sb("cstat", [P, 7, B * KT])
        w0n = sb("w0n", [P, 4, D])
        wT = [sb(f"wT{n}", [P, 4, D]) for n in range(2)]
        w1n = sb("w1n", [P, 3, D])
        w1t = w1n
        wsum = sb("wsum", [P, 3])
        walpha = sb("walpha", [P, 3])
        winv = sb("winv", [P, 3])
        bias3 = sb("bias3", [P, 3])
        bqs = sb("bqs", [P, 1])
        kf = sb("kf", [P, NK])
        kr = sb("kr", [P, NK])
        kp = sb("kp", [P, 3, NK], BF16)
        qf = sb("qf", [P, NQ])
        qr = sb("qr", [P, NQ])
        qp = sb("qp", [P, 3, NQ], BF16)
        K = [sb("K0", [P, B, 8, NK], BF16), sb("K1", [P, B, 4, NK], BF16)]
        Q = [sb(f"Q{n}", [P, B, H, NQ], BF16) for n in range(2)]
        V = [sb("V0", [P, B, KT, H, 32]), sb("V1", [P, B, KT, 8, 32])]
        prob = sb("prob", [P, 2, 4, KT, NQ])
        mx = sb("mx", [P, 2, R, 4], BF16)
        nm = sb("nm", [4, 2, NQ], BF16)
        oT = sb("oT", [P, NG, NQ])
        rsum = sb("rsum", [P, R, H])
        hid = prob[:, :, 0, :, :]
        hid1 = prob[:, 0, 0, :, :]
        w1s = sb("w1s", [P, E0, F0])
        w2s = sb("w2s", [P, E0, FC, D])
        b1r = sb("b1r", [E0 * FC, P])
        b1T = sb("b1T", [P, E0 * FC])
        b2r = sb("b2r", [E0, D])
        wreds = sb("wreds", [P, GD])
        wgn = sb("wgn", [E0, GD])
        wgsq = sb("wgsq", [E0, GD])
        wgs = sb("wgs", [E0, 3])
        wgT = sb("wgT", [GD, E0])
        redT = sb("redT", [GD, NQ])
        lg0 = sb("lg0", [P, R, E0 + 7])
        rep0 = sb("rep0", [P, R, 8])
        mr0 = sb("mr0", [P, R, E0 + 7])
        top0 = sb("top0", [P, R, 8])
        oh0 = sb("oh0", [P, B, R, E0])
        ntop0 = sb("ntop0", [P, B, R])
        lgk0 = sb("lgk0", [P, B, R, E0])
        ge0 = sb("ge0", [P, B, R, E0])
        gsum0 = sb("gsum0", [P, B, R])
        score0 = sb("score0", [P, B, R])
        ohT = sb("ohT", [E0, NQ])
        place = K[0][:, :, :, :].rearrange("p b g k -> p (b g k)").bitcast(F32)
        e1w, e2w = (place[:, n * (E1 + 1) * D:(n + 1) * (E1 + 1) * D].rearrange("p (e d) -> p e d", d=D) for n in range(2))
        e1r = sb("e1r", [E1 + 1, D])
        e1T = sb("e1T", [P, E1 + 1])
        e2r = sb("e2r", [E1 + 1, D])
        rWs = sb("rWs", [P, E1])
        lg1 = sb("lg1", [P, R, E1 + 5])
        rep1 = sb("rep1", [P, R, 8])
        mr1 = sb("mr1", [P, R, E1 + 5])
        top1 = sb("top1", [P, R, 8])
        sel1 = sb("sel1", [P, R, E1])
        ntop1 = sb("ntop1", [P, R])
        ge1 = sb("ge1", [P, R, E1])
        gsum1 = sb("gsum1", [P, R])
        rsum1 = sb("rsum1", [P, R])
        cw = sb("cw", [P, B, R, E1 + 1])
        cwT = sb("cwT", [E1 + 1, NQ])

        k_dram = [[nc.dram_tensor(f"k_dram{n}{b}", [6, 2, 64 // (n + 1), NK], BF16, kind="Internal").ap() for b in range(B)]
                  for n in range(2)]
        q_dram = [[nc.dram_tensor(f"q_dram{n}{b}", [6, 2, 64, NQ], BF16, kind="Internal").ap() for b in range(B)]
                  for n in range(2)]

        SA = [stack.enter_context(nc.psum_tensor(f"SA{n}", [P, 512], F32)) for n in range(3)]
        SB = [stack.enter_context(nc.psum_tensor(f"SB{n}", [P, 512], F32)) for n in range(2)]
        OB = stack.enter_context(nc.psum_tensor("OB", [P, 512], F32))
        X = [stack.enter_context(nc.psum_tensor(f"X{n}", [P, 512], F32)) for n in range(2)]
        YB = [OB, SA[2]]
        Y1 = [OB, SA[2], SA[0], SA[1]]

        in_x, in_ctx, in_w0, in_bias0 = [sem("in_x0"), sem("in_x1")], [sem("in_ctx0"), sem("in_ctx1")], [sem("in_w0_kq"), sem("in_w0_vo")], sem("in_bias0")
        in_bv, in_bo, in_gb, in_w1n = sem("in_bv"), sem("in_bo"), sem("in_gb"), sem("in_w1n")
        in_route, in_f0, in_f1 = sem("in_route"), sem("in_f0"), sem("in_f1")
        s_ident, s_const, s_pfill, s_vfill = sem("s_ident"), sem("s_const"), sem("s_pfill"), sem("s_vfill")
        x_full = [sem("x0_full"), sem("x1_full")]
        x_read = [sem("x0_read"), sem("x1_read")]
        s_sa_full, s_sa_max = sem("s_sa_full"), sem("s_sa_max")
        s_shift = sem("s_shift")
        s_sb_full, s_exp = sem("s_sb_full"), sem("s_exp")
        s_ob_full, s_ob_read = sem("s_ob_full"), sem("s_ob_read")
        s_kp, s_qp = sem("s_kp"), sem("s_qp")
        s_kwr = [[sem(f"s_kwr{n}{b}") for b in range(B)] for n in range(2)]
        s_qwr = [[sem(f"s_qwr{n}{b}") for b in range(B)] for n in range(2)]
        s_kst = [[[sem(f"s_kst{n}{b}{part}") for part in range(K_PARTS[n][b])] for b in range(B)] for n in range(2)]
        s_qst = [[[sem(f"s_qst{n}{b}{a}") for a in range(2)] for b in range(B)] for n in range(2)]
        s_stats, s_rstd, s_norm, s_sq, s_rms, s_quant = (sem("s_stats"), sem("s_rstd"), sem("s_norm"), sem("s_sq"),
                                                         sem("s_rms"), sem("s_quant"))
        s_xres, s_bqs = sem("s_xres"), sem("s_bqs")
        s_csq, s_cstat, s_cq = sem("s_csq"), sem("s_cstat"), sem("s_cq")
        s_wabs, s_walpha, s_wtern = sem("s_wabs"), sem("s_walpha"), sem("s_wtern")
        s_wgsq, s_wgnorm, s_wgn = sem("s_wgsq"), sem("s_wgnorm"), sem("s_wgn")
        s_pick, s_gate, s_cw = sem("s_pick"), sem("s_gate"), sem("s_cw")
        s_h0_full, s_h0, s_y0_full, s_y0 = sem("s_h0_full"), sem("s_h0"), sem("s_y0_full"), sem("s_y0")
        s_h1_full, s_h1, s_y1_full, s_y1 = sem("s_h1_full"), sem("s_h1"), sem("s_y1_full"), sem("s_y1")
        s_end0 = sem("s_end0")
        s_stored = sem("s_stored")
        s_v, s_p = sem("s_v"), sem("s_p")

        GQ = 8 * 2
        stage_in = {"q0": xin, "f0": x1, "q1": x2, "o1": att, "f1": x3}

        def fill_view(t):
            return t.rearrange("p g k -> p (g k)").bitcast(F32)

        def xread(bank, *step):
            return x_read[bank], X_COUNT[bank, step]

        def split_group(g):
            return g // 8, g % 8 // NG, g % NG

        def split(engine, then, full, rest, parts, done):
            then(engine.tensor_copy(parts[:, 0, :], full))
            then(engine.tensor_tensor(rest, full, parts[:, 0, :], ALU.subtract))
            then(engine.tensor_copy(parts[:, 1, :], rest))
            engine.tensor_tensor(parts[:, 2, :], rest, parts[:, 1, :], ALU.subtract).then_inc(done, 1)

        def split_step(engine, then, step):
            kind, n, b = step
            rows = P // (n + 1)
            before = nth(*step) - 1
            if kind == "kproj":
                engine.wait_ge(*xread(0, *step))
                if before:
                    engine.wait_ge(s_kp, before)
                    engine.wait_ge(s_kwr[ORDER[kind][before - 1][1]][ORDER[kind][before - 1][2]], 16 * len(K_RUNS))
                split(engine, then, kf[0:rows, :], kr[0:rows, :], kp[0:rows, :, :], s_kp)
            else:
                engine.wait_ge(*xread(1, *step))
                if before:
                    engine.wait_ge(s_qp, before)
                    engine.wait_ge(s_qwr[ORDER[kind][before - 1][1]][ORDER[kind][before - 1][2]], 16 * len(Q_RUNS))
                split(engine, then, qf[:, :], qr[:, :], qp[:, :, :], s_qp)

        block = stack.enter_context(nc.Block())

        @block.sync
        def _(sp):
            sp.dma_start(xin[:, 0, :, :], x[0].rearrange("(r p) d -> p r d", p=P)).then_inc(in_x[0], 16)
            for b in range(B):
                sp.dma_start(cx[:, b * KT:(b + 1) * KT, :], ctx[b].rearrange("(k p) d -> p k d", p=P)).then_inc(in_ctx[b], 16)
                if b == 0:
                    sp.dma_start(xin[:, 1, :, :], x[1].rearrange("(r p) d -> p r d", p=P)).then_inc(in_x[1], 16)

            for n, w in enumerate((Wv, Wo)):
                sp.dma_start(w0n[:, 2 + n, :], w).then_inc(in_w0[1], 16)
            sp.dma_start(bias3[:, 2:3], bv.rearrange("(p o) -> p o", o=1)).then_inc(in_bv, 16)

            def write_blocks(parts, runs, dram, written):
                rows, _, cols = parts.shape
                for j, m, part, rising in runs:
                    src = parts[:, part:part + m, :] if rising else parts[:, part:part + 1, :].broadcast_to([rows, m, cols])
                    sp.dma_start(dram[j:j + m].rearrange("m a r c -> (a r) m c"), src).then_inc(written, 16)

            def read_stack(dst, dram, half, slots, done):
                cols = slice(slots.start * dram.shape[3], slots.stop * dram.shape[3])
                sp.dma_start(dst[64 * half:64 * half + SHIFT_ROW, slots].rearrange("r s c -> r (s c)"),
                             dram[:, half].rearrange("j (d s) c -> j d (s c)", d=DH)[:, :, cols]).then_inc(done, 16)

            def read_keys(n, b, part):
                parts, groups = K_PARTS[n][b], 8 // (n + 1)
                slots = slice(part * groups // parts, (part + 1) * groups // parts)
                for a in range(2):
                    read_stack(K[n][:, b, :, :], k_dram[n][b], a, slots, s_kst[n][b][part])

            for step in SCHEDULE:
                kind = step[0]
                if kind == "kwrite":
                    _, n, b = step
                    sp.wait_ge(s_kp, nth("kproj", n, b))
                    write_blocks(kp[0:P // (n + 1), :, :], K_RUNS, k_dram[n][b], s_kwr[n][b])
                elif kind == "qproj":
                    _, n, b = step
                    sp.wait_ge(s_qp, nth(*step))
                    write_blocks(qp[:, :, :], Q_RUNS, q_dram[n][b], s_qwr[n][b])
                elif kind == "kstack":
                    _, n, b = step
                    sp.wait_ge(s_kwr[n][b], 16 * len(K_RUNS))
                    if (n, b) == (0, 0):
                        sp.wait_ge(s_const, 1)
                    else:
                        sp.wait_ge(s_pfill, 3 if n == 0 else 6)
                    read_keys(n, b, 0)
                elif kind == "qstack":
                    _, n, b = step
                    sp.wait_ge(s_qwr[n][b], 16 * len(Q_RUNS))
                    sp.wait_ge(s_pfill, (1, 4)[b] if n == 0 else 7)
                    for a in range(2):
                        read_stack(Q[n][:, b, 8 * a:8 * a + 8, :], q_dram[n][b], a, slice(0, 8), s_qst[n][b][a])
                        if a == 0 and K_PARTS[n][b] == 2:
                            read_keys(n, b, 1)
                elif step == ("load_w1", 0):
                    sp.dma_start(w1n[:, 0, :], wq1).then_inc(in_w1n, 16)
                    sp.dma_start(w1n[0:64, 1, :], wk1).then_inc(in_w1n, 16)
                elif step == ("load_w1", 1):
                    sp.dma_start(w1n[64:128, 1, :], wv1).then_inc(in_w1n, 16)
                    sp.dma_start(w1n[:, 2, :], wo1).then_inc(in_w1n, 16)
                elif step == ("load_small", 0):
                    sp.dma_start(b1r[:, :], b1.rearrange("e (c f) -> (e c) f", c=FC)).then_inc(in_route, 16)
                    sp.dma_start(b2r[:, :], b2).then_inc(in_route, 16)
                    sp.dma_start(wgn[:, :], wg).then_inc(in_route, 16)
                elif step == ("load_small", 1):
                    sp.dma_start(wreds[:, :], w_red).then_inc(in_route, 16)
                    sp.dma_start(e1r[0:E1, :], eb1).then_inc(in_route, 16)
                    sp.dma_start(e1r[E1:E1 + 1, :], sb1.rearrange("(o d) -> o d", o=1)).then_inc(in_route, 16)
                elif step == ("load_small", 2):
                    sp.dma_start(e2r[0:E1, :], eb2).then_inc(in_route, 16)
                    sp.dma_start(e2r[E1:E1 + 1, :], sb2.rearrange("(o d) -> o d", o=1)).then_inc(in_route, 16)
                    sp.dma_start(rWs[:, :], rW).then_inc(in_route, 16)
                elif step == ("load_small", 3):
                    sp.dma_start(gamma_b[:, :], gamma.rearrange("(o d) -> o d", o=1).broadcast_to([P, D])).then_inc(in_gb, 16)
                    sp.dma_start(beta_b[:, :], beta.rearrange("(o d) -> o d", o=1).broadcast_to([P, D])).then_inc(in_gb, 16)
                    sp.dma_start(rb_b[:, :], rb.rearrange("(o d) -> o d", o=1).broadcast_to([P, E1])).then_inc(in_gb, 16)
                elif kind == "load_expert":
                    e = step[1]
                    sp.dma_start(w1s[:, e, :], w1[e]).then_inc(in_f0, 16)
                    sp.dma_start(w2s[:, e, :, :], w2[e].rearrange("(c f) d -> f c d", c=FC)).then_inc(in_f0, 16)
                elif kind == "max_rows":
                    n, b, g = split_group(step[1])
                    row = 64 * (g // 2) + SHIFT_ROW
                    sp.wait_ge(*xread(0, *step))
                    sp.wait_ge(s_sa_full, 8 * (step[1] + 1))
                    sp.dma_start(Q[n][row:row + 1, b, 4 * g:4 * g + 4, :], nm[:, step[1] % 2, :]).then_inc(s_shift, 16)
                elif step == ("hidden0", 0, 0, 0):
                    sp.wait_ge(s_sb_full, 8 * 8)
                    sp.dma_start(e1w[:, 0:E1, :], eW1.rearrange("e d h -> d e h")).then_inc(in_f1, 16)
                    sp.dma_start(e1w[:, E1, :], sW1).then_inc(in_f1, 16)
                    sp.dma_start(e2w[:, 0:E1, :], eW2.rearrange("e h d -> h e d")).then_inc(in_f1, 16)
                    sp.dma_start(e2w[:, E1, :], sW2).then_inc(in_f1, 16)
                elif kind == "store":
                    b = step[1]
                    sp.wait_ge(s_y1, (b + 1) * (E1 + 1) * R)
                    sp.dma_start(out[b].rearrange("(r p) d -> p r d", p=P), acc[:, b, :, :]).then_inc(s_stored, 16)
            sp.wait_ge(s_stored, 16 * B)

        @block.gpsimd
        def _(pool):
            count = [0]

            def then(ins):
                count[0] += 1
                ins.then_inc(s_p, 1)
                pool.wait_ge(s_p, count[0])

            then(pool.memset(ident[:, :], 0.0))
            pool.affine_select(out=ident[:, :], in_=ident[:, :], compare_op=ALU.not_equal, fill=1.0, base=0,
                               pattern=[[-1, P]], channel_multiplier=1).then_inc(s_ident, 1)
            pool.memset(expo[:, :], -0.5).then_inc(s_vfill, 1)
            pool.memset(expo_half[:, :], 0.5).then_inc(s_vfill, 1)
            pool.wait_ge(s_vfill, 2)
            pool.memset(fill_view(Q[0][:, 0]), 0.0).then_inc(s_pfill, 1)
            pool.dma_start(bo_b[:, :], bo.rearrange("(o d) -> o d", o=1).broadcast_to([P, D])).then_inc(in_bo, 16)

            for step in SCHEDULE:
                kind = step[0]
                if kind == "stats":
                    _, stage, b = step
                    pool.wait_ge(s_stats, nth(*step))
                    then(pool.tensor_scalar(vareps[:, :], mv[:, :, 1], 1.0, LN_EPS, ALU.mult, ALU.add))
                    pool.tensor_tensor(rstd[:, :], vareps[:, :], expo[:, 0:R], ALU.pow).then_inc(s_rstd, 1)
                elif kind == "norm" and step[1] in ("q1", "o1"):
                    pool.wait_ge(s_sq, NORMQ.index(step) + 1)
                    then(pool.tensor_scalar(ms[:, :], sumsq[:, :], 1.0 / D, 1e-6, ALU.mult, ALU.add))
                    pool.tensor_tensor(rms[:, :], ms[:, :], expo[:, 0:R], ALU.pow).then_inc(s_rms, 1)
                elif kind == "fills":
                    pool.memset(V[0][:, 0].rearrange("p k h c -> p (k h c)"), 1.0).then_inc(s_pfill, 1)
                    pool.memset(fill_view(K[0][:, 1]), TWO_ONES).then_inc(s_pfill, 1)
                    pool.memset(fill_view(Q[0][:, 1]), 0.0).then_inc(s_pfill, 1)
                    pool.memset(V[0][:, 1].rearrange("p k h c -> p (k h c)"), 1.0).then_inc(s_pfill, 1)
                elif kind == "bulk":
                    pool.memset(K[1][:, :, :, :].rearrange("p b g k -> p (b g k)").bitcast(F32), TWO_ONES).then_inc(s_pfill, 1)
                    pool.memset(Q[1][:, :, :, :].rearrange("p b g k -> p (b g k)").bitcast(F32), 0.0).then_inc(s_pfill, 1)
                    pool.memset(V[1][:, :, :, :, :].rearrange("p b k h c -> p (b k h c)"), 1.0).then_inc(s_pfill, 1)
                    pool.wait_ge(in_x[0], 16)
                    pool.wait_ge(in_x[1], 16)
                    pool.wait_ge(in_bo, 16)
                    for b in range(B):
                        for r in range(R):
                            last = pool.tensor_tensor(xres[:, b, r, :], xin[:, b, r, :], bo_b[:, :], ALU.add)
                    last.then_inc(s_xres, 1)
                elif step in ON_GPSIMD:
                    split_step(pool, then, step)
                elif kind == "ctx_measure":
                    pool.wait_ge(s_csq, 2)
                    then(pool.tensor_scalar(cstat[:, 2, :], cstat[:, 0, :], 1.0 / D, 1e-6, ALU.mult, ALU.add))
                    pool.tensor_tensor(cstat[:, 3, :], cstat[:, 2, :], expo[:, :], ALU.pow).then_inc(s_cstat, 1)
                elif kind == "ctx_quant":
                    pool.wait_ge(s_cstat, 2)
                    for k in range(B * KT):
                        last = pool.tensor_scalar(csq[:, k, :], cx[:, k, :], cstat[:, 5, k:k + 1], MAGIC, ALU.mult, ALU.add)
                    then(last)
                    for k in range(B * KT):
                        last = pool.tensor_scalar(csq[:, k, :], csq[:, k, :], -MAGIC, cstat[:, 6, k:k + 1], ALU.add, ALU.mult)
                    last.then_inc(s_cq, 1)
                elif kind == "w1_quant":
                    pool.wait_ge(s_walpha, 1)
                    for n in range(3):
                        last = pool.tensor_scalar(w1t[:, n, :], w1n[:, n, :], winv[:, n:n + 1], MAGIC, ALU.mult, ALU.add)
                    then(last)
                    then(pool.tensor_scalar(w1t[:, :, :], w1t[:, :, :], -MAGIC, 1.0, ALU.add, ALU.mult))
                    then(pool.tensor_scalar(w1t[:, :, :], w1t[:, :, :], 1.0, -1.0, ALU.min, ALU.max))
                    for n in range(3):
                        last = pool.tensor_scalar(w1t[:, n, :], w1t[:, n, :], walpha[:, n:n + 1], 1.0, ALU.mult, ALU.mult)
                    last.then_inc(s_wtern, 1)
                elif kind == "wg_norm":
                    pool.wait_ge(s_wgsq, 1)
                    pool.tensor_tensor(wgs[:, 1:2], wgs[:, 0:1], expo_half[0:E0, 0:1], ALU.pow).then_inc(s_wgnorm, 1)

        @block.scalar
        def _(act):
            for n, w in enumerate((Wk, Wq)):
                act.dma_start(w0n[:, n, :], w).then_inc(in_w0[0], 16)
            for n, bias in enumerate((bq, bk)):
                act.dma_start(bias3[:, n:n + 1], bias.rearrange("(p a d) -> a d p", p=8, a=2),
                              allow_slow_non_contiguous=True).then_inc(in_bias0, 16)

            for step in SCHEDULE:
                kind = step[0]
                if kind == "ctx_turn":
                    c = step[1]
                    act.wait_ge(x_full[c], X_COUNT[c, step])
                    act.activation(ctxT[:, c * NK:(c + 1) * NK], X[c][:, :], ACT.Copy).then_inc(x_read[c], 1)
                elif kind == "ctxq_turn":
                    c = step[1]
                    act.wait_ge(x_full[c], X_COUNT[c, step])
                    act.wait_ge(*xread(1, "vproj", 0, 1))
                    act.wait_ge(*xread(0, "kproj", 0, 1))
                    act.activation(ctxT[:, c * NK:(c + 1) * NK], X[c][:, :], ACT.Copy).then_inc(x_read[c], 1)
                elif kind == "kproj":
                    _, n, b = step
                    act.wait_ge(x_full[0], X_COUNT[0, step])
                    if n == 0 and b == 0:
                        act.wait_ge(in_bias0, 32)
                    if nth(*step) > 1:
                        act.wait_ge(s_kp, nth(*step) - 1)
                    rows = P // (n + 1)
                    if n == 0:
                        act.activation(kf[:, :], X[0][:, :], ACT.Identity, bias=bias3[:, 1:2]).then_inc(x_read[0], 1)
                    else:
                        act.activation(kf[0:rows, :], X[0][0:rows, :], ACT.Copy).then_inc(x_read[0], 1)
                elif kind == "qproj":
                    _, n, b = step
                    act.wait_ge(x_full[1], X_COUNT[1, step])
                    if nth(*step) > 1:
                        act.wait_ge(s_qp, nth(*step) - 1)
                    if n == 0:
                        act.wait_ge(s_bqs, 1)
                        act.activation(qf[:, :], X[1][:, 0:NQ], ACT.Identity, bias=bqs[:, :], scale=QSCALE).then_inc(x_read[1], 1)
                    else:
                        act.activation(qf[:, :], X[1][:, 0:NQ], ACT.Copy, scale=QSCALE).then_inc(x_read[1], 1)
                elif kind == "vproj":
                    _, n, b = step
                    heads = H // (n + 1)
                    act.wait_ge(x_full[1], X_COUNT[1, step])
                    act.wait_ge(s_pfill, (2, 5)[b] if n == 0 else 8)
                    act.activation(V[n][:, b].rearrange("p k h c -> p (k h) c")[:, :, 0:DH],
                                   X[1][:, 0:KT * heads * DH].rearrange("p (n c) -> p n c", c=DH),
                                   ACT.Copy).then_inc(x_read[1], 1)
                elif kind == "max_rows":
                    g = step[1]
                    act.wait_ge(x_full[0], X_COUNT[0, step])
                    if g >= 2:
                        act.wait_ge(s_shift, 16 * (g - 1))
                    act.activation(nm[:, g % 2, :], X[0][0:4, 0:NQ], ACT.Copy).then_inc(x_read[0], 1)
                elif kind == "exp":
                    _, g, i = step
                    if i == 0 and g >= 2:
                        act.wait_ge(s_ob_full, g - 1)
                    if i == 0 and g in (8, 9):
                        act.wait_ge(s_y0_full, B * E0 * R)
                    for u in range(2):
                        n = 8 * g + 2 * i + u
                        act.wait_ge(s_sb_full, n + 1)
                        act.activation(prob[:, g % 2, i, 2 * u:2 * u + 2, :].rearrange("p k q -> p (k q)"), SB[u][:, :],
                                       ACT.Exp).then_inc(s_exp, 1)
                elif kind == "values" and step[2] == KT - 1:
                    g = step[1]
                    act.wait_ge(s_ob_full, g + 1)
                    if g % NG == 0 and g:
                        n, b, _ = split_group(g - 1)
                        act.wait_ge(x_full[1], X_COUNT[1, ("out_turn", n, b)])
                    act.activation(oT[:, g % NG, :], OB[:, 0:NQ], ACT.Copy).then_inc(s_ob_read, 1)
                elif kind == "ctx_measure":
                    act.wait_ge(in_ctx[0], 16)
                    act.wait_ge(in_ctx[1], 16)
                    for k in range(B * KT):
                        last = act.activation(csq[:, k, :], cx[:, k, :], ACT.Square, accum_out=cstat[:, 0, k:k + 1])
                    last.then_inc(s_csq, 1)
                elif kind == "norm" and step[1] in ("q1", "o1"):
                    b = step[2]
                    act.wait_ge(s_norm, nth(*step))
                    for r in range(R):
                        last = act.activation(junk[:, r, :], hn[:, b, r, :], ACT.Square, accum_out=sumsq[:, r:r + 1])
                    last.then_inc(s_sq, 1)
                elif kind in ("turn", "att_turn", "red0", "bias0", "bias1") and step in ON_SCALAR:
                    b = step[-1]
                    act.wait_ge(x_full[0], X_COUNT[0, step])
                    if kind == "turn":
                        last = act.activation(hT[:, b, :], X[0][:, 0:NQ], ACT.Copy)
                    elif kind == "att_turn" and step[1] == 0:
                        act.wait_ge(in_bv, 16)
                        last = act.activation(attT[:, b, :], X[0][:, 0:NQ], ACT.Identity, bias=bias3[:, 2:3])
                    elif kind == "att_turn":
                        last = act.activation(attT[:, b, :], X[0][:, 0:NQ], ACT.Copy)
                    elif kind == "red0":
                        last = act.activation(redT[:, :], X[0][0:GD, 0:NQ], ACT.Copy)
                    elif kind == "bias0":
                        last = act.activation(ohT[:, :], X[0][0:E0, 0:NQ], ACT.Copy)
                    else:
                        last = act.activation(cwT[:, :], X[0][0:E1 + 1, 0:NQ], ACT.Copy)
                    last.then_inc(x_read[0], 1)
                elif kind == "gate_exp0":
                    b = step[1]
                    act.wait_ge(s_gate, LOGITS0[b])
                    for r in range(R):
                        act.activation(ge0[:, b, r, :], lgk0[:, b, r, :], ACT.Exp, bias=ntop0[:, b, r:r + 1],
                                       accum_out=gsum0[:, b, r:r + 1]).then_inc(s_pick, 1)
                elif kind == "logits1":
                    b = step[1]
                    act.wait_ge(s_gate, LOGITS1[b])
                    for r in range(R):
                        act.activation(ge1[:, r, :], lg1[:, r, 0:E1], ACT.Exp, bias=ntop1[:, r:r + 1],
                                       accum_out=gsum1[:, r:r + 1]).then_inc(s_pick, 1)
                elif kind == "hidden0":
                    _, b, e, q = step
                    if b == 0 and e < 2 and q == 0:
                        act.wait_ge(s_ob_full, 8)
                    if (b, e, q) == (0, 0, 0):
                        act.wait_ge(*xread(0, "bias_turn"))
                    n = b * E0 + e
                    if n >= 2:
                        act.wait_ge(s_y0_full, R * (n - 1))
                    act.wait_ge(s_h0_full, 2 * n + q + 1)
                    for c in range(2 * q, 2 * q + 2):
                        last = act.activation(hid[:, n % 2, c, :], SB[q][:, (c % 2) * NQ:(c % 2 + 1) * NQ], ACT.Gelu,
                                              bias=b1T[:, e * FC + c:e * FC + c + 1])
                    last.then_inc(s_h0, 1)
                elif kind == "hidden1":
                    _, b, e = step
                    n = b * (E1 + 1) + e
                    if n == 0:
                        act.wait_ge(s_ob_full, GQ)
                    if n >= 4:
                        act.wait_ge(s_y1_full, R * (n - 3))
                    act.wait_ge(s_h1_full, n + 1)
                    act.activation(hid1[:, n % 4, :], SB[n % 2][:, 0:NQ], ACT.Relu, bias=e1T[:, e:e + 1]).then_inc(s_h1, 1)

        @block.vector
        def _(dve):
            count = [0]

            def then(ins):
                count[0] += 1
                ins.then_inc(s_v, 1)
                dve.wait_ge(s_v, count[0])

            dve.memset(fill_view(K[0][:, 0]), TWO_ONES).then_inc(s_const, 1)

            for step in SCHEDULE:
                kind = step[0]
                if kind == "w0_turn":
                    dve.wait_ge(x_full[1], X_COUNT[1, step])
                    if step[1] == 0:
                        for n in range(2):
                            last = dve.tensor_copy(wT[0][:, n, :].rearrange("i (a d p) -> i a d p", a=2, d=8),
                                                   X[1][:, n * D:(n + 1) * D].rearrange("i (p a d) -> i a d p", p=8, a=2))
                        last.then_inc(x_read[1], 1)
                        dve.wait_ge(in_bias0, 32)
                        dve.tensor_scalar(bqs[:, :], bias3[:, 0:1], QSCALE, None, ALU.mult).then_inc(s_bqs, 1)
                    else:
                        dve.tensor_copy(wT[0][:, 2:4, :].rearrange("i n o -> i (n o)"), X[1][:, 0:2 * D]).then_inc(x_read[1], 1)
                elif kind == "constants":
                    dve.memset(ones[:, :], 1.0).then_inc(s_const, 1)
                    then(dve.memset(halves[:, :], 0.0))
                    for a in range(2):
                        last = dve.memset(halves[64 * a:64 * a + 64, 64 * a:64 * a + 64], 1.0)
                    last.then_inc(s_const, 1)
                    dve.wait_ge(s_ident, 1)
                    dve.tensor_scalar(negident[:, :], ident[:, :], -1.0, None, ALU.mult).then_inc(s_ident, 1)
                    for t in (lg0, lg1, rep0, rep1):
                        last = dve.memset(t[:, :, :], LOWEST)
                    last.then_inc(s_const, 1)
                    dve.memset(cw[:, :, :, E1:E1 + 1], 1.0).then_inc(s_const, 1)
                elif kind == "stats":
                    _, stage, b = step
                    src = stage_in[stage]
                    if stage == "q0":
                        dve.wait_ge(in_x[b], 16)
                    elif stage == "q1":
                        dve.wait_ge(s_end0, b + 1)
                    elif stage == "o1":
                        dve.wait_ge(*xread(1, "out_turn", 1, b))
                    else:
                        dve.wait_ge(*xread(1, "out_proj", int(stage == "f1"), b))
                    for r in range(R):
                        last = dve.bn_stats(bst[:, r, :], src[:, b, r, :])
                    then(last)
                    for r in range(R):
                        last = dve.bn_aggr(mv[:, r, :], bst[:, r, :])
                    last.then_inc(s_stats, 1)
                elif kind == "norm":
                    _, stage, b = step
                    src = stage_in[stage]
                    if stage == "o1":
                        dve.wait_ge(in_gb, 48)
                        dve.wait_ge(s_stats, nth("stats", stage, b))
                        for r in range(R):
                            last = dve.tensor_scalar(hn[:, b, r, :], src[:, b, r, :], mv[:, r, 0:1], None, ALU.subtract)
                        then(last)
                    dve.wait_ge(s_rstd, nth("stats", stage, b))
                    if stage == "o1":
                        for r in range(R):
                            last = dve.scalar_tensor_tensor(hn[:, b, r, :], hn[:, b, r, :], rstd[:, r:r + 1], gamma_b[:, :],
                                                            ALU.mult, ALU.mult)
                        then(last)
                    for r in range(R):
                        if stage == "o1":
                            last = dve.tensor_tensor(hn[:, b, r, :], hn[:, b, r, :], beta_b[:, :], ALU.add)
                        else:
                            last = dve.tensor_scalar(hn[:, b, r, :], src[:, b, r, :], mv[:, r, 0:1], rstd[:, r:r + 1],
                                                     ALU.subtract, ALU.mult)
                    last.then_inc(s_norm, 1)
                    if stage in ("q0", "f0", "f1"):
                        continue
                    dve.wait_ge(s_norm, nth(*step))
                    then(dve.tensor_reduce(amax[:, :], hn[:, b, :, :], AX, ALU.max, apply_absolute_value=True))
                elif kind == "quant":
                    _, stage, b = step
                    dve.wait_ge(s_rms, nth(*step))
                    then(dve.tensor_tensor(mxn[:, :], amax[:, :], rms[:, :], ALU.mult))
                    then(dve.tensor_scalar(mxn[:, :], mxn[:, :], 1e-5, None, ALU.max))
                    then(dve.reciprocal(inv[:, :], mxn[:, :]))
                    dve.tensor_scalar(dq[:, :], mxn[:, :], 1.0 / 127.0, None, ALU.mult)
                    then(dve.scalar_tensor_tensor(qs[:, :], inv[:, :], 127.0, rms[:, :], ALU.mult, ALU.mult))
                    for r in range(R):
                        last = dve.tensor_scalar(hn[:, b, r, :], hn[:, b, r, :], qs[:, r:r + 1], MAGIC, ALU.mult, ALU.add)
                    then(last)
                    for r in range(R):
                        last = dve.tensor_scalar(hn[:, b, r, :], hn[:, b, r, :], -MAGIC, dq[:, r:r + 1], ALU.add, ALU.mult)
                    last.then_inc(s_quant, 1)
                elif kind == "turn" and step not in ON_SCALAR:
                    _, stage, b = step
                    dve.wait_ge(x_full[0], X_COUNT[0, step])
                    dve.tensor_copy(hT[:, b, :], X[0][:, 0:NQ]).then_inc(x_read[0], 1)
                elif kind in ("kproj", "qproj") and step not in ON_GPSIMD:
                    split_step(dve, then, step)
                elif kind == "scores":
                    _, g, i = step
                    for r in range(R):
                        n = 8 * g + 2 * i + r
                        if i == 0 and g >= 2:
                            dve.wait_ge(x_full[0], X_COUNT[0, ("max_rows", g - 2)])
                        dve.wait_ge(s_sa_full, n + 1)
                        dve.tensor_reduce(mx[:, g % 2, r, i:i + 1], SA[SCORE_BANK[n]][:, :], AX, ALU.max).then_inc(s_sa_max, 1)
                elif kind == "bias_turn":
                    dve.wait_ge(x_full[0], X_COUNT[0, step])
                    dve.tensor_copy(b1T[:, :], X[0][:, 0:E0 * FC])
                    dve.tensor_copy(e1T[:, :], X[0][:, 64:64 + E1 + 1]).then_inc(x_read[0], 1)
                    dve.wait_ge(in_route, 16 * 9)
                    dve.tensor_tensor_reduce(wgsq[:, :], wgn[:, :], wgn[:, :], 1.0, 0.0, ALU.mult, ALU.add,
                                             wgs[:, 0:1]).then_inc(s_wgsq, 1)
                elif kind == "ctx_measure":
                    dve.wait_ge(in_ctx[0], 16)
                    dve.wait_ge(in_ctx[1], 16)
                    dve.tensor_reduce(cstat[:, 1, :], cx[:, :, :], AX, ALU.max, apply_absolute_value=True).then_inc(s_csq, 1)
                elif kind == "ctx_quant":
                    dve.wait_ge(s_csq, 2)
                    dve.wait_ge(s_cstat, 1)
                    then(dve.tensor_tensor(cstat[:, 4, :], cstat[:, 1, :], cstat[:, 3, :], ALU.mult))
                    then(dve.tensor_scalar(cstat[:, 4, :], cstat[:, 4, :], 1e-5, None, ALU.max))
                    then(dve.reciprocal(cstat[:, 5, :], cstat[:, 4, :]))
                    then(dve.scalar_tensor_tensor(cstat[:, 5, :], cstat[:, 5, :], 127.0, cstat[:, 3, :], ALU.mult, ALU.mult))
                    dve.tensor_scalar(cstat[:, 6, :], cstat[:, 4, :], 1.0 / 127.0, None, ALU.mult).then_inc(s_cstat, 1)
                elif kind == "wg_norm":
                    dve.wait_ge(s_wgnorm, 1)
                    then(dve.tensor_scalar(wgs[:, 1:2], wgs[:, 1:2], 1e-4, None, ALU.max))
                    then(dve.reciprocal(wgs[:, 2:3], wgs[:, 1:2]))
                    dve.tensor_scalar(wgn[:, :], wgn[:, :], wgs[:, 2:3], None, ALU.mult).then_inc(s_wgn, 1)
                elif kind == "w1_measure":
                    dve.wait_ge(in_w1n, 64)
                    dve.tensor_reduce(wsum[:, :], w1n[:, :, :], AX, ALU.add, apply_absolute_value=True).then_inc(s_wabs, 1)
                    dve.wait_ge(x_full[1], X_COUNT[1, step])
                    for n, size in enumerate((D * D, D * D // 2, D * D)):
                        last = dve.tensor_scalar(walpha[:, n:n + 1], X[1][:, n:n + 1], 1.0 / size, 1e-5, ALU.mult, ALU.max)
                    last.then_inc(x_read[1], 1)
                    dve.wait_ge(*xread(1, *step))
                    dve.reciprocal(winv[:, :], walpha[:, :]).then_inc(s_walpha, 1)
                elif kind == "w1_turn":
                    dve.wait_ge(x_full[1], X_COUNT[1, step])
                    dve.tensor_copy(wT[1][:, 0, 0:64].rearrange("i (a d r) -> i a d r", a=2, d=8),
                                    X[1][:, D:D + 64].rearrange("i (r a d) -> i a d r", r=4, a=2))
                    dve.tensor_copy(wT[1][:, 2, 0:64], X[1][:, D + 64:2 * D])
                    for a in range(2):
                        dve.tensor_copy(wT[1][:, 1, 64 * a:64 * a + 64].rearrange("i (d r g) -> i d r g", d=8, r=4),
                                        X[1][:, 0:D].rearrange("i (r a g d) -> i a d r g", r=4, a=2, g=2)[:, a])
                    dve.tensor_copy(wT[1][:, 3, :], X[1][:, 2 * D:3 * D])
                    dve.tensor_copy(wgT[:, :], X[1][0:GD, 3 * D:3 * D + E0]).then_inc(x_read[1], 1)
                elif kind == "out_turn":
                    _, n, b = step
                    for r in range(R):
                        dve.wait_ge(x_full[r], X_COUNT[r, step])
                        slots = X[r][:, :].rearrange("q (s c) -> q s c", c=32)
                        then(dve.reciprocal(rsum[:, r, :], slots[:, :, DH]))
                        for a in range(2):
                            src = slots[:, 8 * a:8 * a + 8, 0:DH]
                            w = rsum[:, r, 8 * a:8 * a + 8].unsqueeze(2).broadcast_to([P, 8, DH])
                            if n == 0:
                                dst = att[:, b, r, :].rearrange("q (p a d) -> q a p d", p=8, a=2)[:, a]
                            else:
                                src = src.rearrange("q (r g) d -> q r g d", g=2)
                                w = w.rearrange("q (r g) d -> q r g d", g=2)
                                dst = att[:, b, r, :].rearrange("q (r a g d) -> q a r g d", r=4, a=2, g=2)[:, a]
                            last = dve.tensor_tensor(dst, src, w, ALU.mult)
                        if r == 0:
                            last.then_inc(x_read[0], 1)
                        else:
                            last.then_inc(x_read[1], 1)
                elif kind == "att_turn" and step not in ON_SCALAR:
                    _, n, b = step
                    dve.wait_ge(x_full[0], X_COUNT[0, step])
                    if n == 0:
                        dve.wait_ge(in_bv, 16)
                        dve.tensor_scalar(attT[:, b, :], X[0][:, 0:NQ], bias3[:, 2:3], None, ALU.add).then_inc(x_read[0], 1)
                    else:
                        dve.tensor_copy(attT[:, b, :], X[0][:, 0:NQ]).then_inc(x_read[0], 1)
                elif kind == "out_proj":
                    _, n, b = step
                    dve.wait_ge(x_full[1], X_COUNT[1, step])
                    if n == 0:
                        dve.wait_ge(s_xres, 1)
                    dst, res = ((x1, xres), (x3, x2))[n]
                    dve.tensor_tensor(dst[:, b].rearrange("p r d -> p (r d)"), X[1][:, 0:NQ],
                                      res[:, b].rearrange("p r d -> p (r d)"), ALU.add).then_inc(x_read[1], 1)
                elif kind == "red0" and step not in ON_SCALAR:
                    b = step[1]
                    dve.wait_ge(x_full[0], X_COUNT[0, step])
                    dve.tensor_copy(redT[:, :], X[0][0:GD, 0:NQ]).then_inc(x_read[0], 1)
                elif kind == "logits0":
                    b = step[1]
                    dve.wait_ge(s_const, 5)
                    dve.wait_ge(x_full[1], X_COUNT[1, step])
                    logits = X[1][:, 0:R * E0].rearrange("p (r e) -> p r e", r=R)
                    dve.tensor_copy(lgk0[:, b, :, :], logits)
                    dve.tensor_copy(lg0[:, :, 0:E0], logits).then_inc(x_read[1], 1)
                    dve.wait_ge(*xread(1, *step))
                    for r in range(R):
                        last = dve.max(top0[:, r, :], lg0[:, r, :])
                    then(last)
                    dve.tensor_scalar(ntop0[:, b, :], top0[:, :, 0], -1.0, None, ALU.mult).then_inc(s_gate, 1)
                    then(dve.tensor_copy(rep0[:, :, 0:1], top0[:, :, 0:1]))
                    for r in range(R):
                        last = dve.match_replace(mr0[:, r, :], rep0[:, r, :], lg0[:, r, :], MARK)
                    then(last)
                    dve.tensor_tensor(oh0[:, b, :, :], mr0[:, :, 0:E0], lg0[:, :, 0:E0], ALU.not_equal).then_inc(s_cw, 1)
                elif kind == "bias0":
                    b = step[1]
                    if step not in ON_SCALAR:
                        dve.wait_ge(x_full[0], X_COUNT[0, step])
                        dve.tensor_copy(ohT[:, :], X[0][0:E0, 0:NQ]).then_inc(x_read[0], 1)
                    dve.wait_ge(x_full[1], X_COUNT[1, step])
                    dve.wait_ge(s_y0, OUTPUTS_BEFORE[step])
                    dve.tensor_tensor(acc[:, b].rearrange("p r d -> p (r d)"), X[1][:, 0:NQ],
                                      acc[:, b].rearrange("p r d -> p (r d)"), ALU.add).then_inc(x_read[1], 1)
                    dve.wait_ge(*xread(1, *step))
                elif kind == "output0":
                    _, b, e, r = step
                    n = R * (b * E0 + e) + r
                    dve.wait_ge(s_y0_full, n + 1)
                    if e == 0:
                        dve.wait_ge(s_cw, CW_AT["logits0", b])
                        dve.tensor_scalar(acc[:, b, r, :], YB[r][:, 0:D], oh0[:, b, r, e:e + 1], None, ALU.mult).then_inc(s_y0, 1)
                    else:
                        dve.wait_ge(s_y0, n - 1)
                        dve.scalar_tensor_tensor(acc[:, b, r, :], YB[r][:, 0:D], oh0[:, b, r, e:e + 1], acc[:, b, r, :],
                                                 ALU.mult, ALU.add).then_inc(s_y0, 1)
                elif kind == "end0":
                    b = step[1]
                    dve.wait_ge(s_pick, GATE_EXP0[b] + R)
                    dve.wait_ge(s_y0, (b + 1) * E0 * R)
                    then(dve.reciprocal(score0[:, b, :], gsum0[:, b, :]))
                    for r in range(R):
                        last = dve.scalar_tensor_tensor(x2[:, b, r, :], acc[:, b, r, :], score0[:, b, r:r + 1],
                                                        x1[:, b, r, :], ALU.mult, ALU.add)
                    last.then_inc(s_end0, 1)
                elif kind == "logits1":
                    b = step[1]
                    dve.wait_ge(x_full[1], X_COUNT[1, step])
                    dve.tensor_tensor(lg1[:, :, 0:E1], X[1][:, 0:R * E1].rearrange("p (r e) -> p r e", r=R),
                                      rb_b[:, :].unsqueeze(1).broadcast_to([P, R, E1]), ALU.add).then_inc(x_read[1], 1)
                    dve.wait_ge(*xread(1, *step))
                    for r in range(R):
                        last = dve.max(top1[:, r, :], lg1[:, r, :])
                    then(last)
                    dve.tensor_scalar(ntop1[:, :], top1[:, :, 0], -1.0, None, ALU.mult).then_inc(s_gate, 1)
                    then(dve.tensor_copy(rep1[:, :, 0:TOP], top1[:, :, 0:TOP]))
                    for r in range(R):
                        last = dve.match_replace(mr1[:, r, :], rep1[:, r, :], lg1[:, r, :], MARK)
                    then(last)
                    then(dve.tensor_tensor(sel1[:, :, :], mr1[:, :, 0:E1], lg1[:, :, 0:E1], ALU.not_equal))
                elif kind == "pick1":
                    b = step[1]
                    dve.wait_ge(s_pick, EXP1[b])
                    then(dve.reciprocal(rsum1[:, :], gsum1[:, :]))
                    for r in range(R):
                        last = dve.scalar_tensor_tensor(cw[:, b, r, 0:E1], ge1[:, r, :], rsum1[:, r:r + 1], sel1[:, r, :],
                                                        ALU.mult, ALU.mult)
                    last.then_inc(s_cw, 1)
                elif kind == "bias1":
                    b = step[1]
                    if step not in ON_SCALAR:
                        dve.wait_ge(x_full[0], X_COUNT[0, step])
                        dve.tensor_copy(cwT[:, :], X[0][0:E1 + 1, 0:NQ]).then_inc(x_read[0], 1)
                    dve.wait_ge(x_full[1], X_COUNT[1, step])
                    dve.wait_ge(s_y1, OUTPUTS_BEFORE[step])
                    dve.tensor_tensor(acc[:, b].rearrange("p r d -> p (r d)"), X[1][:, 0:NQ],
                                      acc[:, b].rearrange("p r d -> p (r d)"), ALU.add).then_inc(x_read[1], 1)
                    dve.wait_ge(*xread(1, *step))
                elif kind == "output1":
                    _, b, e, r = step
                    n = R * (b * (E1 + 1) + e) + r
                    dve.wait_ge(s_y1_full, n - r + R)
                    if e == 0:
                        dve.wait_ge(s_cw, CW_AT["pick1", b])
                    else:
                        dve.wait_ge(s_y1, n - 1)
                    dve.scalar_tensor_tensor(acc[:, b, r, :], Y1[n // R % 4][:, r * D:(r + 1) * D], cw[:, b, r, e:e + 1],
                                             (x3 if e == 0 else acc)[:, b, r, :],
                                             ALU.mult, ALU.add).then_inc(s_y1, 1)

        @block.tensor
        def _(pe):
            pe.wait_ge(s_ident, 1)

            def fill(bank, step):
                n = X_COUNT[bank, step]
                if n > 1:
                    pe.wait_ge(x_read[bank], n - 1)

            for step in SCHEDULE:
                kind = step[0]
                if kind == "ctx_turn" or kind == "ctxq_turn":
                    c = step[1]
                    src = cx if kind == "ctx_turn" else csq
                    fill(c, step)
                    if kind == "ctx_turn":
                        pe.wait_ge(in_ctx[c], 16)
                    else:
                        pe.wait_ge(s_cq, 1)
                    for k in range(KT):
                        last = pe.transpose(X[c][:, k * P:(k + 1) * P], src[:, c * KT + k, :], ident[:, :])
                    last.then_inc(x_full[c], 1)
                elif kind == "w0_turn":
                    fill(1, step)
                    pe.wait_ge(in_w0[step[1]], 32)
                    for n in range(2):
                        last = pe.transpose(X[1][:, n * D:(n + 1) * D], w0n[:, 2 * step[1] + n, :], ident[:, :])
                    last.then_inc(x_full[1], 1)
                elif kind == "w1_measure":
                    fill(1, step)
                    pe.wait_ge(s_wabs, 1)
                    pe.wait_ge(s_const, 3)
                    for n in range(3):
                        last = pe.matmul(X[1][:, n:n + 1], (halves if n == 1 else ones)[:, :], wsum[:, n:n + 1],
                                         start=True, stop=True)
                    last.then_inc(x_full[1], 1)
                elif kind == "w1_turn":
                    fill(1, step)
                    pe.wait_ge(s_wtern, 1)
                    for n in range(3):
                        pe.transpose(X[1][:, n * D:(n + 1) * D], w1t[:, n, :], ident[:, :])
                    pe.wait_ge(s_wgn, 1)
                    pe.transpose(X[1][0:GD, 3 * D:3 * D + E0], wgn[:, :], ident[0:E0, 0:E0]).then_inc(x_full[1], 1)
                elif kind == "bias_turn":
                    fill(0, step)
                    pe.wait_ge(in_route, 16 * 9)
                    pe.transpose(X[0][:, 0:E0 * FC], b1r[:, :], ident[0:E0 * FC, 0:E0 * FC])
                    pe.transpose(X[0][:, 64:64 + E1 + 1], e1r[:, :], ident[0:E1 + 1, 0:E1 + 1]).then_inc(x_full[0], 1)
                elif kind == "turn":
                    _, stage, b = step
                    fill(0, step)
                    if stage in ("q0", "f0", "f1"):
                        pe.wait_ge(s_norm, nth("norm", stage, b))
                    else:
                        pe.wait_ge(s_quant, nth("quant", stage, b))
                    for r in range(R):
                        last = pe.transpose(X[0][:, r * P:(r + 1) * P], hn[:, b, r, :], ident[:, :])
                    last.then_inc(x_full[0], 1)
                elif kind == "kproj":
                    _, n, b = step
                    fill(0, step)
                    pe.wait_ge(*xread(1, *(("w0_turn", 0), ("w1_turn",))[n]))
                    pe.wait_ge(*xread(b, ("ctx_turn", "ctxq_turn")[n], b))
                    rows = P // (n + 1)
                    pe.matmul(X[0][0:rows, :], wT[n][:, 0, 0:rows], ctxT[:, b * NK:(b + 1) * NK],
                              start=True, stop=True).then_inc(x_full[0], 1)
                elif kind == "vproj":
                    _, n, b = step
                    fill(1, step)
                    pe.wait_ge(*xread(b, ("ctx_turn", "ctxq_turn")[n], b))
                    pe.wait_ge(*xread(1, *(("w0_turn", 1), ("w1_turn",))[n]))
                    w = D // (n + 1)
                    for k in range(KT):
                        last = pe.matmul(X[1][:, k * w:(k + 1) * w], ctxT[:, b * NK + k * P:b * NK + (k + 1) * P],
                                         wT[n][:, 2, 0:w], start=True, stop=True)
                    last.then_inc(x_full[1], 1)
                elif kind == "qproj":
                    _, n, b = step
                    fill(1, step)
                    pe.wait_ge(*xread(0, "turn", ("q0", "q1")[n], b))
                    pe.wait_ge(*xread(1, *(("w0_turn", 0), ("w1_turn",))[n]))
                    pe.matmul(X[1][:, 0:NQ], wT[n][:, 1, :], hT[:, b, :], start=True, stop=True).then_inc(x_full[1], 1)
                elif kind == "scores":
                    _, gg, i = step
                    n, b, g = split_group(gg)
                    if i == 0 and g < K_PARTS[n][b]:
                        pe.wait_ge(s_kst[n][b][g], 16 * 2)
                    if i == 0 and g % 2 == 0:
                        pe.wait_ge(s_qst[n][b][g // 2], 16)
                    s = 4 * g + i
                    for r in range(R):
                        u = 8 * gg + 2 * i + r
                        if SCORE_BEFORE[u] >= 0:
                            pe.wait_ge(s_sa_max, SCORE_BEFORE[u] + 1)
                        if u == LENT_UNTIL:
                            pe.wait_ge(s_y0, B * E0 * R)
                        pe.matmul(SA[SCORE_BANK[u]][:, :], Q[n][:, b, s, r * P:(r + 1) * P], K[n][:, b, key_group(n, s), :],
                                  start=True, stop=True).then_inc(s_sa_full, 1)
                elif kind == "max_rows":
                    g = step[1]
                    pe.wait_ge(s_sa_max, 8 * (g + 1))
                    if g == 0:
                        pe.wait_ge(s_ident, 2)
                    fill(0, step)
                    for r in range(R):
                        last = pe.matmul(X[0][0:4, r * P:(r + 1) * P], mx[:, g % 2, r, :], negident[:, :], start=True, stop=True)
                    last.then_inc(x_full[0], 1)
                elif kind == "exp":
                    _, gg, i = step
                    n, b, g = split_group(gg)
                    s = 4 * g + i
                    if i == 0:
                        pe.wait_ge(s_shift, 16 * (gg + 1))
                    if gg == 8 and i == 0:
                        pe.wait_ge(s_h0, 2 * B * E0)
                    for u in range(2):
                        m = 8 * gg + 2 * i + u
                        if m >= 2:
                            pe.wait_ge(s_exp, m - 1)
                        for k in range(2):
                            kt = 2 * u + k
                            last = pe.matmul(SB[u][:, k * NQ:(k + 1) * NQ],
                                             K[n][:, b, key_group(n, s), kt * P:(kt + 1) * P], Q[n][:, b, s, :],
                                             start=True, stop=True)
                        last.then_inc(s_sb_full, 1)
                elif kind == "values":
                    _, gg, kt = step
                    n, b, g = split_group(gg)
                    if kt == 0:
                        pe.wait_ge(s_exp, 8 * (gg + 1))
                        pe.wait_ge(*xread(1, "vproj", n, b))
                        if gg:
                            pe.wait_ge(s_ob_read, gg)
                        if gg == 8:
                            pe.wait_ge(s_y0, B * E0 * R)
                    for j in range(4):
                        last = pe.matmul(OB[32 * j:32 * j + 32, 0:NQ], V[n][:, b, kt, value_head(n, 4 * g + j), :],
                                         prob[:, gg % 2, j, kt, :], start=(kt == 0), stop=(kt == KT - 1))
                    if kt == KT - 1:
                        last.then_inc(s_ob_full, 1)
                elif kind == "out_turn":
                    _, n, b = step
                    pe.wait_ge(s_ob_read, 8 * n + NG * (b + 1))
                    for r in range(R):
                        fill(r, step)
                        for g in range(NG):
                            last = pe.transpose(X[r][:, g * P:(g + 1) * P], oT[:, g, r * P:(r + 1) * P], ident[:, :])
                        last.then_inc(x_full[r], 1)
                elif kind == "att_turn":
                    _, n, b = step
                    fill(0, step)
                    if n == 0:
                        pe.wait_ge(*xread(1, "out_turn", n, b))
                    else:
                        pe.wait_ge(s_quant, nth("quant", "o1", b))
                    for r in range(R):
                        last = pe.transpose(X[0][:, r * P:(r + 1) * P], (att, hn)[n][:, b, r, :], ident[:, :])
                    last.then_inc(x_full[0], 1)
                elif kind == "out_proj":
                    _, n, b = step
                    fill(1, step)
                    pe.wait_ge(*xread(0, "att_turn", n, b))
                    for r in range(R):
                        last = pe.matmul(X[1][:, r * D:(r + 1) * D], attT[:, b, r * P:(r + 1) * P], wT[n][:, 3, :],
                                         start=True, stop=True)
                    last.then_inc(x_full[1], 1)
                elif kind == "red0":
                    b = step[1]
                    fill(0, step)
                    pe.wait_ge(*xread(0, "turn", "f0", b))
                    pe.matmul(X[0][0:GD, 0:NQ], wreds[:, :], hT[:, b, :], start=True, stop=True).then_inc(x_full[0], 1)
                elif kind == "logits0":
                    b = step[1]
                    fill(1, step)
                    pe.wait_ge(*xread(0, "red0", b))
                    for r in range(R):
                        last = pe.matmul(X[1][:, r * E0:(r + 1) * E0], redT[:, r * P:(r + 1) * P], wgT[:, :], start=True, stop=True)
                    last.then_inc(x_full[1], 1)
                elif kind == "bias0":
                    b = step[1]
                    fill(0, step)
                    pe.wait_ge(s_cw, CW_AT["logits0", b])
                    for r in range(R):
                        last = pe.transpose(X[0][0:E0, r * P:(r + 1) * P], oh0[:, b, r, :], ident[:, :])
                    last.then_inc(x_full[0], 1)
                    fill(1, step)
                    pe.wait_ge(*xread(0, *step))
                    for r in range(R):
                        last = pe.matmul(X[1][:, r * D:(r + 1) * D], ohT[:, r * P:(r + 1) * P], b2r[:, :], start=True, stop=True)
                    last.then_inc(x_full[1], 1)
                elif kind == "hidden0":
                    _, b, e, q = step
                    n = b * E0 + e
                    if n == 0 and q == 0:
                        pe.wait_ge(s_exp, 64)
                        pe.wait_ge(in_f0, 16 * 2 * E0)
                    if n >= 1:
                        pe.wait_ge(s_h0, 2 * n + q - 1)
                    for c in range(2 * q, 2 * q + 2):
                        last = pe.matmul(SB[q][:, (c % 2) * NQ:(c % 2 + 1) * NQ], w1s[:, e, c * P:(c + 1) * P], hT[:, b, :],
                                         start=True, stop=True)
                    last.then_inc(s_h0_full, 1)
                elif kind == "output0":
                    _, b, e, r = step
                    n = b * E0 + e
                    pe.wait_ge(s_h0, 2 * n + 2)
                    if n == 0 and r == 0:
                        pe.wait_ge(s_ob_read, 8)
                        pe.wait_ge(s_sa_max, 64)
                    if n >= 1:
                        pe.wait_ge(s_y0, R * n + r - 1)
                    for c in range(FC):
                        last = pe.matmul(YB[r][:, 0:D], hid[:, n % 2, c, r * P:(r + 1) * P], w2s[:, e, c, :],
                                         start=(c == 0), stop=(c == FC - 1))
                    last.then_inc(s_y0_full, 1)
                elif kind == "logits1":
                    b = step[1]
                    fill(1, step)
                    pe.wait_ge(*xread(0, "turn", "f1", b))
                    for r in range(R):
                        last = pe.matmul(X[1][:, r * E1:(r + 1) * E1], hT[:, b, r * P:(r + 1) * P], rWs[:, :], start=True, stop=True)
                    last.then_inc(x_full[1], 1)
                elif kind == "bias1":
                    b = step[1]
                    fill(0, step)
                    pe.wait_ge(s_cw, CW_AT["pick1", b])
                    for r in range(R):
                        last = pe.transpose(X[0][0:E1 + 1, r * P:(r + 1) * P], cw[:, b, r, :], ident[:, :])
                    last.then_inc(x_full[0], 1)
                    fill(1, step)
                    pe.wait_ge(*xread(0, *step))
                    for r in range(R):
                        last = pe.matmul(X[1][:, r * D:(r + 1) * D], cwT[:, r * P:(r + 1) * P], e2r[:, :], start=True, stop=True)
                    last.then_inc(x_full[1], 1)
                elif kind == "hidden1":
                    _, b, e = step
                    n = b * (E1 + 1) + e
                    if n == 0:
                        pe.wait_ge(s_exp, 128)
                        pe.wait_ge(in_f1, 64)
                    if n >= 2:
                        pe.wait_ge(s_h1, n - 1)
                    pe.matmul(SB[n % 2][:, 0:NQ], e1w[:, e, :], hT[:, b, :], start=True, stop=True).then_inc(s_h1_full, 1)
                elif kind == "output1":
                    _, b, e, r = step
                    n = b * (E1 + 1) + e
                    pe.wait_ge(s_h1, n + 1)
                    if n == 0 and r == 0:
                        pe.wait_ge(s_ob_read, GQ)
                        pe.wait_ge(s_sa_max, 8 * GQ)
                    if n >= 4 and r == 0:
                        pe.wait_ge(s_y1, R * (n - 3))
                    pe.matmul(Y1[n % 4][:, r * D:(r + 1) * D], hid1[:, n % 4, r * P:(r + 1) * P], e2w[:, e, :],
                              start=True, stop=True).then_inc(s_y1_full, 1)


def _counts():
    gate, pick, cws = 0, 0, 0
    logits0, logits1, gexp0, exp1, cw_at = {}, {}, {}, {}, {}
    normq = []
    for s in SCHEDULE:
        if s[0] == "norm":
            if s[1] in ("q1", "o1"):
                normq.append(s)
        if s[0] in ("logits0", "logits1"):
            gate += 1
            (logits0 if s[0] == "logits0" else logits1)[s[1]] = gate
        if s[0] == "gate_exp0":
            gexp0[s[1]] = pick
            pick += R
        if s[0] == "logits1":
            pick += R
            exp1[s[1]] = pick
        if s[0] in ("logits0", "pick1"):
            cws += 1
            cw_at[s[0], s[1]] = cws
    return logits0, logits1, gexp0, exp1, cw_at, normq


LOGITS0, LOGITS1, GATE_EXP0, EXP1, CW_AT, NORMQ = _counts()


_INS = ["x", "ctx_1024", "L0_xattn_Wq", "L0_xattn_bq", "L0_xattn_Wk", "L0_xattn_bk", "L0_xattn_Wv", "L0_xattn_bv",
        "L0_xattn_Wo", "L0_xattn_bo", "L0_ffn_w_red", "L0_ffn_wg", "L0_ffn_w1", "L0_ffn_b1", "L0_ffn_w2", "L0_ffn_b2",
        "L1_xattn_wq", "L1_xattn_wk", "L1_xattn_wv", "L1_xattn_wo", "L1_xattn_ln_gamma", "L1_xattn_ln_beta",
        "L1_ffn_router_W", "L1_ffn_router_b", "L1_ffn_sW1", "L1_ffn_sb1", "L1_ffn_sW2", "L1_ffn_sb2",
        "L1_ffn_eW1", "L1_ffn_eb1", "L1_ffn_eW2", "L1_ffn_eb2"]


def kernel(**inputs):
    import concourse.bacc as _bacc
    from concourse.bass_utils import run_bass_kernel_spmd as _run

    nc = _bacc.Bacc("TRN2", target_bir_lowering=False, num_devices=1)
    arrays, args = {}, []
    for name in _INS:
        a = np.ascontiguousarray(inputs[name])
        arrays[f"in_{name}_dram"] = a
        args.append(nc.dram_tensor(f"in_{name}_dram", a.shape, mybir.dt.from_np(a.dtype), kind="ExternalInput").ap())
    args.append(nc.dram_tensor("out_0_dram", (B, NQ, D), F32, kind="ExternalOutput").ap())
    transformer(nc, *args)
    r = _run(nc, [arrays], core_ids=[0])
    return r.results[0]["out_0_dram"]
```
